# Optimizing a Trainium2 kernel written in Bass

```python
import numpy as np
import jax
import jax.numpy as jnp

def _softmax(x, axis=-1):
    return jax.nn.softmax(x, axis=axis)

def _gelu(x):
    return jax.nn.gelu(x, approximate=True)

def _silu(x):
    return jax.nn.silu(x)

def _sigmoid(x):
    return jax.nn.sigmoid(x)

def _layernorm(x, axis=-1, eps=1e-05):
    m = jnp.mean(x, axis=axis, keepdims=True)
    v = jnp.var(x, axis=axis, keepdims=True)
    return (x - m) / jnp.sqrt(v + eps)

def _scatter_add(tgt, idx, src, axis=0):
    return tgt.at[idx].add(src)

def _segment_sum(src, seg, n):
    return jax.ops.segment_sum(src, seg, n)
kernel_name = 'mk_flamingo_gated_d2_seqx_r8_ca52ba'

def setup_inputs(seed: int=0):
    np.random.seed(seed)
    _w = jnp.asarray

    def _rec_inputs():
        import jax
        import jax.numpy as jnp
        _rk = jax.random.key(seed)
        x = 7.22e-05 + 1 * jax.random.normal(jax.random.fold_in(_rk, 1), (32, 128, 128), jnp.float32)
        _lenS = 128 - jax.random.randint(jax.random.fold_in(_rk, 7), (32,), 0, max(1, 128 // 4) + 1, jnp.int32)
        _lenS2 = 128 - jax.random.randint(jax.random.fold_in(_rk, 8), (32,), 0, max(1, 128 // 4) + 1, jnp.int32)
        _ctx_1024P = jax.random.normal(jax.random.fold_in(_rk, 11), (32, 16, 128), jnp.float32)
        _ctx_1024c = jax.random.dirichlet(jax.random.fold_in(_rk, 511), 0.3 * jnp.ones((16,), jnp.float32), (32, 128))
        _ctx_1024t = jnp.einsum('bsk,bkd->bsd', _ctx_1024c, _ctx_1024P)
        _ctx_1024t = _ctx_1024t * jax.lax.rsqrt(jnp.mean(jnp.square(_ctx_1024t)) + 1e-12) * 0.953939
        ctx_1024 = 4.13588e-05 + 0.999923 * (_ctx_1024t + 0.3 * jax.random.normal(jax.random.fold_in(_rk, 611), (32, 128, 128), jnp.float32))
        _validS = jnp.arange(128)[None, :] < _lenS[:, None]
        _validS2 = jnp.arange(128)[None, :] < _lenS2[:, None]
        _causal = jnp.tril(jnp.ones((128, 128), dtype=bool))
        mask_BxS2_bf1 = jnp.ones((32, 128), dtype=bool)
        _g = jax.random.normal(jax.random.fold_in(_rk, 9001), (2, 2), jnp.float32)
        _g = jnp.sign(_g) * jnp.maximum(jnp.abs(_g), 1.0) + (_g == 0) * 1.0
        g_xattn = _g[0]
        g_ffn = _g[1]
        return (x, ctx_1024, mask_BxS2_bf1, g_xattn, g_ffn)
    x, ctx_1024, mask_BxS2_bf1, g_xattn, g_ffn = _rec_inputs()

    def _L0_xattn_setup():
        import jax, jax.numpy as jnp
        import numpy as np
        D_MODEL = 128
        NHEAD = 16
        D_K = D_MODEL // NHEAD
        key = jax.random.key(seed)
        ks = jax.random.split(key, 11)
        B, S = (4, 256)
        s = 1.0 / np.sqrt(D_MODEL)
        return {'query': jax.random.normal(ks[0], (B, S, D_MODEL), jnp.float32), 'key': jax.random.normal(ks[1], (B, S, D_MODEL), jnp.float32), 'value': jax.random.normal(ks[2], (B, S, D_MODEL), jnp.float32), 'wq': jax.random.normal(ks[3], (D_MODEL, D_MODEL), jnp.float32) * s, 'bq': jnp.zeros((D_MODEL,), jnp.float32), 'wk': jax.random.normal(ks[4], (D_MODEL, D_MODEL), jnp.float32) * s, 'bk': jnp.zeros((D_MODEL,), jnp.float32), 'wv': jax.random.normal(ks[5], (D_MODEL, D_MODEL), jnp.float32) * s, 'bv': jnp.zeros((D_MODEL,), jnp.float32), 'wo': jax.random.normal(ks[6], (D_MODEL, D_MODEL), jnp.float32) * s, 'bo': jnp.zeros((D_MODEL,), jnp.float32)}
    _L0_xattn_all = _L0_xattn_setup()
    _L0_xattn_in = {k: v for k, v in _L0_xattn_all.items() if k in ('wq', 'bq', 'wk', 'bk', 'wv', 'bv', 'wo', 'bo')}
    del _L0_xattn_all

    def _L0_ffn_setup():
        import jax, jax.numpy as jnp
        import numpy as np
        D = 128
        N_EXP = 8
        TOP_K = 1
        key = jax.random.key(seed)
        ks = jax.random.split(key, 7)
        s = 0.02
        return {'x': jax.random.normal(ks[0], (4, 256, D), jnp.float32), 'gate_w': jax.random.normal(ks[1], (D, N_EXP), jnp.float32) * s, 'gate_b': jnp.zeros((N_EXP,), jnp.float32), 'w1': jax.random.normal(ks[2], (N_EXP, D, 4 * D), jnp.float32) * s, 'b1': jnp.zeros((N_EXP, 4 * D), jnp.float32), 'w2': jax.random.normal(ks[3], (N_EXP, 4 * D, D), jnp.float32) * s, 'b2': jnp.zeros((N_EXP, D), jnp.float32)}
    _L0_ffn_all = _L0_ffn_setup()
    _L0_ffn_in = {k: v for k, v in _L0_ffn_all.items() if k in ('gate_w', 'gate_b', 'w1', 'b1', 'w2', 'b2')}
    del _L0_ffn_all

    def _L1_xattn_setup():
        import jax, jax.numpy as jnp
        import numpy as np
        N_HEADS = 16
        D_MODEL = 128
        HEAD_DIM = D_MODEL // N_HEADS
        MASK_FILL = -100000000.0

        def _split_heads(x):
            B, S, _ = x.shape
            return x.reshape(B, S, N_HEADS, HEAD_DIM).transpose(0, 2, 1, 3)
        key = jax.random.key(seed)
        ks = jax.random.split(key, 12)
        B, L, P = (2, 256, 256)
        s = 1.0 / np.sqrt(D_MODEL).astype(np.float32)
        inp = {'q': jax.random.normal(ks[0], (B, L, D_MODEL), dtype=jnp.float32), 'k': jax.random.normal(ks[1], (B, P, D_MODEL), dtype=jnp.float32), 'v': jax.random.normal(ks[2], (B, P, D_MODEL), dtype=jnp.float32), 'attention_mask': jnp.ones((B, P), dtype=bool), 'Wq': jax.random.normal(ks[3], (D_MODEL, D_MODEL), dtype=jnp.float32) * s, 'bq': jnp.zeros((D_MODEL,), dtype=jnp.float32), 'Wk': jax.random.normal(ks[4], (D_MODEL, D_MODEL), dtype=jnp.float32) * s, 'bk': jnp.zeros((D_MODEL,), dtype=jnp.float32), 'Wv': jax.random.normal(ks[5], (D_MODEL, D_MODEL), dtype=jnp.float32) * s, 'bv': jnp.zeros((D_MODEL,), dtype=jnp.float32), 'Wo': jax.random.normal(ks[6], (D_MODEL, D_MODEL), dtype=jnp.float32) * s, 'bo': jnp.zeros((D_MODEL,), dtype=jnp.float32)}
        return inp
    _L1_xattn_all = _L1_xattn_setup()
    _L1_xattn_in = {k: v for k, v in _L1_xattn_all.items() if k in ('Wq', 'bq', 'Wk', 'bk', 'Wv', 'bv', 'Wo', 'bo')}
    del _L1_xattn_all

    def _L1_ffn_setup():
        import jax, jax.numpy as jnp
        import numpy as np
        B, S, D, F, E = (4, 256, 128, 512, 8)
        key = jax.random.key(seed)
        ks = jax.random.split(key, 7)
        s1 = 1.0 / np.sqrt(D)
        s2 = 1.0 / np.sqrt(F)
        x = jax.random.normal(ks[0], (B, S, D), dtype=jnp.float32)
        W1 = jax.random.uniform(ks[1], (E, D, F), jnp.float32, -s1, s1)
        b1 = jax.random.uniform(ks[2], (E, F), jnp.float32, -s1, s1)
        W2 = jax.random.uniform(ks[3], (E, F, D), jnp.float32, -s2, s2)
        b2 = jax.random.uniform(ks[4], (E, D), jnp.float32, -s2, s2)
        Wr = jax.random.uniform(ks[5], (D, E), jnp.float32, -s1, s1)
        br = jax.random.uniform(ks[6], (E,), jnp.float32, -s1, s1)
        return {'x': x, 'W1': W1, 'b1': b1, 'W2': W2, 'b2': b2, 'Wr': Wr, 'br': br}
    _L1_ffn_all = _L1_ffn_setup()
    _L1_ffn_in = {k: v for k, v in _L1_ffn_all.items() if k in ('W1', 'b1', 'W2', 'b2', 'Wr', 'br')}
    del _L1_ffn_all
    return {'x': x, 'ctx_1024': ctx_1024, 'mask_BxS2_bf1': mask_BxS2_bf1, 'g_xattn': g_xattn, 'g_ffn': g_ffn, 'L0_xattn_wq': _L0_xattn_in['wq'], 'L0_xattn_bq': _L0_xattn_in['bq'], 'L0_xattn_wk': _L0_xattn_in['wk'], 'L0_xattn_bk': _L0_xattn_in['bk'], 'L0_xattn_wv': _L0_xattn_in['wv'], 'L0_xattn_bv': _L0_xattn_in['bv'], 'L0_xattn_wo': _L0_xattn_in['wo'], 'L0_xattn_bo': _L0_xattn_in['bo'], 'L0_ffn_gate_w': _L0_ffn_in['gate_w'], 'L0_ffn_gate_b': _L0_ffn_in['gate_b'], 'L0_ffn_w1': _L0_ffn_in['w1'], 'L0_ffn_b1': _L0_ffn_in['b1'], 'L0_ffn_w2': _L0_ffn_in['w2'], 'L0_ffn_b2': _L0_ffn_in['b2'], 'L1_xattn_Wq': _L1_xattn_in['Wq'], 'L1_xattn_bq': _L1_xattn_in['bq'], 'L1_xattn_Wk': _L1_xattn_in['Wk'], 'L1_xattn_bk': _L1_xattn_in['bk'], 'L1_xattn_Wv': _L1_xattn_in['Wv'], 'L1_xattn_bv': _L1_xattn_in['bv'], 'L1_xattn_Wo': _L1_xattn_in['Wo'], 'L1_xattn_bo': _L1_xattn_in['bo'], 'L1_ffn_W1': _L1_ffn_in['W1'], 'L1_ffn_b1': _L1_ffn_in['b1'], 'L1_ffn_W2': _L1_ffn_in['W2'], 'L1_ffn_b2': _L1_ffn_in['b2'], 'L1_ffn_Wr': _L1_ffn_in['Wr'], 'L1_ffn_br': _L1_ffn_in['br']}

def reference(x, ctx_1024, mask_BxS2_bf1, g_xattn, g_ffn, L0_xattn_wq, L0_xattn_bq, L0_xattn_wk, L0_xattn_bk, L0_xattn_wv, L0_xattn_bv, L0_xattn_wo, L0_xattn_bo, L0_ffn_gate_w, L0_ffn_gate_b, L0_ffn_w1, L0_ffn_b1, L0_ffn_w2, L0_ffn_b2, L1_xattn_Wq, L1_xattn_bq, L1_xattn_Wk, L1_xattn_bk, L1_xattn_Wv, L1_xattn_bv, L1_xattn_Wo, L1_xattn_bo, L1_ffn_W1, L1_ffn_b1, L1_ffn_W2, L1_ffn_b2, L1_ffn_Wr, L1_ffn_br):
    import jax
    import jax.numpy as jnp

    def _L0_xattn_ref(query, key, value, wq, bq, wk, bk, wv, bv, wo, bo):
        import jax, jax.numpy as jnp
        import numpy as np
        D_MODEL = 128
        NHEAD = 16
        D_K = D_MODEL // NHEAD
        B, Sq, _ = query.shape
        Sk = key.shape[1]
        scale = 1.0 / np.sqrt(D_K).astype(np.float32)
        Q = (query @ wq.T + bq).reshape(B, Sq, NHEAD, D_K).transpose(0, 2, 1, 3)
        K = (key @ wk.T + bk).reshape(B, Sk, NHEAD, D_K).transpose(0, 2, 1, 3)
        V = (value @ wv.T + bv).reshape(B, Sk, NHEAD, D_K).transpose(0, 2, 1, 3)
        scores = jnp.einsum('bhqd,bhkd->bhqk', Q, K) * scale
        attn = jax.nn.softmax(scores, axis=-1)
        ctx = jnp.einsum('bhqk,bhkd->bhqd', attn, V)
        ctx = ctx.transpose(0, 2, 1, 3).reshape(B, Sq, D_MODEL)
        return ctx @ wo.T + bo

    def _L0_ffn_ref(x, gate_w, gate_b, w1, b1, w2, b2):
        import jax, jax.numpy as jnp
        import numpy as np
        D = 128
        N_EXP = 8
        TOP_K = 1
        b, s, d = x.shape
        xf = x.reshape(-1, d)
        logits = xf @ gate_w + gate_b
        pb = jax.nn.softmax(logits, axis=-1)
        _, idx = jax.lax.top_k(pb, TOP_K)
        sel = jnp.any(idx[:, :, None] == jnp.arange(N_EXP)[None, None, :], axis=1)
        weights = pb * sel

        def expert_step(acc, params):
            w1e, b1e, w2e, b2e, wgt = params
            h = jax.nn.gelu(xf @ w1e + b1e, approximate=False)
            y = h @ w2e + b2e
            return (acc + wgt[:, None] * y, None)
        out0 = jnp.zeros_like(xf)
        out, _ = jax.lax.scan(expert_step, out0, (w1, b1, w2, b2, weights.T))
        return out.reshape(b, s, d)

    def _L1_xattn_ref(q, k, v, attention_mask, Wq, bq, Wk, bk, Wv, bv, Wo, bo):
        import jax, jax.numpy as jnp
        import numpy as np
        N_HEADS = 16
        D_MODEL = 128
        HEAD_DIM = D_MODEL // N_HEADS
        MASK_FILL = -100000000.0

        def _split_heads(x):
            B, S, _ = x.shape
            return x.reshape(B, S, N_HEADS, HEAD_DIM).transpose(0, 2, 1, 3)
        qm = _split_heads(q @ Wq.T + bq)
        km = _split_heads(k @ Wk.T + bk)
        vm = _split_heads(v @ Wv.T + bv)
        scores = jnp.einsum('bnlh,bnph->bnlp', qm, km) / np.sqrt(HEAD_DIM).astype(np.float32)
        mask = attention_mask[:, None, None, :]
        scores = jnp.where(mask, scores, MASK_FILL)
        attn = jax.nn.softmax(scores, axis=-1)
        out = jnp.einsum('bnlp,bnph->bnlh', attn, vm)
        B, _, L, _ = out.shape
        out = out.transpose(0, 2, 1, 3).reshape(B, L, D_MODEL)
        return out @ Wo.T + bo

    def _L1_ffn_ref(x, W1, b1, W2, b2, Wr, br):
        import jax, jax.numpy as jnp
        import numpy as np
        B, S, D, F, E = (4, 256, 128, 512, 8)
        b, s, d = x.shape
        e = Wr.shape[1]
        logits = x @ Wr + br
        idx = jnp.argmax(logits, axis=-1)
        probs = jax.nn.softmax(logits, axis=-1)
        gates = jnp.take_along_axis(probs, idx[..., None], axis=-1)[..., 0]
        xf = x.reshape(-1, d)
        idxf = idx.reshape(-1)
        gf = gates.reshape(-1)
        out = jnp.zeros_like(xf)
        for ei in range(e):
            h = jax.nn.gelu(xf @ W1[ei] + b1[ei], approximate=False)
            y = h @ W2[ei] + b2[ei]
            mask = (idxf == ei).astype(xf.dtype)
            out = out + y * (gf * mask)[:, None]
        return out.reshape(b, s, d)
    x = x + jnp.tanh(g_xattn[0]) * _L0_xattn_ref(_layernorm(x, axis=-1), ctx_1024, ctx_1024, L0_xattn_wq, L0_xattn_bq, L0_xattn_wk, L0_xattn_bk, L0_xattn_wv, L0_xattn_bv, L0_xattn_wo, L0_xattn_bo)
    x = x + jnp.tanh(g_ffn[0]) * _L0_ffn_ref(_layernorm(x, axis=-1), L0_ffn_gate_w, L0_ffn_gate_b, L0_ffn_w1, L0_ffn_b1, L0_ffn_w2, L0_ffn_b2)
    x = x + jnp.tanh(g_xattn[1]) * _L1_xattn_ref(_layernorm(x, axis=-1), ctx_1024, ctx_1024, mask_BxS2_bf1, L1_xattn_Wq, L1_xattn_bq, L1_xattn_Wk, L1_xattn_bk, L1_xattn_Wv, L1_xattn_bv, L1_xattn_Wo, L1_xattn_bo)
    x = x + jnp.tanh(g_ffn[1]) * _L1_ffn_ref(_layernorm(x, axis=-1), L1_ffn_W1, L1_ffn_b1, L1_ffn_W2, L1_ffn_b2, L1_ffn_Wr, L1_ffn_br)
    return x

_drawn_inputs = setup_inputs


def setup_inputs(seed=0):
    import zlib

    import numpy as np

    out = dict(_drawn_inputs(seed))
    spreads = {'g_ffn': (-1.0, 0.6),
     'L0_xattn_bq': (0.0, 0.406),
     'L0_xattn_bk': (0.0, 0.8),
     'L0_xattn_bv': (0.0, 0.1),
     'L0_xattn_bo': (0.0, 0.1),
     'L0_ffn_gate_b': (0.0, 0.616),
     'L0_ffn_b1': (0.0, 0.8),
     'L0_ffn_b2': (0.0, 0.591),
     'L1_xattn_bq': (0.0, 0.368),
     'L1_xattn_bk': (0.0, 0.8),
     'L1_xattn_bv': (0.0, 0.1),
     'L1_xattn_bo': (0.0, 0.1)}
    factors = {'L0_ffn_gate_w': 3.924,
     'L0_ffn_w1': 7.091,
     'L0_ffn_w2': 6.512,
     'L1_ffn_b1': 8.0,
     'L1_ffn_b2': 8.0,
     'L1_ffn_br': 4.804}
    for name, (base, spread) in spreads.items():
        noise = np.random.default_rng([zlib.crc32(name.encode()), seed]).standard_normal(out[name].shape)
        drawn = base * np.exp(spread * noise) if base else spread * noise
        out[name] = jnp.asarray(drawn.astype(out[name].dtype))
    for name, factor in factors.items():
        out[name] = (out[name] * factor).astype(out[name].dtype)
    return out
```

```python
import numpy as np
from contextlib import ExitStack

import concourse.bass as bass
from concourse import mybir
from concourse.alu_op_type import AluOpType as ALU


class Group:

    def __init__(self, layer, turn, ring):
        self.layer, self.turn, self.ring = layer, turn, ring

    def at(self, k):
        r = self.ring + k
        return Group(self.layer, self.turn + r // 3, r % 3)

    @property
    def g(self):
        return self.turn * 3 + self.ring

    def count(self, n_groups):
        return self.turn * 3 + (self.ring + n_groups * self.layer)

    def laps(self, n_groups):
        return self.turn + self.layer * len(range(self.ring, n_groups, 3))


def wait(eng, sem, value):
    if isinstance(value, int) and value <= 0:
        return
    eng.wait_ge(sem, value)


def alone(eng, sem, value):
    wait(eng, sem, value)
    if not isinstance(value, int):
        eng.nop(nofuse=True)


def flamingo_kernel(nc, x, ctx_1024, mask_BxS2_bf1, g_xattn, g_ffn,
                    L0_xattn_wq, L0_xattn_bq, L0_xattn_wk, L0_xattn_bk, L0_xattn_wv, L0_xattn_bv, L0_xattn_wo,
                    L0_xattn_bo, L0_ffn_gate_w, L0_ffn_gate_b, L0_ffn_w1, L0_ffn_b1, L0_ffn_w2, L0_ffn_b2,
                    L1_xattn_Wq, L1_xattn_bq, L1_xattn_Wk, L1_xattn_bk, L1_xattn_Wv, L1_xattn_bv, L1_xattn_Wo,
                    L1_xattn_bo, L1_ffn_W1, L1_ffn_b1, L1_ffn_W2, L1_ffn_b2, L1_ffn_Wr, L1_ffn_br, out,
                    stage=99):
    f32, bf16, u8 = mybir.dt.float32, mybir.dt.bfloat16, mybir.dt.uint8
    i32, u32 = mybir.dt.int32, mybir.dt.uint32
    ACT = mybir.ActivationFunctionType
    AX = mybir.AxisListType.X

    NB, S, DM = x.shape
    H, DK = 16, 8
    GB = 2
    NG = NB // GB
    W = GB * S
    NP = H // 2
    PRODUCTS = [(0, 0), (0, 1), (0, 2), (1, 0), (1, 1), (2, 0)]
    NPR = len(PRODUCTS)
    RUNS = [(0, 3), (3, 2), (5, 1)]
    RP = 2 * NPR * DK
    RS = RP + 3
    RT = RS + 6
    E, F = L0_ffn_w1.shape[0], L0_ffn_w1.shape[2]
    FC = F // 128
    T = 128
    NT = NB * S // T + E - 1
    EPS = 1e-5
    SCALE = float(np.float32(1.0) / np.sqrt(np.float32(DK)))
    FILL = 1e8

    wqkvo = [(L0_xattn_wq, L0_xattn_wk, L0_xattn_wv, L0_xattn_wo), (L1_xattn_Wq, L1_xattn_Wk, L1_xattn_Wv, L1_xattn_Wo)]
    bqkvo = [(L0_xattn_bq, L0_xattn_bk, L0_xattn_bv, L0_xattn_bo), (L1_xattn_bq, L1_xattn_bk, L1_xattn_bv, L1_xattn_bo)]
    gates = [(L0_ffn_gate_w, L0_ffn_gate_b), (L1_ffn_Wr, L1_ffn_br)]

    stack = ExitStack()
    with stack:
        def sb(name, shape, dt=f32):
            return stack.enter_context(nc.sbuf_tensor(name, shape, dt))

        def sem(name):
            return stack.enter_context(nc.semaphore(name))

        def row(ap):
            return ap.rearrange("(a n) -> a n", a=1)

        x_sb = sb("x_sb", [128, NB, DM])
        xn2 = sb("xn2", [128, NB, DM])
        wnat = xn2[:, 0:8, :]
        wT = sb("wT", [128, 8, DM])
        bnat = sb("bnat", [4, DM])
        bperm = sb("bperm", [4, DM])
        bcol = sb("bcol", [128, 4])
        bvr = sb("bvr", [128, 2, DM])
        bor = sb("bor", [128, 2, DM])
        gr = sb("gr", [128, 4])
        tg = sb("tg", [128, 4])
        gw = sb("gw", [128, 2, E])
        gb = sb("gb", [128, 2, E])
        ident = sb("ident", [128, 128])
        identb = sb("identb", [128, 128], bf16)
        half = sb("half", [128, 2])
        ones_m = sb("ones_m", [128, 4, 32])
        maskrep = sb("maskrep", [128, NB * S], u8)
        mask8 = sb("mask8", [NB, S], u8)
        mval = sb("mval", [NB, S])
        mparts = sb("mparts", [NB, 3, S], bf16)
        mres = sb("mres", [NB, S])

        EW = 2 * F + FC + DM
        ex = sb("ex", [128, E, EW])
        b1T = sb("b1T", [128, 2, E * FC])
        b1n = sb("b1n", [E * FC, 2, 128])
        tri = sb("tri", [128, 128])
        ones = sb("ones", [128, 256])
        e_row = sb("e_row", [128, NB, E])
        t_row = sb("t_row", [1, NT, E])
        e_int, t_int = sb("e_int", [128, NB, E], i32), sb("t_int", [1, NT, E], i32)
        top, gsum, gate = sb("top", [128, NB]), sb("gsum", [128, NB]), sb("gate", [128, NB])
        below, expd = sb("below", [128, NB, E]), sb("expd", [128, NB, E])
        notop, first, chosen = sb("notop", [128, NB, E]), sb("first", [128, NB]), sb("chosen", [128, NB, E])
        tot, cum, pos = sb("tot", [128, E, NB]), sb("cum", [128, E, NB]), sb("pos", [128, E, NB])
        cnt, cumn, tiles, cumt, off = (sb(n, [128, E]) for n in ("cnt", "cumn", "tiles", "cumt", "off"))
        cnt_i = sb("cnt_i", [128, 2, E], i32)
        slot_f, slot = sb("slot_f", [128, NB]), sb("slot", [128, NB], u32)
        past, texp_f, texp = sb("past", [1, NT, E]), sb("texp_f", [1, NT]), sb("texp", [1, NT], i32)
        stg = [sb(f"stg{u}", [128, EW]) for u in range(2)]
        xs = [sb(f"xs{u}", [128, DM]) for u in range(2)]
        xsT = [sb(f"xsT{u}", [128, T]) for u in range(2)]
        hb = [sb(f"hb{u}", [128, FC, T]) for u in range(2)]
        hT = [sb(f"hT{u}", [128, FC, T]) for u in range(2)]
        ys = [sb(f"ys{u}", [128, DM]) for u in range(2)]
        yg = [sb(f"yg{j}", [128, GB, DM]) for j in range(3)]
        ixg = [sb(f"ixg{j}", [128, GB], u32) for j in range(3)]

        Qst = [sb(f"Qst{j}", [128, NP, 2, GB, S], bf16) for j in range(3)]
        Kst = [sb(f"Kst{j}", [128, NP, GB, S], bf16) for j in range(3)]
        Vm = [sb(f"Vm{j}", [128, GB, 4, 128]) for j in range(3)]
        cg = [sb(f"cg{j}", [128, GB, DM]) for j in range(3)]
        cgT = sb("cgT", [128, W])
        xn = sb("xn", [128, GB, DM])
        xn2g = sb("xn2g", [128, GB, DM])
        xT = sb("xT", [128, W])
        Qf, Kf = sb("Qf", [128, W]), sb("Kf", [128, W])
        qres, kres = sb("qres", [128, W]), sb("kres", [128, W])
        qp, kp = sb("qp", [128, 3, W], bf16), sb("kp", [128, 3, W], bf16)
        P = sb("P", [128, 2, 512])
        negm = sb("negm", [128, GB, 2, NP])
        nres = sb("nres", [128, GB, 2, NP])
        negp = sb("negp", [128, GB, 2, 3, NP], bf16)
        mT = sb("mT", [48, GB, 128], bf16)
        R = sb("R", [128, GB, 128])
        cT = sb("cT", [128, GB, 128])
        st1, st2 = sb("st1", [128, GB, 6]), sb("st2", [128, GB, 6])
        mv1, mv2 = sb("mv1", [128, GB, 2]), sb("mv2", [128, GB, 2])
        ve1, ve2 = sb("ve1", [128, GB]), sb("ve2", [128, GB])
        rs1, rs2 = sb("rs1", [128, GB]), sb("rs2", [128, GB])
        x2T = sb("x2T", [128, W])
        logits = sb("logits", [128, NB, E])

        SB = [stack.enter_context(nc.psum_tensor(f"SB{i}", [128, 512], f32)) for i in range(2)]
        ST = [stack.enter_context(nc.psum_tensor(f"ST{i}", [128, 512], f32)) for i in range(2)]
        PV = [stack.enter_context(nc.psum_tensor(f"PV{i}", [128, 512], f32)) for i in range(2)]
        M = [stack.enter_context(nc.psum_tensor(f"M{i}", [128, 512], f32)) for i in range(2)]

        q_dram = nc.dram_tensor("q_parts", [3, 3, 2 * DK, NP * 2 * W], bf16, kind="Internal").ap()
        k_dram = nc.dram_tensor("k_parts", [3, 3, 2 * DK, NP * W], bf16, kind="Internal").ap()
        m_dram = nc.dram_tensor("mask_parts", [3, NB * S], bf16, kind="Internal").ap()

        xs_dram = nc.dram_tensor("tokens_by_expert", [NT * T, DM], f32, kind="Internal").ap()
        ys_dram = nc.dram_tensor("expert_outputs", [NT * T, DM], f32, kind="Internal").ap()

        s_ex, s_b1l, s_b1t, s_b1s, s_xz = (sem(n) for n in (
            "experts_loaded", "b1_loaded", "b1_transposed", "b1_stored", "tokens_zeroed"))
        s_ri, s_rt = sem("route_constants"), sem("route_steps")
        s_rx, s_rc, s_slot = sem("route_exp"), sem("route_counts"), sem("slots_ready")
        s_sc = sem("tokens_scattered")
        s_sg = [sem(f"stage_filled{u}") for u in range(2)]
        s_xl = [sem(f"tile_loaded{u}") for u in range(2)]
        s_ysw = [sem(f"tile_written{u}") for u in range(2)]
        s_ft, s_fte, s_f1, s_fb, s_fg, s_f2, s_fy = (sem(n) for n in (
            "tile_transposed", "tileT_stored", "hidden_done", "hidden_biased", "hidden_gelu", "expert_done", "expert_stored"))
        s_ix, s_yg, s_xu = sem("index_copied"), [sem(f"rows_gathered{j}") for j in range(3)], sem("x_updated")
        s_w, s_x, s_b, s_mk = sem("w_loaded"), sem("x_loaded"), sem("small_loaded"), sem("mask_loaded")
        s_c = [sem(f"ctx_loaded{j}") for j in range(3)]
        s_bk = sem("bias_columns_loaded")
        s_id, s_cst, s_set = sem("ident_steps"), sem("constants_ready"), sem("setup_steps")
        s_tg, s_wtp, s_wte, s_wo_s = sem("tanh_ready"), sem("w_transposed"), sem("w_stored"), sem("out_w_scaled")
        s_mst, s_mpw = sem("mask_steps"), sem("mask_parts_written")
        s_st1, s_pw1, s_xn = sem("norm1_stats"), sem("norm1_rstd"), sem("xn_ready")
        s_v1, s_v2, s_ag1, s_ag2 = sem("norm1_eps"), sem("norm2_eps"), sem("norm1_bn"), sem("norm2_bn")
        s_xT, s_xTe = sem("xT_done"), sem("xT_stored")
        s_cTp, s_cTe = sem("ctxT_done"), sem("ctxT_stored")
        s_q, s_qf, s_k, s_kf, s_v, s_vm = (sem(n) for n in ("q_done", "q_stored", "k_done", "k_stored", "v_done", "v_stored"))
        s_qs, s_ks = sem("q_split"), sem("k_split")
        s_qi, s_ki, s_ni = sem("q_split_steps"), sem("k_split_steps"), sem("max_split_steps")
        s_sl, s_gt, s_rk = sem("slot_steps"), sem("gate_steps"), sem("route_rows")
        s_qt, s_kt = sem("q_rest"), sem("k_rest")
        s_qw, s_kw = [sem(f"q_parts_in_dram{j}") for j in range(3)], [sem(f"k_parts_in_dram{j}") for j in range(3)]
        s_qr, s_kr = [sem(f"q_stack_loaded{j}") for j in range(3)], [sem(f"k_stack_loaded{j}") for j in range(3)]
        s_s, s_max = sem("scores_done"), sem("max_done")
        s_ns, s_mTp, s_mTe = sem("max_split"), sem("max_transposed"), sem("max_stored")
        s_md = [sem(f"max_rows_loaded{b}") for b in range(GB)]
        s_st, s_exp, s_pv = sem("shifted_scores_done"), sem("exp_done"), sem("pv_done")
        s_rec, s_nrm, s_wo, s_xa = sem("recip_done"), sem("ctx_normed"), sem("out_proj_done"), sem("x_added")
        s_xb = sem("out_bias_added")
        s_st2, s_pw2, s_xn2 = sem("norm2_stats"), sem("norm2_rstd"), sem("xn2_ready")
        s_q0, s_dz, s_bT, s_bp, s_bc = (sem(n) for n in ("q_rows_zero", "dram_zeroed", "bias_transposed", "bias_permuted", "bias_columns"))
        s_qz, s_kz = sem("q_stacks_zero"), sem("k_stacks_set")
        s_x2k = sem("xn2_kept")
        s_x2T, s_x2Te, s_lg, s_lga = sem("xn2T_done"), sem("xn2T_stored"), sem("logits_done"), sem("logits_stored")
        s_out = sem("out_written")

        NXZ = -(-NT * T // 1024)
        expert_ins = [(L0_ffn_w1, L0_ffn_b1, L0_ffn_w2, L0_ffn_b2), (L1_ffn_W1, L1_ffn_b1, L1_ffn_W2, L1_ffn_b2)]
        NXD = 8

        def span(gr_):
            return bass.ds(gr_.g * GB, GB) if not isinstance(gr_.g, int) else slice(gr_.g * GB, gr_.g * GB + GB)

        def one(index):
            return bass.ds(index, 1) if not isinstance(index, int) else slice(index, index + 1)

        def cols(gr_):
            return bass.ds(gr_.g * W, W) if not isinstance(gr_.g, int) else slice(gr_.g * W, gr_.g * W + W)

        def turns(layer, step):
            def parts(g):
                return {"A1": -3 <= g <= NG - 4, "A2": -2 <= g <= NG - 3, "B": -1 <= g <= NG - 2,
                        "C": 0 <= g <= NG - 1, "D": 1 <= g <= NG}
            first, rounds = 2, (NG - 5) // 3
            for g in range(-3, first):
                step(Group(layer, g // 3, g % 3), **parts(g))
            yield rounds, lambda i: [step(Group(layer, i + (first + u) // 3, (first + u) % 3), **parts(first))
                                     for u in range(3)]
            for g in range(first + 3 * rounds, NG + 1):
                step(Group(layer, g // 3, g % 3), **parts(g))

        def tile_rows(i):
            return slice(i * T, i * T + T) if isinstance(i, int) else bass.ds(i * T, T)

        def tile_laps(L, i, u):
            return L * len(range(u, NT, 2)) + (i // 2)

        def experts(eng, L, step):
            for i in range(-2, 2):
                step(L, i, i % 2, T2=True, F1=i >= -1, F2=i >= 0)
            full = (NT - 2) // 2 * 2
            with eng.Fori(1, full // 2) as h:
                for u in range(2):
                    step(L, h * 2 + u, u, T2=True, F1=True, F2=True)
            for i in range(full, NT):
                step(L, i, i % 2, T2=i + 2 < NT, F1=i + 1 < NT, F2=True)

        def attention(eng, layer, step):
            for n, body in turns(layer, step):
                with eng.Fori(0, n) as i:
                    body(i)

        block = stack.enter_context(nc.Block())

        @block.sync
        def _(sp):
            for L in range(2):
                for n in range(4):
                    sp.dma_start(wnat[:, 4 * L + n, :], wqkvo[L][n]).then_inc(s_w, 16)
            for n in range(NXD):
                k = NB // NXD
                sp.dma_start(x_sb[:, n * k:(n + 1) * k, :], x[n * k:(n + 1) * k].rearrange("b s d -> s b d")).then_inc(s_x, 16)
            sp.dma_start(maskrep[:, :], mask_BxS2_bf1.rearrange("b s -> (b s)").partition_broadcast(128)).then_inc(s_mk, 16)
            sp.dma_start(mask8[:, :], mask_BxS2_bf1).then_inc(s_mk, 16)
            def expert_loads(L):
                w1, b1, w2, b2 = expert_ins[L]
                sp.dma_start(ex[:, :, 0:F], w1.rearrange("e p n -> p e n")).then_inc(s_ex, 16)
                for c in range(FC):
                    sp.dma_start(ex[:, :, F + c * DM:F + (c + 1) * DM],
                                 w2[:, c * 128:(c + 1) * 128, :].rearrange("e p n -> p e n")).then_inc(s_ex, 16)
                sp.dma_start(ex[:, :, 2 * F + FC:EW], b2.partition_broadcast(128)).then_inc(s_ex, 16)

            for L in range(2):
                sp.dma_start(b1n[:, L, :], expert_ins[L][1].rearrange("e (c p) -> (e c) p", p=128)).then_inc(s_b1l, 16)
            expert_loads(0)
            sp.wait_ge(s_qz, 1)
            for n in range(0, NT * T, 1024):
                k = min(1024, NT * T - n) // 64
                sp.dma_start(xs_dram[n:n + k * 64].rearrange("(k p) d -> p k d", p=64),
                             Qst[0][0:64, :, :, :, :].rearrange("r p s b q -> r (p s b q)")[:, 0:2 * k * DM].bitcast(f32)
                             .rearrange("p (k d) -> p k d", k=k)).then_inc(s_xz, 16)
            sp.wait_ge(s_qz, 1)
            for j in range(3):
                sp.dma_start(q_dram[j].rearrange("t r n -> (t r) n"), Qst[0][0:6 * DK].rearrange("r p s b q -> r (p s b q)")
                             ).then_inc(s_dz, 16)
            sp.wait_ge(s_mst, 5)
            sp.dma_start(m_dram.rearrange("r (b k) -> b r k", b=NB), mparts[:, :, :]).then_inc(s_mpw, 16)

            def step(c, A1, A2, B, C, D):
                a, a1 = c.at(2), c.at(3)
                if A1:
                    alone(sp, s_cTp, a1.count(NG) - 2)
                    sp.dma_start(cg[a1.ring][:, :, :], ctx_1024[span(a1)].rearrange("b s d -> s b d")).then_inc(s_c[a1.ring], 16)
                if A2:
                    j, N = a.ring, a.count(NG)
                    alone(sp, s_st, (N - 3) * 8 + 8)
                    if isinstance(a.g, int) and a.g == 0:
                        sp.wait_ge(s_cst, 12)
                        sp.wait_ge(s_kz, 6)
                        sp.wait_ge(s_mpw, 16)
                        sp.wait_ge(s_dz, 48)
                        sp.wait_ge(s_xz, NXZ * 16)
                    alone(sp, s_qs, N + 1)
                    for s in range(2):
                        sp.dma_start(q_dram[j][:, s * DK:(s + 1) * DK, :].rearrange("t d (p s n) -> s (d p) t n", p=NP, s=2)[s],
                                     qp[64 * s:64 * s + 64, :, :]).then_inc(s_qw[j], 16)
                    alone(sp, s_ks, N + 1)
                    sp.dma_start(k_dram[j].rearrange("t r (p n) -> (r p) t n", p=NP), kp[:, :, :]).then_inc(s_kw[j], 16)
                    alone(sp, s_qw[j], (a.laps(NG) + 1) * 32)
                    for n, runs in RUNS:
                        t = PRODUCTS[n][0]
                        sp.dma_start(Qst[j][2 * DK * n:2 * DK * (n + runs)].rearrange("r p s b q -> r (p s b q)"),
                                     q_dram[j, t:t + 1].to_broadcast([runs, 2 * DK, NP * 2 * W])).then_inc(s_qr[j], 16)
                    alone(sp, s_kw[j], (a.laps(NG) + 1) * 16)
                    for n, runs in RUNS:
                        t = PRODUCTS[n][1]
                        sp.dma_start(Kst[j][2 * DK * n:2 * DK * (n + runs)].rearrange("r p b k -> r (p b k)"),
                                     k_dram[j, t:t + runs].rearrange("t r n -> (t r) n")).then_inc(s_kr[j], 16)
                    if a.layer == 1:
                        src = m_dram[:, cols(a)].rearrange("r (o n) -> r o n", o=1).to_broadcast([3, NP, W])
                        sp.dma_start(Kst[j][RP:RS].rearrange("r p b k -> r p (b k)"), src).then_inc(s_kr[j], 16)

            def tile_load(L, i, u):
                alone(sp, s_ft, L * NT + i - 1)
                sp.dma_start(xs[u][:, :], xs_dram[tile_rows(i), :]).then_inc(s_xl[u], 16)

            def tile_store(L, i, u):
                alone(sp, s_fy, L * NT + i + 1)
                sp.dma_start(ys_dram[tile_rows(i), :], ys[u][:, :]).then_inc(s_ysw[u], 16)

            def slot_step(L, i, u, T2, F1, F2):
                if T2:
                    tile_load(L, i + 2, u)
                if F2:
                    tile_store(L, i, u)

            for L in range(1 if stage == 0 else 2):
                attention(sp, L, step)
                if stage == 0:
                    break
                sp.wait_ge(s_sc, (L + 1) * NB * 16)
                experts(sp, L, slot_step)
                if L == 0:
                    for u in range(2):
                        sp.wait_ge(s_sg[u], len(range(u, NT, 2)))
                    expert_loads(1)
            if stage > 0:
                for g in range(NG):
                    sp.wait_ge(s_xu, (NG + g + 1) * GB)
                    sp.dma_start(out[g * GB:g * GB + GB].rearrange("b s d -> s b d"),
                                 x_sb[:, g * GB:g * GB + GB, :]).then_inc(s_out, 16)
                sp.wait_ge(s_out, NG * 16)
            if stage == 0:
                sp.wait_ge(s_xa, NB)
                sp.wait_ge(s_lga, NG)
                sp.dma_start(out.rearrange("b s d -> s b d"), x_sb[:, :, :]).then_inc(s_out, 16)
                sp.wait_ge(s_out, 16)

        def k_loads(gr_):
            plain, masked = len(RUNS) * 16, (len(RUNS) + 1) * 16
            if gr_.layer == 0:
                return (gr_.turn + 1) * plain
            return len(range(gr_.ring, NG, 3)) * plain + (gr_.turn + 1) * masked

        @block.gpsimd
        def _(pool):
            pool.memset(ident[:, :], 0.0).then_inc(s_id, 1)
            pool.memset(ones_m[:, :, :], 0.0).then_inc(s_id, 1)
            pool.memset(half[:, :], -0.5).then_inc(s_cst, 1)
            pool.wait_ge(s_id, 2)
            pool.affine_select(out=ident[:, :], in_=ident[:, :], compare_op=ALU.not_equal, fill=1.0, base=0,
                               pattern=[[-1, 128]], channel_multiplier=1).then_inc(s_id, 1)
            for j in range(3):
                if j == 0:
                    pool.memset(Qst[j][:, :, :, :, :], 0.0).then_inc(s_qz, 1)
                pool.memset(Vm[j][:, :, :, :], 0.0).then_inc(s_cst, 1)
            for k in range(4):
                pool.memset(ones_m[:, k, 8 * k:8 * k + 8], 1.0).then_inc(s_cst, 1)
            pool.wait_ge(s_id, 3)
            pool.tensor_copy(identb[:, :], ident[:, :]).then_inc(s_cst, 1)

            def split(src, res, parts, steps, base, done):
                pool.tensor_copy(parts(0), src).then_inc(steps, 1)
                pool.wait_ge(steps, base + 1)
                pool.tensor_tensor(res, src, parts(0), ALU.subtract).then_inc(steps, 1)
                alone(pool, steps, base + 2)
                pool.tensor_copy(parts(1), res).then_inc(steps, 1)
                pool.wait_ge(steps, base + 3)
                pool.tensor_tensor(parts(2), res, parts(1), ALU.subtract).then_inc(done, 1)

            def rests(src, res, parts, rounded, rest, done, N):
                pool.wait_ge(rounded, 2 * N + 1)
                pool.tensor_tensor(res, src, parts[:, 0, :], ALU.subtract).then_inc(rest, 1)
                pool.wait_ge(rounded, 2 * N + 2)
                pool.tensor_tensor(parts[:, 2, :], res, parts[:, 1, :], ALU.subtract).then_inc(done, 1)

            def max_split(gr_, b):
                n = gr_.count(NG) * GB + b
                pool.wait_ge(s_max, gr_.count(NG) * 8 + 4 * b + 4)
                alone(pool, s_mTp, n - 1)
                split(negm[:, b, :, :], nres[:, b, :, :], lambda t: negp[:, b, :, t, :], s_ni, n * 3, s_ns)

            def rstd(stats, mv, ve, rs, s_stat, s_v, s_pw, N):
                alone(pool, s_stat, N + 1)
                pool.tensor_scalar_add(ve[:, :], mv[:, :, 1], EPS).then_inc(s_v, 1)
                pool.wait_ge(s_v, N + 1)
                pool.tensor_tensor(rs[:, :], ve[:, :], half[:, :], ALU.pow).then_inc(s_pw, 1)

            def gather(gr_, indices, N):
                j = gr_.ring
                pool.tensor_copy(ixg[j][:, :], indices).then_inc(s_ix, 1)
                alone(pool, s_ix, N + 1)
                for b in range(GB):
                    pool.indirect_dma_start(
                        out=yg[j][:, b, :], out_offset=None, in_=ys_dram[:, :],
                        in_offset=bass.IndirectOffsetOnAxis(ap=ixg[j][:, b:b + 1], axis=0)).then_inc(s_yg[j], 16)

            def step(c, A1, A2, B, C, D):
                s, a, d, a1 = c.at(1), c.at(2), c.at(-1), c.at(3)
                if A1 and a1.layer == 1:
                    gather(a1, slot[:, span(a1)], a1.g)
                if C:
                    max_split(c, 1)
                if A2:
                    N = a.count(NG)
                    rests(Qf[:, :], qres[:, :], qp, s_qi, s_qt, s_qs, N)
                    rests(Kf[:, :], kres[:, :], kp, s_ki, s_kt, s_ks, N)
                    pool.wait_ge(s_xn, N + 1)
                    pool.tensor_tensor(x_sb[:, span(a), :], x_sb[:, span(a), :],
                                       bor[:, a.layer:a.layer + 1, :].to_broadcast([128, GB, DM]), ALU.add).then_inc(s_xb, 1)
                if D:
                    rstd(st2, mv2, ve2, rs2, s_ag2, s_v2, s_pw2, d.count(NG))
                if B:
                    max_split(s, 0)
                if A1:
                    rstd(st1, mv1, ve1, rs1, s_ag1, s_v1, s_pw1, a1.count(NG))
                if D:
                    pool.wait_ge(s_xn2, d.count(NG) + 1)
                    pool.tensor_copy(xn2[:, span(d), :], xn2g[:, :, :]).then_inc(s_x2k, 1)

            pool.iota(e_int[:, :, :], pattern=[[0, NB], [1, E]], base=0, channel_multiplier=0).then_inc(s_ri, 1)
            pool.iota(t_int[:, :, :], pattern=[[1, NT], [0, E]], base=0, channel_multiplier=0).then_inc(s_ri, 1)
            pool.memset(tri[:, :], 1.0).then_inc(s_ri, 1)
            pool.wait_ge(s_ri, 3)
            pool.affine_select(out=tri[:, :], in_=tri[:, :], compare_op=ALU.is_gt, fill=0.0, base=0,
                               pattern=[[1, 128]], channel_multiplier=-1).then_inc(s_ri, 1)
            pool.memset(ones[:, :], 1.0).then_inc(s_ri, 1)

            def slot_step(L, i, u, T2, F1, F2):
                if F1:
                    t = i + 1
                    e = pool.value_load(texp[0:1, one(t)], min_val=0, max_val=E - 1)
                    wait(pool, s_fy, L * NT + t - 1)
                    pool.tensor_copy(stg[1 - u][:, :], ex[:, bass.ds(e, 1), :].rearrange("p o n -> p (o n)")
                                     ).then_inc(s_sg[1 - u], 1)

            pool.wait_ge(s_wo_s, 5)
            for L in range(1 if stage == 0 else 2):
                if L == 1:
                    for u in range(2):
                        pool.wait_ge(s_ysw[u], len(range(u, NT, 2)) * 16)
                attention(pool, L, step)
                if stage == 0:
                    break
                pool.wait_ge(s_slot, L + 1)
                pool.wait_ge(s_ex, (L + 1) * 6 * 16)
                pool.wait_ge(s_b1s, L + 2)
                if L == 0:
                    pool.wait_ge(s_xz, NXZ * 16)
                else:
                    for u in range(2):
                        pool.wait_ge(s_xl[u], len(range(u, NT, 2)) * 16)
                for b in range(NB):
                    if b == 0:
                        pool.wait_ge(s_x2k, NG * (L + 1))
                    pool.indirect_dma_start(
                        out=xs_dram[:, :], out_offset=bass.IndirectOffsetOnAxis(ap=slot[:, b:b + 1], axis=0),
                        in_=xn2[:, b, :], in_offset=None).then_inc(s_sc, 16)
                experts(pool, L, slot_step)
            if stage > 0:
                for u in range(2):
                    pool.wait_ge(s_ysw[u], 2 * len(range(u, NT, 2)) * 16)
                for g in range(NG):
                    gr_ = Group(2, g // 3, g % 3)
                    if g >= 3:
                        pool.wait_ge(s_xu, (NG + g - 3 + 1) * GB)
                    gather(gr_, slot[:, g * GB:g * GB + GB], NG + g)

        @block.scalar
        def _(act):
            for L in range(2):
                for n in (0, 1):
                    act.dma_start(bnat[2 * L + n:2 * L + n + 1, :], row(bqkvo[L][n])).then_inc(s_bk, 16)
                act.dma_start(bvr[:, L, :], bqkvo[L][2].partition_broadcast(128)).then_inc(s_b, 16)
                act.dma_start(bor[:, L, :], bqkvo[L][3].partition_broadcast(128)).then_inc(s_b, 16)
                act.dma_start(gw[:, L, :], gates[L][0]).then_inc(s_b, 16)
                act.dma_start(gb[:, L, :], gates[L][1].partition_broadcast(128)).then_inc(s_b, 16)
            act.dma_start(gr[:, 0:2], g_xattn.partition_broadcast(128)).then_inc(s_b, 16)
            act.dma_start(gr[:, 2:4], g_ffn.partition_broadcast(128)).then_inc(s_b, 16)
            act.wait_ge(s_b, 10 * 16)
            act.activation(tg[:, :], gr[:, :], ACT.Tanh).then_inc(s_tg, 1)

            def first_part(gr_, src, parts, ready, written, each, rounded):
                N = gr_.count(NG)
                act.wait_ge(ready, N + 1)
                if not (isinstance(N, int) and N == 0):
                    before = Group(0, (NG - 1) // 3, (NG - 1) % 3) if isinstance(gr_.g, int) and gr_.g == 0 else gr_.at(-1)
                    act.wait_ge(written[before.ring], (before.laps(NG) + 1) * each)
                act.activation(parts[:, 0, :], src[:, :], ACT.Copy).then_inc(rounded, 1)

            def second_part(gr_, res, parts, rest, rounded):
                act.wait_ge(rest, gr_.count(NG) + 1)
                act.activation(parts[:, 1, :], res[:, :], ACT.Copy).then_inc(rounded, 1)

            def keep_max(gr_, b):
                n = gr_.count(NG) * GB + b
                act.wait_ge(s_mTp, n + 1)
                wait(act, s_md[b], (gr_.count(NG)) * 32)
                act.activation(mT[:, b, :], M[b][0:48, 0:64].bitcast(bf16), ACT.Copy).then_inc(s_mTe, 1)
                act.wait_ge(s_mTe, n + 1)
                for s in range(2):
                    act.dma_start(Qst[gr_.ring][RS + 3 * s:RS + 3 * s + 3, :, s, b, :],
                                  mT[24 * s:24 * s + 24, b, :]).then_inc(s_md[b], 16)

            def step(c, A1, A2, B, C, D):
                s, a, d = c.at(1), c.at(2), c.at(-1)
                for n in range(8):
                    if C:
                        m = c.count(NG) * 8 + n
                        act.wait_ge(s_st, m + 1)
                        wait(act, s_pv, m - 1)
                        act.activation(P[:, n % 2, :], ST[n % 2][:, :], ACT.Exp).then_inc(s_exp, 1)
                    if n == 0 and A2:
                        act.wait_ge(s_xT, a.count(NG) + 1)
                        wait(act, s_q, a.count(NG))
                        act.activation(xT[:, :], M[0][:, 0:W], ACT.Copy).then_inc(s_xTe, 1)
                    if n == 1:
                        if C:
                            keep_max(c, 1)
                        if A2:
                            act.wait_ge(s_q, a.count(NG) + 1)
                            wait(act, s_qs, a.count(NG))
                            act.activation(Qf[:, :], M[0][:, 0:W], ACT.Identity, scale=SCALE,
                                           bias=bcol[:, 2 * a.layer:2 * a.layer + 1]).then_inc(s_qf, 1)
                            first_part(a, Qf, qp, s_qf, s_qw, 32, s_qi)
                    if n == 2 and A2:
                        act.wait_ge(s_cTp, a.count(NG) + 1)
                        wait(act, s_v, a.count(NG))
                        act.activation(cgT[:, :], M[1][:, 0:W], ACT.Copy).then_inc(s_cTe, 1)
                    if n == 2 and A2:
                        second_part(a, qres, qp, s_qt, s_qi)
                    if n == 3 and A2:
                        if a.layer == 0:
                            act.wait_ge(s_k, a.count(NG) + 1)
                            wait(act, s_ks, a.count(NG))
                            act.activation(Kf[:, :], M[0][:, 0:W], ACT.Identity, bias=bcol[:, 1:2]).then_inc(s_kf, 1)
                        first_part(a, Kf, kp, s_kf, s_kw, 16, s_ki)
                    if n == 4 and A2:
                        second_part(a, kres, kp, s_kt, s_ki)
                    if n == 5 and B:
                        keep_max(s, 0)
                    if n == 6 and D:
                        act.wait_ge(s_x2T, d.count(NG) + 1)
                        wait(act, s_lg, d.count(NG))
                        act.activation(x2T[:, :], M[1][:, 0:W], ACT.Copy).then_inc(s_x2Te, 1)

            def slot_step(L, i, u, T2, F1, F2):
                if T2:
                    n = L * NT + i + 2
                    act.wait_ge(s_ft, n + 1)
                    wait(act, s_f1, n - 1)
                    act.activation(xsT[u][:, :], M[u][:, 0:T], ACT.Copy).then_inc(s_fte, 1)
                if F1:
                    n = L * NT + i + 1
                    act.wait_ge(s_fb, n + 1)
                    wait(act, s_f2, n - 1)
                    act.activation(hT[1 - u][:, :, :], hb[1 - u][:, :, :], ACT.Gelu).then_inc(s_fg, 1)

            act.wait_ge(s_wo_s, 5)
            for L in range(1 if stage == 0 else 2):
                attention(act, L, step)
                if stage == 0:
                    break
                act.wait_ge(s_rt, L * 16 + 2)
                act.activation(expd[:, :, :], below[:, :, :], ACT.Exp).then_inc(s_rx, 1)
                experts(act, L, slot_step)

        @block.vector
        def _(dve):
            for j in range(3):
                dve.memset(Kst[j][96:128, :, :, :], 1.0).then_inc(s_kz, 1)
                dve.wait_ge(s_kz, 2 * j + 1)
                dve.memset(Kst[j][96:96 + 3, :, :, :], 0.0).then_inc(s_kz, 1)
                if j == 0:
                    dve.wait_ge(s_qz, 1)
                else:
                    dve.memset(Qst[j][96:128, :, :, :, :], 0.0).then_inc(s_q0, 1)
                    dve.wait_ge(s_q0, j)
                dve.memset(Qst[j][96:96 + 3, :, :, :, :], 1.0).then_inc(s_cst, 1)
            for L in range(2):
                for n in range(4):
                    m = 4 * L + n
                    dve.wait_ge(s_wtp, m + 1)
                    src = M[m % 2][:, 0:128]
                    if n < 2:
                        for s in range(2):
                            last = dve.tensor_copy(wT[:, m, :].rearrange("p (s d k e) -> p s d k e", s=2, d=DK, k=4)[:, s],
                                                   src.rearrange("p (e s k d) -> p s d k e", s=2, d=DK, k=4)[:, s])
                        last.then_inc(s_wte, 1)
                    else:
                        dve.tensor_copy(wT[:, m, :], src).then_inc(s_wte, 1)
            dve.wait_ge(s_tg, 1)
            dve.wait_ge(s_wte, 8)
            dve.wait_ge(s_bk, 4 * 16)
            for s in range(2):
                last = dve.tensor_copy(bperm[:, :].rearrange("p (s d k e) -> p s d k e", s=2, d=DK, k=4)[:, s],
                                       bnat[:, :].rearrange("p (e s k d) -> p s d k e", s=2, d=DK, k=4)[:, s])
            last.then_inc(s_bp, 1)
            dve.wait_ge(s_bT, 1)
            dve.tensor_copy(bcol[:, :], M[0][:, 0:4]).then_inc(s_bc, 1)
            dve.wait_ge(s_bc, 1)
            for L in range(2):
                dve.tensor_scalar(wT[:, 4 * L + 3, :], wT[:, 4 * L + 3, :], tg[:, L:L + 1], None, ALU.mult).then_inc(s_wo_s, 1)
                dve.tensor_scalar(bor[:, L, :], bor[:, L, :], tg[:, L:L + 1], None, ALU.mult).then_inc(s_wo_s, 1)
            dve.tensor_scalar(bcol[:, :].rearrange("p (l n) -> p l n", n=2)[:, :, 0],
                              bcol[:, :].rearrange("p (l n) -> p l n", n=2)[:, :, 0], SCALE, None, ALU.mult).then_inc(s_wo_s, 1)
            dve.wait_ge(s_mk, 32)
            dve.tensor_scalar(mval[:, :], mask8[:, :], FILL, -FILL, ALU.mult, ALU.add).then_inc(s_mst, 1)
            dve.wait_ge(s_mst, 1)
            dve.tensor_copy(mparts[:, 0, :], mval[:, :]).then_inc(s_mst, 1)
            dve.wait_ge(s_mst, 2)
            dve.tensor_tensor(mres[:, :], mval[:, :], mparts[:, 0, :], ALU.subtract).then_inc(s_mst, 1)
            dve.wait_ge(s_mst, 3)
            dve.tensor_copy(mparts[:, 1, :], mres[:, :]).then_inc(s_mst, 1)
            dve.wait_ge(s_mst, 4)
            dve.tensor_tensor(mparts[:, 2, :], mres[:, :], mparts[:, 1, :], ALU.subtract).then_inc(s_mst, 1)

            def norm(gr_, b):
                n = gr_.count(NG) * GB + b
                dve.wait_ge(s_pv, gr_.count(NG) * 8 + 4 * b + 4)
                dve.reciprocal(R[:, b, :], PV[b][:, 128:256]).then_inc(s_rec, 1)
                dve.wait_ge(s_rec, n + 1)
                wait(dve, s_wo, n - 1)
                dve.tensor_tensor(cT[:, b, :], PV[b][:, 0:128], R[:, b, :], ALU.mult).then_inc(s_nrm, 1)

            def x_add(gr_, b):
                n = gr_.count(NG) * GB + b
                dve.wait_ge(s_wo, n + 1)
                dve.wait_ge(s_xb, gr_.count(NG) + 1)
                at = one(gr_.g * GB + b)
                dve.tensor_tensor(x_sb[:, at, :], x_sb[:, at, :],
                                  PV[b][:, 256:384].rearrange("p (o n) -> p o n", o=1), ALU.add).then_inc(s_xa, 1)

            def x_update(gr_, layer, N, j):
                dve.wait_ge(s_yg[j], (gr_.turn + 1 + (layer - 1) * len(range(j, NG, 3))) * GB * 16)
                for b in range(GB):
                    at = one(gr_.g * GB + b)
                    dve.scalar_tensor_tensor(x_sb[:, at, :], yg[j][:, b:b + 1, :], gate[:, at], x_sb[:, at, :],
                                             ALU.mult, ALU.add).then_inc(s_xu, 1)

            def stats(gr_, st, mv, s_stat, s_agg, s_used, N):
                alone(dve, s_used, N)
                for b in range(GB):
                    dve.bn_stats(st[:, b, :], x_sb[:, one(gr_.g * GB + b), :].rearrange("p o n -> p (o n)")).then_inc(s_stat, 1)
                for b in range(GB):
                    alone(dve, s_stat, N * GB + b + 1)
                    last = dve.bn_aggr(mv[:, b, :], st[:, b, :])
                last.then_inc(s_agg, 1)

            def normed(gr_, mv, rs, to, done):
                for b in range(GB):
                    last = dve.tensor_scalar(to(b), x_sb[:, one(gr_.g * GB + b), :], mv[:, b, 0:1], rs[:, b:b + 1],
                                             ALU.subtract, ALU.mult)
                last.then_inc(done, 1)

            def step(c, A1, A2, B, C, D):
                s, a, d, a1 = c.at(1), c.at(2), c.at(-1), c.at(3)
                for n in range(8):
                    if B:
                        m = s.count(NG) * 8 + n
                        b, k = n // 4, n % 4
                        dve.wait_ge(s_s, m + 1)
                        if k == 0:
                            wait(dve, s_ns, s.count(NG) * GB + b - 1)
                        dve.tensor_reduce(negm[:, b, :, 2 * k:2 * k + 2].rearrange("q s e -> q e s"),
                                          SB[n % 2][:, :].rearrange("q (e s k) -> q e s k", e=2, s=2), AX, ALU.max,
                                          negate=True).then_inc(s_max, 1)
                    if n == 0 and D:
                        norm(d, 1)
                    if n == 3 and D:
                        x_add(d, 1)
                    if n == 3 and A2 and a.layer == 1:
                        dve.wait_ge(s_k, a.count(NG) + 1)
                        wait(dve, s_ks, a.count(NG))
                        dve.scalar_tensor_tensor(Kf[:, :], M[0][:, 0:W], bcol[:, 3:4], maskrep[:, cols(a)],
                                                 ALU.add, ALU.mult).then_inc(s_kf, 1)
                    if n == 4:
                        if C:
                            norm(c, 0)
                        if A2:
                            dve.wait_ge(s_v, a.count(NG) + 1)
                            wait(dve, s_pv, (a.count(NG) - 3) * 8 + 8)
                            for k in range(4):
                                last = dve.tensor_tensor(
                                    Vm[a.ring][:, :, k, :].rearrange("p b (g c) -> p b g c", c=32)[:, :, :, 8 * k:8 * k + 8],
                                    M[1][:, 0:W].rearrange("p (b g k d) -> p k b g d", b=GB, k=4, d=DK)[:, k],
                                    bvr[:, a.layer:a.layer + 1, :].to_broadcast([128, GB, DM]).rearrange(
                                        "p b (g k d) -> p k b g d", k=4, d=DK)[:, k], ALU.add)
                            last.then_inc(s_vm, 1)
                        if D:
                            alone(dve, s_xa, (d.count(NG) + 1) * GB)
                            stats(d, st2, mv2, s_st2, s_ag2, s_xn2, d.count(NG))
                    if n == 5:
                        if A1:
                            if a1.layer == 0:
                                dve.wait_ge(s_x, 16 * NXD)
                            else:
                                x_update(a1, 1, a1.g, a1.ring)
                                alone(dve, s_xu, (a1.g + 1) * GB)
                            stats(a1, st1, mv1, s_st1, s_ag1, s_xn, a1.count(NG))
                        if D:
                            dve.wait_ge(s_pw2, d.count(NG) + 1)
                            wait(dve, s_x2T, d.count(NG))
                            wait(dve, s_x2k, d.count(NG))
                            normed(d, mv2, rs2, lambda b: xn2g[:, b:b + 1, :], s_xn2)
                    if n == 6 and A1:
                        dve.wait_ge(s_pw1, a1.count(NG) + 1)
                        wait(dve, s_xT, a1.count(NG))
                        normed(a1, mv1, rs1, lambda b: xn[:, b:b + 1, :], s_xn)
                    if n == 7:
                        if C:
                            x_add(c, 0)
                        if D:
                            dve.wait_ge(s_lg, d.count(NG) + 1)
                            dve.tensor_tensor(logits[:, span(d), :], M[0][:, 0:GB * E].rearrange("p (b e) -> p b e", e=E),
                                              gb[:, d.layer:d.layer + 1, :].to_broadcast([128, GB, E]), ALU.add).then_inc(s_lga, 1)

            def route(L):
                R0 = L * 16
                n = [R0]

                def then(ins):
                    n[0] += 1
                    ins.then_inc(s_rt, 1)
                    dve.wait_ge(s_rt, n[0])

                dve.wait_ge(s_b1s, L + 1)
                if L == 1:
                    for u in range(2):
                        dve.wait_ge(s_sg[u], len(range(u, NT, 2)))
                dve.tensor_copy(ex[:, :, 2 * F:2 * F + FC], b1T[:, L, :].rearrange("p (e c) -> p e c", c=FC)).then_inc(s_b1s, 1)
                dve.wait_ge(s_lga, NG * (L + 1))
                every = lambda a: a.rearrange("p (b o) -> p b o", o=1).to_broadcast([128, NB, E])
                by_e = lambda a: a.rearrange("p (e o) -> p e o", o=1).to_broadcast([128, E, NB])
                then(dve.tensor_reduce(top[:, :], logits[:, :, :], AX, ALU.max))
                if L == 1:
                    pass
                then(dve.tensor_tensor(below[:, :, :], logits[:, :, :], every(top[:, :]), ALU.subtract))
                then(dve.tensor_scalar(notop[:, :, :], below[:, :, :], 0.0, float(E), ALU.is_lt, ALU.mult))
                then(dve.tensor_tensor(notop[:, :, :], notop[:, :, :], e_row[:, :, :], ALU.add))
                then(dve.tensor_reduce(first[:, :], notop[:, :, :], AX, ALU.min))
                then(dve.tensor_tensor(chosen[:, :, :], e_row[:, :, :], every(first[:, :]), ALU.is_equal))
                dve.wait_ge(s_rc, L + 1)
                then(dve.tensor_copy(tot[:, :, :], PV[0][:, 256:512].rearrange("p (b e) -> p e b", e=E)))
                then(dve.tensor_reduce(cnt[:, :], tot[:, :, :], AX, ALU.add))
                dve.tensor_scalar(cnt_i[:, 0, :], cnt[:, :], float(T - 1), None, ALU.add).then_inc(s_set, 1)
                dve.wait_ge(s_set, L * 5 + 1)
                dve.tensor_scalar(cnt_i[:, 1, :], cnt_i[:, 0, :], T.bit_length() - 1, None, ALU.arith_shift_right).then_inc(s_set, 1)
                dve.wait_ge(s_set, L * 5 + 2)
                dve.tensor_copy(tiles[:, :], cnt_i[:, 1, :]).then_inc(s_set, 1)
                dve.wait_ge(s_set, L * 5 + 3)
                dve.tensor_tensor_scan(cumt[:, :], ones[:, 0:E], tiles[:, :], 0.0, ALU.mult, ALU.add).then_inc(s_set, 1)
                dve.tensor_tensor_scan(cumn[:, :], ones[:, 0:E], cnt[:, :], 0.0, ALU.mult, ALU.add).then_inc(s_set, 1)
                dve.wait_ge(s_set, L * 5 + 5)
                then(dve.tensor_tensor(off[:, :], cumt[:, :], tiles[:, :], ALU.subtract))
                then(dve.scalar_tensor_tensor(off[:, :], off[:, :], float(T), cumn[:, :], ALU.mult, ALU.subtract))
                then(dve.tensor_tensor(off[:, :], off[:, :], cnt[:, :], ALU.add))
                then(dve.tensor_tensor_scan(cum[:, :, :].rearrange("p e b -> p (e b)"), ones[:, :],
                                            tot[:, :, :].rearrange("p e b -> p (e b)"), 0.0, ALU.mult, ALU.add))
                then(dve.tensor_tensor(pos[:, :, :], cum[:, :, :], tot[:, :, :], ALU.subtract))
                then(dve.tensor_tensor(pos[:, :, :], pos[:, :, :], by_e(off[:, :]), ALU.add))
                then(dve.tensor_tensor(pos[:, :, :], PV[0][:, 0:256].rearrange("p (b e) -> p e b", e=E), pos[:, :, :], ALU.add))
                then(dve.tensor_tensor(pos[:, :, :], pos[:, :, :], chosen[:, :, :].rearrange("p b e -> p e b"), ALU.mult))
                assert n[0] == R0 + 16
                dve.tensor_reduce(slot_f[:, :], pos[:, :, :].rearrange("p e b -> p b e"), AX, ALU.add).then_inc(s_sl, 1)
                dve.tensor_tensor(past[:, :, :], t_row[:, :, :],
                                  cumt[0:1, :].rearrange("p (o e) -> p o e", o=1).to_broadcast([1, NT, E]), ALU.is_ge).then_inc(s_sl, 1)
                dve.wait_ge(s_sl, L * 4 + 2)
                dve.tensor_copy(slot[:, :], slot_f[:, :]).then_inc(s_sl, 1)
                dve.tensor_reduce(texp_f[:, :], past[:, :, :], AX, ALU.add).then_inc(s_sl, 1)
                dve.wait_ge(s_sl, L * 4 + 4)
                if L == 1:
                    for u in range(2):
                        dve.wait_ge(s_sg[u], len(range(u, NT, 2)))
                dve.tensor_scalar(texp[:, :], texp_f[:, :], float(E - 1), None, ALU.min).then_inc(s_slot, 1)
                dve.wait_ge(s_rx, L + 1)
                dve.tensor_reduce(gsum[:, :], expd[:, :, :], AX, ALU.add).then_inc(s_gt, 1)
                dve.wait_ge(s_gt, L * 3 + 1)
                dve.reciprocal(gate[:, :], gsum[:, :]).then_inc(s_gt, 1)
                dve.wait_ge(s_gt, L * 3 + 2)
                dve.tensor_scalar(gate[:, :], gate[:, :], tg[:, 2 + L:3 + L], None, ALU.mult).then_inc(s_gt, 1)
                dve.wait_ge(s_gt, L * 3 + 3)

            def slot_step(L, i, u, T2, F1, F2):
                if F1:
                    n = L * NT + i + 1
                    dve.wait_ge(s_f1, n + 1)
                    wait(dve, s_fg, n - 1)
                    dve.tensor_tensor(hb[1 - u][:, :, :], SB[1 - u][:, :].rearrange("p (c t) -> p c t", c=FC),
                                      stg[1 - u][:, 2 * F:2 * F + FC].rearrange("p (c o) -> p c o", o=1).to_broadcast([128, FC, T]),
                                      ALU.add).then_inc(s_fb, 1)
                if F2:
                    n = L * NT + i
                    dve.wait_ge(s_f2, n + 1)
                    before = tile_laps(L, i, u)
                    wait(dve, s_ysw[u], before * 16)
                    dve.tensor_tensor(ys[u][:, :], ST[u][:, 0:DM], stg[u][:, 2 * F + FC:EW], ALU.add).then_inc(s_fy, 1)

            dve.wait_ge(s_ri, 2)
            dve.tensor_copy(e_row[:, :, :], e_int[:, :, :]).then_inc(s_rk, 1)
            dve.tensor_copy(t_row[:, :, :], t_int[:, :, :]).then_inc(s_rk, 1)
            dve.wait_ge(s_b1t, 1)
            dve.tensor_copy(b1T[:, :, :], M[1][:, 0:2 * E * FC].rearrange("p (l n) -> p l n", l=2)).then_inc(s_b1s, 1)
            dve.wait_ge(s_rk, 2)

            for L in range(1 if stage == 0 else 2):
                attention(dve, L, step)
                if stage == 0:
                    break
                route(L)
                experts(dve, L, slot_step)
            if stage > 0:
                for g in range(NG):
                    x_update(Group(2, g // 3, g % 3), 2, NG + g, g % 3)

        @block.tensor
        def _(pe):
            pe.wait_ge(s_id, 3)
            for m in range(8):
                if m == 0:
                    pe.wait_ge(s_w, 8 * 16)
                wait(pe, s_wte, m - 1)
                pe.transpose(M[m % 2][:, 0:128], wnat[:, m, :], ident[:, :]).then_inc(s_wtp, 1)
            pe.wait_ge(s_wte, 8)
            pe.wait_ge(s_bp, 1)
            pe.transpose(M[0][:, 0:4], bperm[:, :], ident[0:4, 0:4]).then_inc(s_bT, 1)
            pe.wait_ge(s_wo_s, 5)
            pe.wait_ge(s_cst, 12)
            pe.wait_ge(s_kz, 6)
            pe.wait_ge(s_b1l, 32)
            for L in range(2):
                last = pe.transpose(M[1][:, 32 * L:32 * L + 32], b1n[:, L, :], ident[0:32, 0:32])
            last.then_inc(s_b1t, 1)
            pe.wait_ge(s_b1s, 1)

            def scores(gr_, n):
                m, b, k = gr_.count(NG) * 8 + n, n // 4, n % 4
                if n == 0:
                    pe.wait_ge(s_qr[gr_.ring], (gr_.laps(NG) + 1) * len(RUNS) * 16)
                    pe.wait_ge(s_kr[gr_.ring], k_loads(gr_))
                wait(pe, s_max, m - 1)
                q, kk = Qst[gr_.ring], Kst[gr_.ring]
                for e in range(2):
                    for s in range(2):
                        c0 = (2 * e + s) * 128
                        last = pe.matmul(SB[n % 2][:, c0:c0 + 128], q[0:RS, 2 * k + e, s, b, :], kk[0:RS, 2 * k + e, b, :],
                                         start=True, stop=True)
                last.then_inc(s_s, 1)

            def shifted(gr_, n):
                m, b, k = gr_.count(NG) * 8 + n, n // 4, n % 4
                if k == 0:
                    pe.wait_ge(s_md[b], (gr_.count(NG) + 1) * 32)
                wait(pe, s_exp, m - 1)
                for e in range(2):
                    last = pe.matmul(ST[n % 2][:, 256 * e:256 * e + 256], Kst[gr_.ring][0:RT, 2 * k + e, b, :],
                                     Qst[gr_.ring][0:RT, 2 * k + e, :, b, :], start=True, stop=True)
                last.then_inc(s_st, 1)

            def values(gr_, n):
                m, b, k = gr_.count(NG) * 8 + n, n // 4, n % 4
                pe.wait_ge(s_exp, m + 1)
                if n == 0:
                    pe.wait_ge(s_vm, gr_.count(NG) + 1)
                if k == 0:
                    wait(pe, s_xa, gr_.count(NG) * GB + b - 1)
                for g in range(4):
                    pe.matmul(PV[b][32 * g:32 * g + 32, 0:128], Vm[gr_.ring][:, b, k, 32 * g:32 * g + 32],
                              P[:, n % 2, 128 * g:128 * g + 128], start=(k == 0), stop=(k == 3), skip_group_check=True)
                for g in range(4):
                    last = pe.matmul(PV[b][32 * g:32 * g + 32, 128:256], ones_m[:, k, :],
                                     P[:, n % 2, 128 * g:128 * g + 128], start=False, stop=(k == 3), skip_group_check=True)
                last.then_inc(s_pv, 1)

            def out_proj(gr_, b):
                pe.wait_ge(s_nrm, gr_.count(NG) * GB + b + 1)
                pe.matmul(PV[b][:, 256:384], cT[:, b, :], wT[:, 4 * gr_.layer + 3, :], start=True, stop=True).then_inc(s_wo, 1)

            def max_rows(gr_, b):
                alone(pe, s_ns, gr_.count(NG) * GB + b + 1)
                pe.transpose(M[b][0:48, 0:64].bitcast(bf16), negp[:, b, :, :, :].rearrange("q s t p -> q (s t p)"),
                             identb[:, :]).then_inc(s_mTp, 1)

            def step(c, A1, A2, B, C, D):
                s, a, d = c.at(1), c.at(2), c.at(-1)
                N = a.count(NG)
                for n in range(8):
                    if C:
                        shifted(c, n)
                    if B:
                        scores(s, n)
                    if n >= 1 and C:
                        values(c, n - 1)
                    if n == 0 and D:
                        values(d, 7)
                    if n == 0 and A2:
                        pe.wait_ge(s_xn, N + 1)
                        wait(pe, s_lga, c.count(NG) - 1)
                        wait(pe, s_mTe, c.count(NG) * GB + 1)
                        for b in range(GB):
                            last = pe.transpose(M[0][:, 128 * b:128 * b + 128], xn[:, b, :], ident[:, :])
                        last.then_inc(s_xT, 1)
                    if n == 1 and C:
                        wait(pe, s_x2Te, c.count(NG) - 1)
                        wait(pe, s_vm, c.count(NG) + 2 if A2 else NG * (c.layer + 1))
                        max_rows(c, 1)
                    if n == 1 and A2:
                        pe.wait_ge(s_xTe, N + 1)
                        pe.matmul(M[0][:, 0:W], wT[:, 4 * a.layer, :], xT[:, :], start=True, stop=True).then_inc(s_q, 1)
                    if n == 2:
                        if D:
                            out_proj(d, 1)
                        if A2:
                            pe.wait_ge(s_c[a.ring], (a.laps(NG) + 1) * 16)
                            wait(pe, s_vm, N)
                            wait(pe, s_mTe, c.count(NG) * GB + 2)
                            for b in range(GB):
                                last = pe.transpose(M[1][:, 128 * b:128 * b + 128], cg[a.ring][:, b, :], ident[:, :])
                            last.then_inc(s_cTp, 1)
                    if n == 3 and A2:
                        pe.wait_ge(s_cTe, N + 1)
                        pe.wait_ge(s_qf, N + 1)
                        pe.matmul(M[0][:, 0:W], wT[:, 4 * a.layer + 1, :], cgT[:, :], start=True, stop=True).then_inc(s_k, 1)
                    if n == 4 and A2:
                        wait(pe, s_mTe, c.count(NG) * GB + 2)
                        for b in range(GB):
                            last = pe.matmul(M[1][:, 128 * b:128 * b + 128], cgT[:, 128 * b:128 * b + 128], wT[:, 4 * a.layer + 2, :],
                                             start=True, stop=True)
                        last.then_inc(s_v, 1)
                    if n == 5 and B:
                        if A2:
                            pe.wait_ge(s_kf, N + 1)
                        else:
                            wait(pe, s_lga, c.count(NG) - 1)
                        max_rows(s, 0)
                    if n == 6:
                        if C:
                            out_proj(c, 0)
                        if D:
                            pe.wait_ge(s_xn2, d.count(NG) + 1)
                            if A2:
                                pe.wait_ge(s_vm, N + 1)
                            elif C:
                                pe.wait_ge(s_mTe, c.count(NG) * GB + 2)
                            for b in range(GB):
                                last = pe.transpose(M[1][:, 128 * b:128 * b + 128], xn2g[:, b, :], ident[:, :])
                            last.then_inc(s_x2T, 1)
                    if n == 7 and D:
                        pe.wait_ge(s_x2Te, d.count(NG) + 1)
                        if B:
                            pe.wait_ge(s_mTe, s.count(NG) * GB + 1)
                        for b in range(GB):
                            last = pe.matmul(M[0][:, E * b:E * b + E], x2T[:, 128 * b:128 * b + 128], gw[:, d.layer, :],
                                             start=True, stop=True)
                        last.then_inc(s_lg, 1)

            def slot_step(L, i, u, T2, F1, F2):
                if T2:
                    n, t = L * NT + i + 2, i + 2
                    pe.wait_ge(s_xl[u], (tile_laps(L, t, u) + 1) * 16)
                    wait(pe, s_fte, n - 1)
                    pe.transpose(M[u][:, 0:T], xs[u][:, :], ident[:, :]).then_inc(s_ft, 1)
                if F1:
                    n, t = L * NT + i + 1, i + 1
                    pe.wait_ge(s_fte, n + 1)
                    pe.wait_ge(s_sg[1 - u], tile_laps(L, t, 1 - u) + 1)
                    wait(pe, s_fb, n - 1)
                    for c in range(FC):
                        last = pe.matmul(SB[1 - u][:, c * T:(c + 1) * T], stg[1 - u][:, c * 128:(c + 1) * 128], xsT[1 - u][:, :],
                                         start=True, stop=True)
                    last.then_inc(s_f1, 1)
                if F2:
                    n = L * NT + i
                    pe.wait_ge(s_fg, n + 1)
                    wait(pe, s_fy, n - 1)
                    for c in range(FC):
                        last = pe.matmul(ST[u][:, 0:DM], hT[u][:, c, :], stg[u][:, F + c * DM:F + (c + 1) * DM],
                                         start=(c == 0), stop=(c == FC - 1))
                    last.then_inc(s_f2, 1)

            for L in range(1 if stage == 0 else 2):
                attention(pe, L, step)
                if stage == 0:
                    break
                pe.wait_ge(s_rt, L * 16 + 6)
                pe.wait_ge(s_ri, 5)
                pe.wait_ge(s_xa, NB * (L + 1))
                pe.matmul(PV[0][:, 0:256], tri[:, :], chosen[:, :, :].rearrange("p b e -> p (b e)"), start=True, stop=True)
                pe.matmul(PV[0][:, 256:512], ones[:, 0:128], chosen[:, :, :].rearrange("p b e -> p (b e)"),
                          start=True, stop=True).then_inc(s_rc, 1)
                pe.wait_ge(s_lga, NG * (L + 1))
                pe.wait_ge(s_x2Te, NG * (L + 1))
                experts(pe, L, slot_step)
                if L == 0:
                    pe.wait_ge(s_fy, NT)
                    pe.wait_ge(s_slot, 1)


_INS = ["x", "ctx_1024", "mask_BxS2_bf1", "g_xattn", "g_ffn",
        "L0_xattn_wq", "L0_xattn_bq", "L0_xattn_wk", "L0_xattn_bk", "L0_xattn_wv", "L0_xattn_bv", "L0_xattn_wo",
        "L0_xattn_bo", "L0_ffn_gate_w", "L0_ffn_gate_b", "L0_ffn_w1", "L0_ffn_b1", "L0_ffn_w2", "L0_ffn_b2",
        "L1_xattn_Wq", "L1_xattn_bq", "L1_xattn_Wk", "L1_xattn_bk", "L1_xattn_Wv", "L1_xattn_bv", "L1_xattn_Wo",
        "L1_xattn_bo", "L1_ffn_W1", "L1_ffn_b1", "L1_ffn_W2", "L1_ffn_b2", "L1_ffn_Wr", "L1_ffn_br"]


def kernel(**inputs):
    import numpy as _np
    import concourse.bacc as _bacc
    from concourse import mybir as _mybir
    from concourse.bass_utils import run_bass_kernel_spmd as _run

    nc = _bacc.Bacc("TRN2", target_bir_lowering=False, num_devices=1)
    arrays, args = {}, []
    for name in _INS:
        a = _np.ascontiguousarray(inputs[name])
        if a.dtype == _np.bool_:
            a = a.view(_np.uint8)
        arrays[f"in_{name}_dram"] = a
        args.append(nc.dram_tensor(f"in_{name}_dram", a.shape, _mybir.dt.from_np(a.dtype), kind="ExternalInput").ap())
    out = nc.dram_tensor("out_0_dram", inputs["x"].shape, _mybir.dt.float32, kind="ExternalOutput").ap()
    flamingo_kernel(nc, *args, out)
    r = _run(nc, [arrays], core_ids=[0])
    return r.results[0]["out_0_dram"]
```

```python
import numpy as np
from contextlib import ExitStack

import concourse.bass as bass
from concourse import mybir
from concourse.alu_op_type import AluOpType as ALU


class Tile:

    def __init__(self, layer, lap, v):
        self.layer, self.lap, self.v = layer, lap, v

    def at(self, k):
        v = self.v + k
        return Tile(self.layer, self.lap + v // 4, v % 4)

    @property
    def i(self):
        return self.lap * 4 + self.v

    @property
    def u(self):
        return self.v % 2

    def count(self, n_tiles):
        return self.lap * 4 + (self.v + n_tiles * self.layer)

    def laps2(self, n_tiles):
        return self.lap * 2 + (self.v // 2 + self.layer * len(range(self.u, n_tiles, 2)))

    def laps4(self, n_tiles):
        return self.lap + self.layer * len(range(self.v, n_tiles, 4))


class Group:

    def __init__(self, layer, turn, ring):
        self.layer, self.turn, self.ring = layer, turn, ring

    def at(self, k):
        r = self.ring + k
        return Group(self.layer, self.turn + r // 3, r % 3)

    @property
    def g(self):
        return self.turn * 3 + self.ring

    def count(self, n_groups):
        return self.turn * 3 + (self.ring + n_groups * self.layer)

    def laps(self, n_groups):
        return self.turn + self.layer * len(range(self.ring, n_groups, 3))


def wait(eng, sem, value):
    if isinstance(value, int) and value <= 0:
        return
    eng.wait_ge(sem, value)


def alone(eng, sem, value):
    wait(eng, sem, value)
    if not isinstance(value, int):
        eng.nop(nofuse=True)


def flamingo_kernel(nc, x, ctx_1024, mask_BxS2_bf1, g_xattn, g_ffn,
                    L0_xattn_wq, L0_xattn_bq, L0_xattn_wk, L0_xattn_bk, L0_xattn_wv, L0_xattn_bv, L0_xattn_wo,
                    L0_xattn_bo, L0_ffn_gate_w, L0_ffn_gate_b, L0_ffn_w1, L0_ffn_b1, L0_ffn_w2, L0_ffn_b2,
                    L1_xattn_Wq, L1_xattn_bq, L1_xattn_Wk, L1_xattn_bk, L1_xattn_Wv, L1_xattn_bv, L1_xattn_Wo,
                    L1_xattn_bo, L1_ffn_W1, L1_ffn_b1, L1_ffn_W2, L1_ffn_b2, L1_ffn_Wr, L1_ffn_br, out,
                    stage=99):
    f32, bf16, u8 = mybir.dt.float32, mybir.dt.bfloat16, mybir.dt.uint8
    i32, u32 = mybir.dt.int32, mybir.dt.uint32
    ACT = mybir.ActivationFunctionType
    AX = mybir.AxisListType.X

    NB, S, DM = x.shape
    H, DK = 16, 8
    GB = 2
    NG = NB // GB
    W = GB * S
    NP = H // 2
    PRODUCTS = [(0, 0), (0, 1), (0, 2), (1, 0), (1, 1), (2, 0)]
    NPR = len(PRODUCTS)
    RUNS = [(0, 3), (3, 2), (5, 1)]
    RP = 2 * NPR * DK
    RS = RP + 3
    RT = RS + 6
    E, F = L0_ffn_w1.shape[0], L0_ffn_w1.shape[2]
    FC = F // 128
    T = 128
    NT = NB * S // T + E - 1
    EPS = 1e-5
    SCALE = float(np.float32(1.0) / np.sqrt(np.float32(DK)))
    FILL = 1e8

    wqkvo = [(L0_xattn_wq, L0_xattn_wk, L0_xattn_wv, L0_xattn_wo), (L1_xattn_Wq, L1_xattn_Wk, L1_xattn_Wv, L1_xattn_Wo)]
    bqkvo = [(L0_xattn_bq, L0_xattn_bk, L0_xattn_bv, L0_xattn_bo), (L1_xattn_bq, L1_xattn_bk, L1_xattn_bv, L1_xattn_bo)]
    gates = [(L0_ffn_gate_w, L0_ffn_gate_b), (L1_ffn_Wr, L1_ffn_br)]

    stack = ExitStack()
    with stack:
        def sb(name, shape, dt=f32):
            return stack.enter_context(nc.sbuf_tensor(name, shape, dt))

        def sem(name):
            return stack.enter_context(nc.semaphore(name))

        def row(ap):
            return ap.rearrange("(a n) -> a n", a=1)

        x_sb = sb("x_sb", [128, NB, DM])
        xn2 = sb("xn2", [128, NB, DM])
        wnat = xn2[:, 0:8, :]
        wT = sb("wT", [128, 8, DM])
        bnat = sb("bnat", [4, DM])
        bperm = sb("bperm", [4, DM])
        bcol = sb("bcol", [128, 4])
        bvr = sb("bvr", [128, 2, DM])
        bor = sb("bor", [128, 2, DM])
        gr = sb("gr", [128, 4])
        tg = sb("tg", [128, 4])
        gw = sb("gw", [128, 2, E])
        gb = sb("gb", [128, 2, E])
        ident = sb("ident", [128, 128])
        identb = sb("identb", [128, 128], bf16)
        half = sb("half", [128, 2])
        ones_m = sb("ones_m", [128, 4, 32])
        maskrep = sb("maskrep", [128, NB * S], u8)
        mask8 = sb("mask8", [NB, S], u8)
        mval = sb("mval", [NB, S])
        mparts = sb("mparts", [NB, 3, S], bf16)
        mres = sb("mres", [NB, S])

        B1, B2, W2 = F, F + FC, F + FC + DM
        EW = W2 + FC * DM
        ex = sb("ex", [128, E, EW])
        b1T = sb("b1T", [128, 2, E * FC])
        b1n = sb("b1n", [E * FC, 2, 128])
        tri = sb("tri", [128, 128])
        ones = sb("ones", [128, 256])
        e_row = sb("e_row", [128, NB, E])
        t_row = sb("t_row", [1, NT, E])
        e_int, t_int = sb("e_int", [128, NB, E], i32), sb("t_int", [1, NT, E], i32)
        top, gsum, gate = sb("top", [128, NB]), sb("gsum", [128, NB]), sb("gate", [128, NB])
        below, expd = sb("below", [128, NB, E]), sb("expd", [128, NB, E])
        notop, first, chosen = sb("notop", [128, NB, E]), sb("first", [128, NB]), sb("chosen", [128, NB, E])
        tot, cum, pos = sb("tot", [128, E, NB]), sb("cum", [128, E, NB]), sb("pos", [128, E, NB])
        cnt, cumn, tiles, cumt, off = (sb(n, [128, E]) for n in ("cnt", "cumn", "tiles", "cumt", "off"))
        cnt_i = sb("cnt_i", [128, 2, E], i32)
        slot_f, slot = sb("slot_f", [128, NB]), sb("slot", [128, NB], u32)
        past, texp_f, texp = sb("past", [1, NT, E]), sb("texp_f", [1, NT]), sb("texp", [1, NT], i32)
        XR = 4
        stg = [sb(f"stg{v}", [128, W2]) for v in range(XR)]
        xs = [sb(f"xs{v}", [128, DM]) for v in range(XR)]
        xsT = [sb(f"xsT{u}", [128, T]) for u in range(2)]
        hb = [sb(f"hb{u}", [128, FC, T]) for u in range(2)]
        hT = [sb(f"hT{u}", [128, FC, T]) for u in range(2)]
        ys = [sb(f"ys{u}", [128, DM]) for u in range(2)]
        yg = [sb(f"yg{j}", [128, GB, DM]) for j in range(3)]
        ixg = [sb(f"ixg{j}", [128, GB], u32) for j in range(3)]

        Qst = [sb(f"Qst{j}", [128, NP, 2, GB, S], bf16) for j in range(3)]
        Kst = [sb(f"Kst{j}", [128, NP, GB, S], bf16) for j in range(3)]
        Vm = [sb(f"Vm{j}", [128, GB, 4, 128]) for j in range(3)]
        cg = [sb(f"cg{j}", [128, GB, DM]) for j in range(3)]
        cgT = [sb(f"cgT{j}", [128, W]) for j in range(3)]
        xn = sb("xn", [128, GB, DM])
        xn2g = sb("xn2g", [128, GB, DM])
        xT = sb("xT", [128, W])
        Qf, Kf = sb("Qf", [128, W]), sb("Kf", [128, W])
        qres, kres = sb("qres", [128, W]), sb("kres", [128, W])
        qp, kp = sb("qp", [128, 3, W], bf16), sb("kp", [128, 3, W], bf16)
        P = sb("P", [128, 4, 512])
        negm = sb("negm", [128, GB, 2, NP])
        nres = sb("nres", [128, GB, 2, NP])
        negp = sb("negp", [128, GB, 2, 3, NP], bf16)
        mT = sb("mT", [48, GB, 128], bf16)
        R = sb("R", [128, GB, 128])
        cT = sb("cT", [128, GB, 128])
        st1, st2 = sb("st1", [128, GB, 6]), sb("st2", [128, GB, 6])
        mv1, mv2 = sb("mv1", [128, GB, 2]), sb("mv2", [128, GB, 2])
        ve1, ve2 = sb("ve1", [128, GB]), sb("ve2", [128, GB])
        rs1, rs2 = sb("rs1", [128, GB]), sb("rs2", [128, GB])
        x2T = sb("x2T", [128, W])
        logits = sb("logits", [128, NB, E])

        SB = [stack.enter_context(nc.psum_tensor(f"SB{i}", [128, 512], f32)) for i in range(2)]
        ST = [stack.enter_context(nc.psum_tensor(f"ST{i}", [128, 512], f32)) for i in range(2)]
        PV = [stack.enter_context(nc.psum_tensor(f"PV{i}", [128, 512], f32)) for i in range(2)]
        M = [stack.enter_context(nc.psum_tensor(f"M{i}", [128, 512], f32)) for i in range(2)]

        q_dram = nc.dram_tensor("q_parts", [3, 3, 2 * DK, NP * 2 * W], bf16, kind="Internal").ap()
        k_dram = nc.dram_tensor("k_parts", [3, 3, 2 * DK, NP * W], bf16, kind="Internal").ap()
        m_dram = nc.dram_tensor("mask_parts", [3, NB * S], bf16, kind="Internal").ap()

        xs_dram = nc.dram_tensor("tokens_by_expert", [NT * T, DM], f32, kind="Internal").ap()
        ys_dram = nc.dram_tensor("expert_outputs", [NT * T, DM], f32, kind="Internal").ap()

        s_ex, s_b1l, s_b1t, s_b1s, s_xz = (sem(n) for n in (
            "experts_loaded", "b1_loaded", "b1_transposed", "b1_stored", "tokens_zeroed"))
        s_ri, s_rt = sem("route_constants"), sem("route_steps")
        s_rx, s_rc, s_slot = sem("route_exp"), sem("route_counts"), sem("slots_ready")
        s_sc = sem("tokens_scattered")
        s_sg = sem("stage_filled")
        s_xl = [sem(f"tile_loaded{v}") for v in range(XR)]
        s_ysw = [sem(f"tile_written{u}") for u in range(2)]
        s_ft, s_fte, s_f1, s_fb, s_fg, s_f2, s_fy = (sem(n) for n in (
            "tile_transposed", "tileT_stored", "hidden_done", "hidden_biased", "hidden_gelu", "expert_done", "expert_stored"))
        s_ix, s_yg, s_xu = sem("index_copied"), [sem(f"rows_gathered{j}") for j in range(3)], sem("x_updated")
        s_w, s_x, s_b, s_mk = sem("w_loaded"), sem("x_loaded"), sem("small_loaded"), sem("mask_loaded")
        s_c = [sem(f"ctx_loaded{j}") for j in range(3)]
        s_bk = sem("bias_columns_loaded")
        s_id, s_cst, s_set = sem("ident_steps"), sem("constants_ready"), sem("setup_steps")
        s_tg, s_wtp, s_wte, s_wo_s = sem("tanh_ready"), sem("w_transposed"), sem("w_stored"), sem("out_w_scaled")
        s_mst, s_mpw = sem("mask_steps"), sem("mask_parts_written")
        s_st1, s_pw1, s_xn = sem("norm1_stats"), sem("norm1_rstd"), sem("xn_ready")
        s_v1, s_v2, s_ag1, s_ag2 = sem("norm1_eps"), sem("norm2_eps"), sem("norm1_bn"), sem("norm2_bn")
        s_xT, s_xTe = sem("xT_done"), sem("xT_stored")
        s_cTp, s_cTe = sem("ctxT_done"), sem("ctxT_stored")
        s_q, s_qf, s_k, s_kf, s_v, s_vm = (sem(n) for n in ("q_done", "q_stored", "k_done", "k_stored", "v_done", "v_stored"))
        s_qs, s_ks = sem("q_split"), sem("k_split")
        s_qi, s_ki, s_ni = sem("q_split_steps"), sem("k_split_steps"), sem("max_split_steps")
        s_sl, s_gt, s_rk = sem("slot_steps"), sem("gate_steps"), sem("route_rows")
        s_qt, s_kt = sem("q_rest"), sem("k_rest")
        s_qw, s_kw = [sem(f"q_parts_in_dram{j}") for j in range(3)], [sem(f"k_parts_in_dram{j}") for j in range(3)]
        s_qr, s_kr = [sem(f"q_stack_loaded{j}") for j in range(3)], [sem(f"k_stack_loaded{j}") for j in range(3)]
        s_s, s_max = sem("scores_done"), sem("max_done")
        s_ns, s_mTp, s_mTe = sem("max_split"), sem("max_transposed"), sem("max_stored")
        s_md = [sem(f"max_rows_loaded{b}") for b in range(GB)]
        s_st, s_exp, s_pv = sem("shifted_scores_done"), sem("exp_done"), sem("pv_done")
        s_rec, s_nrm, s_wo, s_xa = sem("recip_done"), sem("ctx_normed"), sem("out_proj_done"), sem("x_added")
        s_xb = sem("out_bias_added")
        s_st2, s_pw2, s_xn2 = sem("norm2_stats"), sem("norm2_rstd"), sem("xn2_ready")
        s_q0, s_dz, s_bT, s_bp, s_bc = (sem(n) for n in ("q_rows_zero", "dram_zeroed", "bias_transposed", "bias_permuted", "bias_columns"))
        s_qz, s_kz = sem("q_stacks_zero"), sem("k_stacks_set")
        s_x2k = sem("xn2_kept")
        s_x2T, s_x2Te, s_lg, s_lga = sem("xn2T_done"), sem("xn2T_stored"), sem("logits_done"), sem("logits_stored")
        s_out = sem("out_written")

        NXZ = -(-NT * T // 1024)
        expert_ins = [(L0_ffn_w1, L0_ffn_b1, L0_ffn_w2, L0_ffn_b2), (L1_ffn_W1, L1_ffn_b1, L1_ffn_W2, L1_ffn_b2)]
        NXD = 8

        def span(gr_):
            return bass.ds(gr_.g * GB, GB) if not isinstance(gr_.g, int) else slice(gr_.g * GB, gr_.g * GB + GB)

        def one(index):
            return bass.ds(index, 1) if not isinstance(index, int) else slice(index, index + 1)

        def cols(gr_):
            return bass.ds(gr_.g * W, W) if not isinstance(gr_.g, int) else slice(gr_.g * W, gr_.g * W + W)

        def turns(layer, step):
            def parts(g):
                return {"A0": -5 <= g <= NG - 6, "A1": -4 <= g <= NG - 5, "A2": -3 <= g <= NG - 4, 
                        "A3": -2 <= g <= NG - 3, "B": -1 <= g <= NG - 2, "C": 0 <= g <= NG - 1, "D": 1 <= g <= NG, "D2": 2 <= g <= NG + 1}
            first, rounds = 2, (NG - 5) // 3
            for g in range(-5, first):
                step(Group(layer, g // 3, g % 3), **parts(g))
            yield rounds, lambda i: [step(Group(layer, i + (first + u) // 3, (first + u) % 3), **parts(first))
                                     for u in range(3)]
            for g in range(first + 3 * rounds, NG + 2):
                step(Group(layer, g // 3, g % 3), **parts(g))

        def rows(t):
            return slice(t.i * T, t.i * T + T) if isinstance(t.i, int) else bass.ds(t.i * T, T)

        def experts(eng, L, step):
            for i in range(-2, 2):
                step(Tile(L, i // 4, i % 4), T2=True, F1=i >= -1, F2=i >= 0)
            rounds = (NT - 4) // 4
            with eng.Fori(0, rounds) as h:
                for u in range(2, 6):
                    step(Tile(L, h + u // 4, u % 4), T2=True, F1=True, F2=True)
            for i in range(2 + 4 * rounds, NT):
                step(Tile(L, i // 4, i % 4), T2=i + 2 < NT, F1=i + 1 < NT, F2=True)

        def attention(eng, layer, step):
            for n, body in turns(layer, step):
                with eng.Fori(0, n) as i:
                    body(i)

        block = stack.enter_context(nc.Block())

        @block.sync
        def _(sp):
            for L in range(2):
                for n in range(4):
                    sp.dma_start(wnat[:, 4 * L + n, :], wqkvo[L][n]).then_inc(s_w, 16)
            for n in range(NXD):
                k = NB // NXD
                sp.dma_start(x_sb[:, n * k:(n + 1) * k, :], x[n * k:(n + 1) * k].rearrange("b s d -> s b d")).then_inc(s_x, 16)
            sp.dma_start(maskrep[:, :], mask_BxS2_bf1.rearrange("b s -> (b s)").partition_broadcast(128)).then_inc(s_mk, 16)
            sp.dma_start(mask8[:, :], mask_BxS2_bf1).then_inc(s_mk, 16)
            def expert_loads(L):
                w1, b1, w2, b2 = expert_ins[L]
                sp.dma_start(ex[:, :, 0:F], w1.rearrange("e p n -> p e n")).then_inc(s_ex, 16)
                for c in range(FC):
                    sp.dma_start(ex[:, :, W2 + c * DM:W2 + (c + 1) * DM],
                                 w2[:, c * 128:(c + 1) * 128, :].rearrange("e p n -> p e n")).then_inc(s_ex, 16)
                sp.dma_start(ex[:, :, B2:W2], b2.partition_broadcast(128)).then_inc(s_ex, 16)

            for L in range(2):
                sp.dma_start(b1n[:, L, :], expert_ins[L][1].rearrange("e (c p) -> (e c) p", p=128)).then_inc(s_b1l, 16)
            expert_loads(0)
            sp.wait_ge(s_qz, 1)
            for n in range(0, NT * T, 1024):
                k = min(1024, NT * T - n) // 64
                sp.dma_start(xs_dram[n:n + k * 64].rearrange("(k p) d -> p k d", p=64),
                             Qst[0][0:64, :, :, :, :].rearrange("r p s b q -> r (p s b q)")[:, 0:2 * k * DM].bitcast(f32)
                             .rearrange("p (k d) -> p k d", k=k)).then_inc(s_xz, 16)
            sp.wait_ge(s_qz, 1)
            for j in range(3):
                sp.dma_start(q_dram[j].rearrange("t r n -> (t r) n"), Qst[0][0:6 * DK].rearrange("r p s b q -> r (p s b q)")
                             ).then_inc(s_dz, 16)
            sp.wait_ge(s_mst, 5)
            sp.dma_start(m_dram.rearrange("r (b k) -> b r k", b=NB), mparts[:, :, :]).then_inc(s_mpw, 16)

            def max_rows(gr_, b):
                alone(sp, s_mTe, gr_.count(NG) * GB + b + 1)
                for s in range(2):
                    sp.dma_start(Qst[gr_.ring][RS + 3 * s:RS + 3 * s + 3, :, s, b, :],
                                 mT[24 * s:24 * s + 24, b, :]).then_inc(s_md[b], 16)

            def step(c, A0, A1, A2, A3, B, C, D, D2):
                s1, l, a, a1 = c.at(1), c.at(2), c.at(3), c.at(4)
                if C:
                    max_rows(c, 1)
                if A3:
                    j, N = l.ring, l.count(NG)
                    alone(sp, s_st, (N - 3) * 8 + 8)
                    alone(sp, s_qw[j], (l.laps(NG) + 1) * 32)
                    for n, runs in RUNS:
                        t = PRODUCTS[n][0]
                        sp.dma_start(Qst[j][2 * DK * n:2 * DK * (n + runs)].rearrange("r p s b q -> r (p s b q)"),
                                     q_dram[j, t:t + 1].to_broadcast([runs, 2 * DK, NP * 2 * W])).then_inc(s_qr[j], 16)
                    alone(sp, s_kw[j], (l.laps(NG) + 1) * 16)
                    for n, runs in RUNS:
                        t = PRODUCTS[n][1]
                        sp.dma_start(Kst[j][2 * DK * n:2 * DK * (n + runs)].rearrange("r p b k -> r (p b k)"),
                                     k_dram[j, t:t + runs].rearrange("t r n -> (t r) n")).then_inc(s_kr[j], 16)
                    if l.layer == 1:
                        src = m_dram[:, cols(l)].rearrange("r (o n) -> r o n", o=1).to_broadcast([3, NP, W])
                        sp.dma_start(Kst[j][RP:RS].rearrange("r p b k -> r p (b k)"), src).then_inc(s_kr[j], 16)
                if A1:
                    alone(sp, s_cTp, a1.count(NG) - 2)
                    sp.dma_start(cg[a1.ring][:, :, :], ctx_1024[span(a1)].rearrange("b s d -> s b d")).then_inc(s_c[a1.ring], 16)
                if A2:
                    j, N = a.ring, a.count(NG)
                    if isinstance(a.g, int) and a.g == 0:
                        sp.wait_ge(s_cst, 12)
                        sp.wait_ge(s_kz, 6)
                        sp.wait_ge(s_mpw, 16)
                        sp.wait_ge(s_dz, 48)
                        sp.wait_ge(s_xz, NXZ * 16)
                    alone(sp, s_s, (N - 3) * 8 + 8)
                    alone(sp, s_qs, N + 1)
                    for s in range(2):
                        sp.dma_start(q_dram[j][:, s * DK:(s + 1) * DK, :].rearrange("t d (p s n) -> s (d p) t n", p=NP, s=2)[s],
                                     qp[64 * s:64 * s + 64, :, :]).then_inc(s_qw[j], 16)
                if B:
                    max_rows(s1, 0)
                if A2:
                    alone(sp, s_ks, N + 1)
                    sp.dma_start(k_dram[j].rearrange("t r (p n) -> (r p) t n", p=NP), kp[:, :, :]).then_inc(s_kw[j], 16)

            def tile_load(t):
                alone(sp, s_ft, t.count(NT) - 3)
                sp.dma_start(xs[t.v][:, :], xs_dram[rows(t), :]).then_inc(s_xl[t.v], 16)

            def slot_step(t, T2, F1, F2):
                if isinstance(t.i, int) and t.i == -2:
                    for k in range(2, 4):
                        tile_load(t.at(k))
                if not isinstance(t.i, int) or t.i + 4 < NT:
                    tile_load(t.at(4))
                if F2:
                    alone(sp, s_fy, t.count(NT) + 1)
                    sp.dma_start(ys_dram[rows(t), :], ys[t.u][:, :]).then_inc(s_ysw[t.u], 16)

            for L in range(1 if stage == 0 else 2):
                attention(sp, L, step)
                if stage == 0:
                    break
                sp.wait_ge(s_sc, (L + 1) * NB * 16)
                experts(sp, L, slot_step)
                if L == 0:
                    sp.wait_ge(s_sg, NT)
                    sp.wait_ge(s_f2, NT)
                    expert_loads(1)
            if stage > 0:
                for g in range(NG):
                    sp.wait_ge(s_xu, (NG + g + 1) * GB)
                    sp.dma_start(out[g * GB:g * GB + GB].rearrange("b s d -> s b d"),
                                 x_sb[:, g * GB:g * GB + GB, :]).then_inc(s_out, 16)
                sp.wait_ge(s_out, NG * 16)
            if stage == 0:
                sp.wait_ge(s_xa, NB)
                sp.wait_ge(s_lga, NG)
                sp.dma_start(out.rearrange("b s d -> s b d"), x_sb[:, :, :]).then_inc(s_out, 16)
                sp.wait_ge(s_out, 16)

        def k_loads(gr_):
            plain, masked = len(RUNS) * 16, (len(RUNS) + 1) * 16
            if gr_.layer == 0:
                return (gr_.turn + 1) * plain
            return len(range(gr_.ring, NG, 3)) * plain + (gr_.turn + 1) * masked

        @block.gpsimd
        def _(pool):
            pool.memset(ident[:, :], 0.0).then_inc(s_id, 1)
            pool.memset(ones_m[:, :, :], 0.0).then_inc(s_id, 1)
            pool.memset(half[:, :], -0.5).then_inc(s_cst, 1)
            pool.wait_ge(s_id, 2)
            pool.affine_select(out=ident[:, :], in_=ident[:, :], compare_op=ALU.not_equal, fill=1.0, base=0,
                               pattern=[[-1, 128]], channel_multiplier=1).then_inc(s_id, 1)
            for j in range(3):
                if j == 0:
                    pool.memset(Qst[j][:, :, :, :, :], 0.0).then_inc(s_qz, 1)
                pool.memset(Vm[j][:, :, :, :], 0.0).then_inc(s_cst, 1)
            for k in range(4):
                pool.memset(ones_m[:, k, 8 * k:8 * k + 8], 1.0).then_inc(s_cst, 1)
            pool.wait_ge(s_id, 3)
            pool.tensor_copy(identb[:, :], ident[:, :]).then_inc(s_cst, 1)

            def split(src, res, parts, steps, base, done):
                pool.tensor_copy(parts(0), src).then_inc(steps, 1)
                pool.wait_ge(steps, base + 1)
                pool.tensor_tensor(res, src, parts(0), ALU.subtract).then_inc(steps, 1)
                alone(pool, steps, base + 2)
                pool.tensor_copy(parts(1), res).then_inc(steps, 1)
                pool.wait_ge(steps, base + 3)
                pool.tensor_tensor(parts(2), res, parts(1), ALU.subtract).then_inc(done, 1)

            def rests(src, res, parts, rounded, rest, done, N):
                pool.wait_ge(rounded, 2 * N + 1)
                pool.tensor_tensor(res, src, parts[:, 0, :], ALU.subtract).then_inc(rest, 1)
                pool.wait_ge(rounded, 2 * N + 2)
                pool.tensor_tensor(parts[:, 2, :], res, parts[:, 1, :], ALU.subtract).then_inc(done, 1)

            def max_split(gr_, b):
                n = gr_.count(NG) * GB + b
                pool.wait_ge(s_max, gr_.count(NG) * 8 + 4 * b + 4)
                alone(pool, s_mTp, n - 1)
                split(negm[:, b, :, :], nres[:, b, :, :], lambda t: negp[:, b, :, t, :], s_ni, n * 3, s_ns)

            def rstd(stats, mv, ve, rs, s_stat, s_v, s_pw, N):
                alone(pool, s_stat, N + 1)
                pool.tensor_scalar_add(ve[:, :], mv[:, :, 1], EPS).then_inc(s_v, 1)
                pool.wait_ge(s_v, N + 1)
                pool.tensor_tensor(rs[:, :], ve[:, :], half[:, :], ALU.pow).then_inc(s_pw, 1)

            def gather(gr_, indices, N):
                j = gr_.ring
                pool.tensor_copy(ixg[j][:, :], indices).then_inc(s_ix, 1)
                alone(pool, s_ix, N + 1)
                for b in range(GB):
                    pool.indirect_dma_start(
                        out=yg[j][:, b, :], out_offset=None, in_=ys_dram[:, :],
                        in_offset=bass.IndirectOffsetOnAxis(ap=ixg[j][:, b:b + 1], axis=0)).then_inc(s_yg[j], 16)

            def step(c, A0, A1, A2, A3, B, C, D, D2):
                s, l, a, d, e, a1, a0 = c.at(1), c.at(2), c.at(3), c.at(-1), c.at(-2), c.at(4), c.at(5)
                if C:
                    max_split(c, 1)
                if D2:
                    pool.wait_ge(s_xn2, e.count(NG) + 1)
                    pool.tensor_copy(xn2[:, span(e), :], xn2g[:, :, :]).then_inc(s_x2k, 1)
                if A3:
                    pool.wait_ge(s_xn, l.count(NG) + 1)
                    pool.tensor_tensor(x_sb[:, span(l), :], x_sb[:, span(l), :],
                                       bor[:, l.layer:l.layer + 1, :].to_broadcast([128, GB, DM]), ALU.add).then_inc(s_xb, 1)
                if A1:
                    rstd(st1, mv1, ve1, rs1, s_ag1, s_v1, s_pw1, a1.count(NG))
                if A2:
                    N = a.count(NG)
                    rests(Qf[:, :], qres[:, :], qp, s_qi, s_qt, s_qs, N)
                if B:
                    max_split(s, 0)
                if D:
                    rstd(st2, mv2, ve2, rs2, s_ag2, s_v2, s_pw2, d.count(NG))
                if A2:
                    rests(Kf[:, :], kres[:, :], kp, s_ki, s_kt, s_ks, N)
                if A0 and a0.layer == 1:
                    gather(a0, slot[:, span(a0)], a0.g)

            pool.iota(e_int[:, :, :], pattern=[[0, NB], [1, E]], base=0, channel_multiplier=0).then_inc(s_ri, 1)
            pool.iota(t_int[:, :, :], pattern=[[1, NT], [0, E]], base=0, channel_multiplier=0).then_inc(s_ri, 1)
            pool.memset(tri[:, :], 1.0).then_inc(s_ri, 1)
            pool.wait_ge(s_ri, 3)
            pool.affine_select(out=tri[:, :], in_=tri[:, :], compare_op=ALU.is_gt, fill=0.0, base=0,
                               pattern=[[1, 128]], channel_multiplier=-1).then_inc(s_ri, 1)
            pool.memset(ones[:, :], 1.0).then_inc(s_ri, 1)

            pool.wait_ge(s_wo_s, 5)
            for L in range(1 if stage == 0 else 2):
                if L == 1:
                    for u in range(2):
                        pool.wait_ge(s_ysw[u], len(range(u, NT, 2)) * 16)
                attention(pool, L, step)
                if stage == 0:
                    break
                pool.wait_ge(s_slot, L + 1)
                if L == 0:
                    pool.wait_ge(s_xz, NXZ * 16)
                else:
                    for v in range(XR):
                        pool.wait_ge(s_xl[v], len(range(v, NT, XR)) * 16)
                for b in range(NB):
                    if b == 0:
                        pool.wait_ge(s_x2k, NG * (L + 1))
                    pool.indirect_dma_start(
                        out=xs_dram[:, :], out_offset=bass.IndirectOffsetOnAxis(ap=slot[:, b:b + 1], axis=0),
                        in_=xn2[:, b, :], in_offset=None).then_inc(s_sc, 16)
            if stage > 0:
                for u in range(2):
                    pool.wait_ge(s_ysw[u], 2 * len(range(u, NT, 2)) * 16)
                for g in range(NG):
                    gr_ = Group(2, g // 3, g % 3)
                    if g >= 3:
                        pool.wait_ge(s_xu, (NG + g - 3 + 1) * GB)
                    gather(gr_, slot[:, g * GB:g * GB + GB], NG + g)

        @block.scalar
        def _(act):
            for L in range(2):
                for n in (0, 1):
                    act.dma_start(bnat[2 * L + n:2 * L + n + 1, :], row(bqkvo[L][n])).then_inc(s_bk, 16)
                act.dma_start(bvr[:, L, :], bqkvo[L][2].partition_broadcast(128)).then_inc(s_b, 16)
                act.dma_start(bor[:, L, :], bqkvo[L][3].partition_broadcast(128)).then_inc(s_b, 16)
                act.dma_start(gw[:, L, :], gates[L][0]).then_inc(s_b, 16)
                act.dma_start(gb[:, L, :], gates[L][1].partition_broadcast(128)).then_inc(s_b, 16)
            act.dma_start(gr[:, 0:2], g_xattn.partition_broadcast(128)).then_inc(s_b, 16)
            act.dma_start(gr[:, 2:4], g_ffn.partition_broadcast(128)).then_inc(s_b, 16)
            act.wait_ge(s_b, 10 * 16)
            act.activation(tg[:, :], gr[:, :], ACT.Tanh).then_inc(s_tg, 1)

            def first_part(gr_, src, parts, ready, written, each, rounded):
                N = gr_.count(NG)
                act.wait_ge(ready, N + 1)
                if not (isinstance(N, int) and N == 0):
                    before = Group(0, (NG - 1) // 3, (NG - 1) % 3) if isinstance(gr_.g, int) and gr_.g == 0 else gr_.at(-1)
                    act.wait_ge(written[before.ring], (before.laps(NG) + 1) * each)
                act.activation(parts[:, 0, :], src[:, :], ACT.Copy).then_inc(rounded, 1)

            def second_part(gr_, res, parts, rest, rounded):
                act.wait_ge(rest, gr_.count(NG) + 1)
                act.activation(parts[:, 1, :], res[:, :], ACT.Copy).then_inc(rounded, 1)

            def keep_max(gr_, b):
                n = gr_.count(NG) * GB + b
                act.wait_ge(s_mTp, n + 1)
                wait(act, s_md[b], (gr_.count(NG)) * 32)
                act.activation(mT[:, b, :], M[b][0:48, 0:64].bitcast(bf16), ACT.Copy).then_inc(s_mTe, 1)

            def step(c, A0, A1, A2, A3, B, C, D, D2):
                s, a, d = c.at(1), c.at(3), c.at(-1)
                for n in range(8):
                    if C:
                        m = c.count(NG) * 8 + n
                        act.wait_ge(s_st, m + 1)
                        wait(act, s_pv, m - 3)
                        act.activation(P[:, n % 4, :], ST[n % 2][:, :], ACT.Exp).then_inc(s_exp, 1)
                    if n == 0 and A2:
                        act.wait_ge(s_xT, a.count(NG) + 1)
                        wait(act, s_q, a.count(NG))
                        act.activation(xT[:, :], M[0][:, 0:W], ACT.Copy).then_inc(s_xTe, 1)
                    if n == 1:
                        if C:
                            keep_max(c, 1)
                        if A2:
                            act.wait_ge(s_q, a.count(NG) + 1)
                            wait(act, s_qs, a.count(NG))
                            act.activation(Qf[:, :], M[0][:, 0:W], ACT.Identity, scale=SCALE,
                                           bias=bcol[:, 2 * a.layer:2 * a.layer + 1]).then_inc(s_qf, 1)
                            first_part(a, Qf, qp, s_qf, s_qw, 32, s_qi)
                    if n == 2 and A2:
                        act.wait_ge(s_cTp, a.count(NG) + 1)
                        wait(act, s_v, a.count(NG) - 2)
                        act.activation(cgT[a.ring][:, :], M[1][:, 0:W], ACT.Copy).then_inc(s_cTe, 1)
                    if n == 3 and A2:
                        second_part(a, qres, qp, s_qt, s_qi)
                    if n == 3 and A2:
                        if a.layer == 0:
                            act.wait_ge(s_k, a.count(NG) + 1)
                            wait(act, s_ks, a.count(NG))
                            act.activation(Kf[:, :], M[0][:, 0:W], ACT.Identity, bias=bcol[:, 1:2]).then_inc(s_kf, 1)
                    if n == 4 and A2:
                        first_part(a, Kf, kp, s_kf, s_kw, 16, s_ki)
                    if n == 5 and B:
                        keep_max(s, 0)
                    if n == 6 and A2:
                        second_part(a, kres, kp, s_kt, s_ki)
                    if n == 7 and D:
                        act.wait_ge(s_x2T, d.count(NG) + 1)
                        wait(act, s_lg, d.count(NG))
                        act.activation(x2T[:, :], M[1][:, 0:W], ACT.Copy).then_inc(s_x2Te, 1)

            def slot_step(t, T2, F1, F2):
                if T2:
                    t2 = t.at(2)
                    n = t2.count(NT)
                    act.wait_ge(s_ft, n + 1)
                    wait(act, s_f1, n - 1)
                    act.activation(xsT[t2.u][:, :], M[t2.u][:, 0:T], ACT.Copy).then_inc(s_fte, 1)
                if F1:
                    t1 = t.at(1)
                    n = t1.count(NT)
                    act.wait_ge(s_fb, n + 1)
                    wait(act, s_f2, n - 1)
                    act.activation(hT[t1.u][:, :, :], hb[t1.u][:, :, :], ACT.Gelu).then_inc(s_fg, 1)

            act.wait_ge(s_wo_s, 5)
            for L in range(1 if stage == 0 else 2):
                attention(act, L, step)
                if stage == 0:
                    break
                act.wait_ge(s_rt, L * 16 + 2)
                act.activation(expd[:, :, :], below[:, :, :], ACT.Exp).then_inc(s_rx, 1)
                experts(act, L, slot_step)

        @block.vector
        def _(dve):
            for j in range(3):
                dve.memset(Kst[j][96:128, :, :, :], 1.0).then_inc(s_kz, 1)
                dve.wait_ge(s_kz, 2 * j + 1)
                dve.memset(Kst[j][96:96 + 3, :, :, :], 0.0).then_inc(s_kz, 1)
                if j == 0:
                    dve.wait_ge(s_qz, 1)
                else:
                    dve.memset(Qst[j][96:128, :, :, :, :], 0.0).then_inc(s_q0, 1)
                    dve.wait_ge(s_q0, j)
                dve.memset(Qst[j][96:96 + 3, :, :, :, :], 1.0).then_inc(s_cst, 1)
            for L in range(2):
                for n in range(4):
                    m = 4 * L + n
                    dve.wait_ge(s_wtp, m + 1)
                    src = M[m % 2][:, 0:128]
                    if n < 2:
                        for s in range(2):
                            last = dve.tensor_copy(wT[:, m, :].rearrange("p (s d k e) -> p s d k e", s=2, d=DK, k=4)[:, s],
                                                   src.rearrange("p (e s k d) -> p s d k e", s=2, d=DK, k=4)[:, s])
                        last.then_inc(s_wte, 1)
                    else:
                        dve.tensor_copy(wT[:, m, :], src).then_inc(s_wte, 1)
            dve.wait_ge(s_tg, 1)
            dve.wait_ge(s_wte, 8)
            dve.wait_ge(s_bk, 4 * 16)
            for s in range(2):
                last = dve.tensor_copy(bperm[:, :].rearrange("p (s d k e) -> p s d k e", s=2, d=DK, k=4)[:, s],
                                       bnat[:, :].rearrange("p (e s k d) -> p s d k e", s=2, d=DK, k=4)[:, s])
            last.then_inc(s_bp, 1)
            dve.wait_ge(s_bT, 1)
            dve.tensor_copy(bcol[:, :], M[0][:, 0:4]).then_inc(s_bc, 1)
            dve.wait_ge(s_bc, 1)
            for L in range(2):
                dve.tensor_scalar(wT[:, 4 * L + 3, :], wT[:, 4 * L + 3, :], tg[:, L:L + 1], None, ALU.mult).then_inc(s_wo_s, 1)
                dve.tensor_scalar(bor[:, L, :], bor[:, L, :], tg[:, L:L + 1], None, ALU.mult).then_inc(s_wo_s, 1)
            dve.tensor_scalar(bcol[:, :].rearrange("p (l n) -> p l n", n=2)[:, :, 0],
                              bcol[:, :].rearrange("p (l n) -> p l n", n=2)[:, :, 0], SCALE, None, ALU.mult).then_inc(s_wo_s, 1)
            dve.wait_ge(s_mk, 32)
            dve.tensor_scalar(mval[:, :], mask8[:, :], FILL, -FILL, ALU.mult, ALU.add).then_inc(s_mst, 1)
            dve.wait_ge(s_mst, 1)
            dve.tensor_copy(mparts[:, 0, :], mval[:, :]).then_inc(s_mst, 1)
            dve.wait_ge(s_mst, 2)
            dve.tensor_tensor(mres[:, :], mval[:, :], mparts[:, 0, :], ALU.subtract).then_inc(s_mst, 1)
            dve.wait_ge(s_mst, 3)
            dve.tensor_copy(mparts[:, 1, :], mres[:, :]).then_inc(s_mst, 1)
            dve.wait_ge(s_mst, 4)
            dve.tensor_tensor(mparts[:, 2, :], mres[:, :], mparts[:, 1, :], ALU.subtract).then_inc(s_mst, 1)

            def norm(gr_, b):
                n = gr_.count(NG) * GB + b
                dve.wait_ge(s_pv, gr_.count(NG) * 8 + 4 * b + 4)
                dve.reciprocal(R[:, b, :], PV[b][:, 128:256]).then_inc(s_rec, 1)
                dve.wait_ge(s_rec, n + 1)
                wait(dve, s_wo, n - 1)
                dve.tensor_tensor(cT[:, b, :], PV[b][:, 0:128], R[:, b, :], ALU.mult).then_inc(s_nrm, 1)

            def x_add(gr_, b):
                n = gr_.count(NG) * GB + b
                dve.wait_ge(s_wo, n + 1)
                dve.wait_ge(s_xb, gr_.count(NG) + 1)
                at = one(gr_.g * GB + b)
                dve.tensor_tensor(x_sb[:, at, :], x_sb[:, at, :],
                                  PV[b][:, 256:384].rearrange("p (o n) -> p o n", o=1), ALU.add).then_inc(s_xa, 1)

            def x_update(gr_, layer, N, j):
                dve.wait_ge(s_yg[j], (gr_.turn + 1 + (layer - 1) * len(range(j, NG, 3))) * GB * 16)
                for b in range(GB):
                    at = one(gr_.g * GB + b)
                    dve.scalar_tensor_tensor(x_sb[:, at, :], yg[j][:, b:b + 1, :], gate[:, at], x_sb[:, at, :],
                                             ALU.mult, ALU.add).then_inc(s_xu, 1)

            def stats(gr_, st, mv, s_stat, s_agg, s_used, N):
                alone(dve, s_used, N)
                for b in range(GB):
                    dve.bn_stats(st[:, b, :], x_sb[:, one(gr_.g * GB + b), :].rearrange("p o n -> p (o n)")).then_inc(s_stat, 1)
                for b in range(GB):
                    alone(dve, s_stat, N * GB + b + 1)
                    last = dve.bn_aggr(mv[:, b, :], st[:, b, :])
                last.then_inc(s_agg, 1)

            def normed(gr_, mv, rs, to, done):
                for b in range(GB):
                    last = dve.tensor_scalar(to(b), x_sb[:, one(gr_.g * GB + b), :], mv[:, b, 0:1], rs[:, b:b + 1],
                                             ALU.subtract, ALU.mult)
                last.then_inc(done, 1)

            def step(c, A0, A1, A2, A3, B, C, D, D2):
                s, l, a, d, e, a1 = c.at(1), c.at(2), c.at(3), c.at(-1), c.at(-2), c.at(4)
                for n in range(8):
                    if B:
                        m = s.count(NG) * 8 + n
                        b, k = n // 4, n % 4
                        dve.wait_ge(s_s, m + 1)
                        if k == 0:
                            wait(dve, s_ns, s.count(NG) * GB + b - 1)
                        dve.tensor_reduce(negm[:, b, :, 2 * k:2 * k + 2].rearrange("q s e -> q e s"),
                                          SB[n % 2][:, :].rearrange("q (e s k) -> q e s k", e=2, s=2), AX, ALU.max,
                                          negate=True).then_inc(s_max, 1)
                    if n == 0:
                        if D2:
                            dve.wait_ge(s_lg, e.count(NG) + 1)
                            dve.tensor_tensor(logits[:, span(e), :], M[1][:, 0:GB * E].rearrange("p (b e) -> p b e", e=E),
                                              gb[:, e.layer:e.layer + 1, :].to_broadcast([128, GB, E]), ALU.add).then_inc(s_lga, 1)
                        if D:
                            x_add(d, 0)
                    if n == 1 and D:
                        norm(d, 1)
                    if n == 2:
                        if A1:
                            if a1.layer == 0:
                                dve.wait_ge(s_x, 16 * NXD)
                            else:
                                x_update(a1, 1, a1.g, a1.ring)
                                alone(dve, s_xu, (a1.g + 1) * GB)
                            stats(a1, st1, mv1, s_st1, s_ag1, s_xn, a1.count(NG))
                    if n == 3 and A1:
                        dve.wait_ge(s_pw1, a1.count(NG) + 1)
                        wait(dve, s_xT, a1.count(NG))
                        normed(a1, mv1, rs1, lambda b: xn[:, b:b + 1, :], s_xn)
                    if n == 4 and D:
                        x_add(d, 1)
                    if n == 3 and A2 and a.layer == 1:
                        dve.wait_ge(s_k, a.count(NG) + 1)
                        wait(dve, s_ks, a.count(NG))
                        dve.scalar_tensor_tensor(Kf[:, :], M[0][:, 0:W], bcol[:, 3:4], maskrep[:, cols(a)],
                                                 ALU.add, ALU.mult).then_inc(s_kf, 1)
                    if n == 4:
                        if A3:
                            dve.wait_ge(s_v, l.count(NG) + 1)
                            wait(dve, s_pv, (l.count(NG) - 3) * 8 + 8)
                            for k in range(4):
                                last = dve.tensor_tensor(
                                    Vm[l.ring][:, :, k, :].rearrange("p b (g c) -> p b g c", c=32)[:, :, :, 8 * k:8 * k + 8],
                                    M[1][:, 0:W].rearrange("p (b g k d) -> p k b g d", b=GB, k=4, d=DK)[:, k],
                                    bvr[:, l.layer:l.layer + 1, :].to_broadcast([128, GB, DM]).rearrange(
                                        "p b (g k d) -> p k b g d", k=4, d=DK)[:, k], ALU.add)
                            last.then_inc(s_vm, 1)
                    if n == 4:
                        if D:
                            alone(dve, s_xa, (d.count(NG) + 1) * GB)
                            stats(d, st2, mv2, s_st2, s_ag2, s_xn2, d.count(NG))
                    if n == 5 and C:
                        norm(c, 0)
                    if n == 5:
                        if D:
                            dve.wait_ge(s_pw2, d.count(NG) + 1)
                            wait(dve, s_x2T, d.count(NG))
                            wait(dve, s_x2k, d.count(NG))
                            normed(d, mv2, rs2, lambda b: xn2g[:, b:b + 1, :], s_xn2)

            def route(L):
                R0 = L * 16
                n = [R0]

                def then(ins):
                    n[0] += 1
                    ins.then_inc(s_rt, 1)
                    dve.wait_ge(s_rt, n[0])

                dve.wait_ge(s_b1s, L + 1)
                if L == 1:
                    dve.wait_ge(s_sg, NT)
                dve.tensor_copy(ex[:, :, B1:B2], b1T[:, L, :].rearrange("p (e c) -> p e c", c=FC)).then_inc(s_b1s, 1)
                dve.wait_ge(s_lga, NG * (L + 1))
                every = lambda a: a.rearrange("p (b o) -> p b o", o=1).to_broadcast([128, NB, E])
                by_e = lambda a: a.rearrange("p (e o) -> p e o", o=1).to_broadcast([128, E, NB])
                then(dve.tensor_reduce(top[:, :], logits[:, :, :], AX, ALU.max))
                if L == 1:
                    pass
                then(dve.tensor_tensor(below[:, :, :], logits[:, :, :], every(top[:, :]), ALU.subtract))
                then(dve.tensor_scalar(notop[:, :, :], below[:, :, :], 0.0, float(E), ALU.is_lt, ALU.mult))
                then(dve.tensor_tensor(notop[:, :, :], notop[:, :, :], e_row[:, :, :], ALU.add))
                then(dve.tensor_reduce(first[:, :], notop[:, :, :], AX, ALU.min))
                then(dve.tensor_tensor(chosen[:, :, :], e_row[:, :, :], every(first[:, :]), ALU.is_equal))
                dve.wait_ge(s_rc, L + 1)
                then(dve.tensor_copy(tot[:, :, :], PV[0][:, 256:512].rearrange("p (b e) -> p e b", e=E)))
                then(dve.tensor_reduce(cnt[:, :], tot[:, :, :], AX, ALU.add))
                dve.tensor_scalar(cnt_i[:, 0, :], cnt[:, :], float(T - 1), None, ALU.add).then_inc(s_set, 1)
                dve.wait_ge(s_set, L * 5 + 1)
                dve.tensor_scalar(cnt_i[:, 1, :], cnt_i[:, 0, :], T.bit_length() - 1, None, ALU.arith_shift_right).then_inc(s_set, 1)
                dve.wait_ge(s_set, L * 5 + 2)
                dve.tensor_copy(tiles[:, :], cnt_i[:, 1, :]).then_inc(s_set, 1)
                dve.wait_ge(s_set, L * 5 + 3)
                dve.tensor_tensor_scan(cumt[:, :], ones[:, 0:E], tiles[:, :], 0.0, ALU.mult, ALU.add).then_inc(s_set, 1)
                dve.tensor_tensor_scan(cumn[:, :], ones[:, 0:E], cnt[:, :], 0.0, ALU.mult, ALU.add).then_inc(s_set, 1)
                dve.wait_ge(s_set, L * 5 + 5)
                then(dve.tensor_tensor(off[:, :], cumt[:, :], tiles[:, :], ALU.subtract))
                then(dve.scalar_tensor_tensor(off[:, :], off[:, :], float(T), cumn[:, :], ALU.mult, ALU.subtract))
                then(dve.tensor_tensor(off[:, :], off[:, :], cnt[:, :], ALU.add))
                then(dve.tensor_tensor_scan(cum[:, :, :].rearrange("p e b -> p (e b)"), ones[:, :],
                                            tot[:, :, :].rearrange("p e b -> p (e b)"), 0.0, ALU.mult, ALU.add))
                then(dve.tensor_tensor(pos[:, :, :], cum[:, :, :], tot[:, :, :], ALU.subtract))
                then(dve.tensor_tensor(pos[:, :, :], pos[:, :, :], by_e(off[:, :]), ALU.add))
                then(dve.tensor_tensor(pos[:, :, :], PV[0][:, 0:256].rearrange("p (b e) -> p e b", e=E), pos[:, :, :], ALU.add))
                then(dve.tensor_tensor(pos[:, :, :], pos[:, :, :], chosen[:, :, :].rearrange("p b e -> p e b"), ALU.mult))
                assert n[0] == R0 + 16
                dve.tensor_reduce(slot_f[:, :], pos[:, :, :].rearrange("p e b -> p b e"), AX, ALU.add).then_inc(s_sl, 1)
                dve.tensor_tensor(past[:, :, :], t_row[:, :, :],
                                  cumt[0:1, :].rearrange("p (o e) -> p o e", o=1).to_broadcast([1, NT, E]), ALU.is_ge).then_inc(s_sl, 1)
                dve.wait_ge(s_sl, L * 4 + 2)
                dve.tensor_copy(slot[:, :], slot_f[:, :]).then_inc(s_sl, 1)
                dve.tensor_reduce(texp_f[:, :], past[:, :, :], AX, ALU.add).then_inc(s_sl, 1)
                dve.wait_ge(s_sl, L * 4 + 4)
                if L == 1:
                    dve.wait_ge(s_sg, NT)
                    dve.wait_ge(s_f2, NT)
                dve.tensor_scalar(texp[:, :], texp_f[:, :], float(E - 1), None, ALU.min).then_inc(s_slot, 1)
                dve.wait_ge(s_rx, L + 1)
                dve.tensor_reduce(gsum[:, :], expd[:, :, :], AX, ALU.add).then_inc(s_gt, 1)
                dve.wait_ge(s_gt, L * 3 + 1)
                dve.reciprocal(gate[:, :], gsum[:, :]).then_inc(s_gt, 1)
                dve.wait_ge(s_gt, L * 3 + 2)
                dve.tensor_scalar(gate[:, :], gate[:, :], tg[:, 2 + L:3 + L], None, ALU.mult).then_inc(s_gt, 1)
                dve.wait_ge(s_gt, L * 3 + 3)

            def slot_step(t, T2, F1, F2):
                if T2:
                    t2 = t.at(2)
                    e = dve.value_load(texp[0:1, one(t2.i)], min_val=0, max_val=E - 1)
                    wait(dve, s_f1, t2.count(NT) - 3)
                    wait(dve, s_fy, t2.count(NT) - 3)
                    dve.tensor_copy(stg[t2.v][:, :], ex[:, bass.ds(e, 1), 0:W2].rearrange("p o n -> p (o n)")).then_inc(s_sg, 1)
                if F1:
                    t1 = t.at(1)
                    n = t1.count(NT)
                    dve.wait_ge(s_f1, n + 1)
                    wait(dve, s_fg, n - 1)
                    dve.tensor_tensor(hb[t1.u][:, :, :], SB[t1.u][:, :].rearrange("p (c t) -> p c t", c=FC),
                                      stg[t1.v][:, B1:B2].rearrange("p (c o) -> p c o", o=1).to_broadcast([128, FC, T]),
                                      ALU.add).then_inc(s_fb, 1)
                if F2:
                    n = t.count(NT)
                    dve.wait_ge(s_f2, n + 1)
                    wait(dve, s_ysw[t.u], t.laps2(NT) * 16)
                    dve.tensor_tensor(ys[t.u][:, :], ST[t.u][:, 0:DM], stg[t.v][:, B2:W2], ALU.add).then_inc(s_fy, 1)

            dve.wait_ge(s_ri, 2)
            dve.tensor_copy(e_row[:, :, :], e_int[:, :, :]).then_inc(s_rk, 1)
            dve.tensor_copy(t_row[:, :, :], t_int[:, :, :]).then_inc(s_rk, 1)
            dve.wait_ge(s_b1t, 1)
            dve.tensor_copy(b1T[:, :, :], M[1][:, 0:2 * E * FC].rearrange("p (l n) -> p l n", l=2)).then_inc(s_b1s, 1)
            dve.wait_ge(s_rk, 2)

            for L in range(1 if stage == 0 else 2):
                attention(dve, L, step)
                if stage == 0:
                    break
                route(L)
                dve.wait_ge(s_ex, (L + 1) * 6 * 16)
                dve.wait_ge(s_b1s, L + 2)
                experts(dve, L, slot_step)
            if stage > 0:
                for g in range(NG):
                    x_update(Group(2, g // 3, g % 3), 2, NG + g, g % 3)

        @block.tensor
        def _(pe):
            pe.wait_ge(s_id, 3)
            for m in range(8):
                if m == 0:
                    pe.wait_ge(s_w, 8 * 16)
                wait(pe, s_wte, m - 1)
                pe.transpose(M[m % 2][:, 0:128], wnat[:, m, :], ident[:, :]).then_inc(s_wtp, 1)
            pe.wait_ge(s_wte, 8)
            pe.wait_ge(s_bp, 1)
            pe.transpose(M[0][:, 0:4], bperm[:, :], ident[0:4, 0:4]).then_inc(s_bT, 1)
            pe.wait_ge(s_wo_s, 5)
            pe.wait_ge(s_cst, 12)
            pe.wait_ge(s_kz, 6)
            pe.wait_ge(s_b1l, 32)
            for L in range(2):
                last = pe.transpose(M[1][:, 32 * L:32 * L + 32], b1n[:, L, :], ident[0:32, 0:32])
            last.then_inc(s_b1t, 1)
            pe.wait_ge(s_b1s, 1)

            def scores(gr_, n):
                m, b, k = gr_.count(NG) * 8 + n, n // 4, n % 4
                if n == 0:
                    pe.wait_ge(s_qr[gr_.ring], (gr_.laps(NG) + 1) * len(RUNS) * 16)
                    pe.wait_ge(s_kr[gr_.ring], k_loads(gr_))
                wait(pe, s_max, m - 1)
                q, kk = Qst[gr_.ring], Kst[gr_.ring]
                for e in range(2):
                    for s in range(2):
                        c0 = (2 * e + s) * 128
                        last = pe.matmul(SB[n % 2][:, c0:c0 + 128], q[0:RS, 2 * k + e, s, b, :], kk[0:RS, 2 * k + e, b, :],
                                         start=True, stop=True)
                last.then_inc(s_s, 1)

            def shifted(gr_, n):
                m, b, k = gr_.count(NG) * 8 + n, n // 4, n % 4
                if k == 0:
                    pe.wait_ge(s_md[b], (gr_.count(NG) + 1) * 32)
                wait(pe, s_exp, m - 1)
                for e in range(2):
                    last = pe.matmul(ST[n % 2][:, 256 * e:256 * e + 256], Kst[gr_.ring][0:RT, 2 * k + e, b, :],
                                     Qst[gr_.ring][0:RT, 2 * k + e, :, b, :], start=True, stop=True)
                last.then_inc(s_st, 1)

            def values(gr_, n):
                m, b, k = gr_.count(NG) * 8 + n, n // 4, n % 4
                pe.wait_ge(s_exp, m + 1)
                if n == 0:
                    pe.wait_ge(s_vm, gr_.count(NG) + 1)
                if k == 0:
                    wait(pe, s_xa, gr_.count(NG) * GB + b - 1)
                for g in range(4):
                    pe.matmul(PV[b][32 * g:32 * g + 32, 0:128], Vm[gr_.ring][:, b, k, 32 * g:32 * g + 32],
                              P[:, n % 4, 128 * g:128 * g + 128], start=(k == 0), stop=(k == 3), skip_group_check=True)
                for g in range(4):
                    last = pe.matmul(PV[b][32 * g:32 * g + 32, 128:256], ones_m[:, k, :],
                                     P[:, n % 4, 128 * g:128 * g + 128], start=False, stop=(k == 3), skip_group_check=True)
                last.then_inc(s_pv, 1)

            def out_proj(gr_, b):
                pe.wait_ge(s_nrm, gr_.count(NG) * GB + b + 1)
                pe.matmul(PV[b][:, 256:384], cT[:, b, :], wT[:, 4 * gr_.layer + 3, :], start=True, stop=True).then_inc(s_wo, 1)

            def max_rows(gr_, b):
                alone(pe, s_ns, gr_.count(NG) * GB + b + 1)
                pe.transpose(M[b][0:48, 0:64].bitcast(bf16), negp[:, b, :, :, :].rearrange("q s t p -> q (s t p)"),
                             identb[:, :]).then_inc(s_mTp, 1)

            def step(c, A0, A1, A2, A3, B, C, D, D2):
                s, l, a, d, e = c.at(1), c.at(2), c.at(3), c.at(-1), c.at(-2)
                N = a.count(NG)
                for n in range(8):
                    if C:
                        shifted(c, n)
                    if B:
                        scores(s, n)
                    if n == 4 and A2:
                        pe.wait_ge(s_cTe, N + 1)
                        pe.wait_ge(s_qf, N + 1)
                        pe.matmul(M[0][:, 0:W], wT[:, 4 * a.layer + 1, :], cgT[a.ring][:, :], start=True, stop=True).then_inc(s_k, 1)
                    if n >= 2 and C:
                        values(c, n - 2)
                    if n < 2 and D:
                        values(d, n + 6)
                    if n == 0 and D2:
                        pe.wait_ge(s_x2Te, e.count(NG) + 1)
                        for b in range(GB):
                            last = pe.matmul(M[1][:, E * b:E * b + E], x2T[:, 128 * b:128 * b + 128], gw[:, e.layer, :],
                                             start=True, stop=True)
                        last.then_inc(s_lg, 1)
                    if n == 0 and A2:
                        pe.wait_ge(s_xn, N + 1)
                        wait(pe, s_kf, N)
                        wait(pe, s_mTe, c.count(NG) * GB + 1)
                        for b in range(GB):
                            last = pe.transpose(M[0][:, 128 * b:128 * b + 128], xn[:, b, :], ident[:, :])
                        last.then_inc(s_xT, 1)
                    if n == 1 and C:
                        wait(pe, s_lga, c.count(NG) - 1)
                        wait(pe, s_vm, c.count(NG) + 2 if A3 else NG * (c.layer + 1))
                        max_rows(c, 1)
                    if n == 1 and A2:
                        pe.wait_ge(s_xTe, N + 1)
                        pe.matmul(M[0][:, 0:W], wT[:, 4 * a.layer, :], xT[:, :], start=True, stop=True).then_inc(s_q, 1)
                    if n == 3 and D:
                        out_proj(d, 1)
                    if n == 2:
                        if A2:
                            pe.wait_ge(s_c[a.ring], (a.laps(NG) + 1) * 16)
                            wait(pe, s_vm, N - 1)
                            wait(pe, s_mTe, c.count(NG) * GB + 2)
                            for b in range(GB):
                                last = pe.transpose(M[1][:, 128 * b:128 * b + 128], cg[a.ring][:, b, :], ident[:, :])
                            last.then_inc(s_cTp, 1)
                    if n == 4 and A3:
                        wait(pe, s_mTe, c.count(NG) * GB + 2)
                        pe.wait_ge(s_cTe, N + 1 if A2 else NG * (l.layer + 1))
                        for b in range(GB):
                            last = pe.matmul(M[1][:, 128 * b:128 * b + 128], cgT[l.ring][:, 128 * b:128 * b + 128], wT[:, 4 * l.layer + 2, :],
                                             start=True, stop=True)
                        last.then_inc(s_v, 1)
                    if n == 5 and B:
                        if A2:
                            pe.wait_ge(s_kf, N + 1)
                        max_rows(s, 0)
                    if n == 7:
                        if C:
                            out_proj(c, 0)
                        if D:
                            pe.wait_ge(s_xn2, d.count(NG) + 1)
                            if A3:
                                pe.wait_ge(s_vm, l.count(NG) + 1)
                            elif C:
                                pe.wait_ge(s_mTe, c.count(NG) * GB + 2)
                            for b in range(GB):
                                last = pe.transpose(M[1][:, 128 * b:128 * b + 128], xn2g[:, b, :], ident[:, :])
                            last.then_inc(s_x2T, 1)

            def slot_step(t, T2, F1, F2):
                if T2:
                    t2 = t.at(2)
                    n = t2.count(NT)
                    pe.wait_ge(s_xl[t2.v], (t2.laps4(NT) + 1) * 16)
                    wait(pe, s_fte, n - 1)
                    pe.transpose(M[t2.u][:, 0:T], xs[t2.v][:, :], ident[:, :]).then_inc(s_ft, 1)
                if F1:
                    t1 = t.at(1)
                    n = t1.count(NT)
                    pe.wait_ge(s_fte, n + 1)
                    pe.wait_ge(s_sg, n + 1)
                    wait(pe, s_fb, n - 1)
                    for c in range(FC):
                        last = pe.matmul(SB[t1.u][:, c * T:(c + 1) * T], stg[t1.v][:, c * 128:(c + 1) * 128], xsT[t1.u][:, :],
                                         start=True, stop=True)
                    last.then_inc(s_f1, 1)
                if F2:
                    n = t.count(NT)
                    e = pe.value_load(texp[0:1, one(t.i)], min_val=0, max_val=E - 1)
                    pe.wait_ge(s_fg, n + 1)
                    wait(pe, s_fy, n - 1)
                    for c in range(FC):
                        last = pe.matmul(ST[t.u][:, 0:DM], hT[t.u][:, c, :],
                                         ex[:, bass.ds(e, 1), W2 + c * DM:W2 + (c + 1) * DM].rearrange("p o n -> p (o n)"),
                                         start=(c == 0), stop=(c == FC - 1))
                    last.then_inc(s_f2, 1)

            for L in range(1 if stage == 0 else 2):
                attention(pe, L, step)
                if stage == 0:
                    break
                pe.wait_ge(s_rt, L * 16 + 6)
                pe.wait_ge(s_ri, 5)
                pe.wait_ge(s_xa, NB * (L + 1))
                pe.matmul(PV[0][:, 0:256], tri[:, :], chosen[:, :, :].rearrange("p b e -> p (b e)"), start=True, stop=True)
                pe.matmul(PV[0][:, 256:512], ones[:, 0:128], chosen[:, :, :].rearrange("p b e -> p (b e)"),
                          start=True, stop=True).then_inc(s_rc, 1)
                pe.wait_ge(s_lga, NG * (L + 1))
                pe.wait_ge(s_x2Te, NG * (L + 1))
                pe.wait_ge(s_slot, L + 1)
                pe.wait_ge(s_ex, (L + 1) * 6 * 16)
                experts(pe, L, slot_step)
                if L == 0:
                    pe.wait_ge(s_fy, NT)
                    pe.wait_ge(s_slot, 1)


_INS = ["x", "ctx_1024", "mask_BxS2_bf1", "g_xattn", "g_ffn",
        "L0_xattn_wq", "L0_xattn_bq", "L0_xattn_wk", "L0_xattn_bk", "L0_xattn_wv", "L0_xattn_bv", "L0_xattn_wo",
        "L0_xattn_bo", "L0_ffn_gate_w", "L0_ffn_gate_b", "L0_ffn_w1", "L0_ffn_b1", "L0_ffn_w2", "L0_ffn_b2",
        "L1_xattn_Wq", "L1_xattn_bq", "L1_xattn_Wk", "L1_xattn_bk", "L1_xattn_Wv", "L1_xattn_bv", "L1_xattn_Wo",
        "L1_xattn_bo", "L1_ffn_W1", "L1_ffn_b1", "L1_ffn_W2", "L1_ffn_b2", "L1_ffn_Wr", "L1_ffn_br"]


def kernel(**inputs):
    import numpy as _np
    import concourse.bacc as _bacc
    from concourse import mybir as _mybir
    from concourse.bass_utils import run_bass_kernel_spmd as _run

    nc = _bacc.Bacc("TRN2", target_bir_lowering=False, num_devices=1)
    arrays, args = {}, []
    for name in _INS:
        a = _np.ascontiguousarray(inputs[name])
        if a.dtype == _np.bool_:
            a = a.view(_np.uint8)
        arrays[f"in_{name}_dram"] = a
        args.append(nc.dram_tensor(f"in_{name}_dram", a.shape, _mybir.dt.from_np(a.dtype), kind="ExternalInput").ap())
    out = nc.dram_tensor("out_0_dram", inputs["x"].shape, _mybir.dt.float32, kind="ExternalOutput").ap()
    flamingo_kernel(nc, *args, out)
    r = _run(nc, [arrays], core_ids=[0])
    return r.results[0]["out_0_dram"]
```

```python
import numpy as np
from contextlib import ExitStack

import concourse.bass as bass
from concourse import mybir
from concourse.alu_op_type import AluOpType as ALU


class Tile:

    def __init__(self, layer, lap, v):
        self.layer, self.lap, self.v = layer, lap, v

    def at(self, k):
        v = self.v + k
        return Tile(self.layer, self.lap + v // 4, v % 4)

    @property
    def i(self):
        return self.lap * 4 + self.v

    @property
    def u(self):
        return self.v % 2

    def count(self, n_tiles):
        return self.lap * 4 + (self.v + n_tiles * self.layer)

    def laps2(self, n_tiles):
        return self.lap * 2 + (self.v // 2 + self.layer * len(range(self.u, n_tiles, 2)))

    def laps4(self, n_tiles):
        return self.lap + self.layer * len(range(self.v, n_tiles, 4))


class Group:

    def __init__(self, layer, turn, ring):
        self.layer, self.turn, self.ring = layer, turn, ring

    def at(self, k):
        r = self.ring + k
        return Group(self.layer, self.turn + r // 3, r % 3)

    @property
    def g(self):
        return self.turn * 3 + self.ring

    def count(self, n_groups):
        return self.turn * 3 + (self.ring + n_groups * self.layer)

    def laps(self, n_groups):
        return self.turn + self.layer * len(range(self.ring, n_groups, 3))


def wait(eng, sem, value):
    if isinstance(value, int) and value <= 0:
        return
    eng.wait_ge(sem, value)


def alone(eng, sem, value):
    wait(eng, sem, value)
    if not isinstance(value, int):
        eng.nop(nofuse=True)


def flamingo_kernel(nc, x, ctx_1024, mask_BxS2_bf1, g_xattn, g_ffn,
                    L0_xattn_wq, L0_xattn_bq, L0_xattn_wk, L0_xattn_bk, L0_xattn_wv, L0_xattn_bv, L0_xattn_wo,
                    L0_xattn_bo, L0_ffn_gate_w, L0_ffn_gate_b, L0_ffn_w1, L0_ffn_b1, L0_ffn_w2, L0_ffn_b2,
                    L1_xattn_Wq, L1_xattn_bq, L1_xattn_Wk, L1_xattn_bk, L1_xattn_Wv, L1_xattn_bv, L1_xattn_Wo,
                    L1_xattn_bo, L1_ffn_W1, L1_ffn_b1, L1_ffn_W2, L1_ffn_b2, L1_ffn_Wr, L1_ffn_br, out):
    f32, bf16, u8 = mybir.dt.float32, mybir.dt.bfloat16, mybir.dt.uint8
    i32, u32 = mybir.dt.int32, mybir.dt.uint32
    ACT = mybir.ActivationFunctionType
    AX = mybir.AxisListType.X

    NB, S, DM = x.shape
    H, DK = 16, 8
    GB = 2
    NG = NB // GB
    W = GB * S
    NP = H // 2
    PRODUCTS = [(0, 0), (0, 1), (0, 2), (1, 0), (1, 1), (2, 0)]
    NPR = len(PRODUCTS)
    RUNS = [(0, 3), (3, 2), (5, 1)]
    RP = 2 * NPR * DK
    RS = RP + 3
    RT = RS + 6
    E, F = L0_ffn_w1.shape[0], L0_ffn_w1.shape[2]
    FC = F // 128
    T = 128
    NT = NB * S // T + E - 1
    EPS = 1e-5
    SCALE = float(np.float32(1.0) / np.sqrt(np.float32(DK)))
    FILL = 1e8

    wqkvo = [(L0_xattn_wq, L0_xattn_wk, L0_xattn_wv, L0_xattn_wo), (L1_xattn_Wq, L1_xattn_Wk, L1_xattn_Wv, L1_xattn_Wo)]
    bqkvo = [(L0_xattn_bq, L0_xattn_bk, L0_xattn_bv, L0_xattn_bo), (L1_xattn_bq, L1_xattn_bk, L1_xattn_bv, L1_xattn_bo)]
    gates = [(L0_ffn_gate_w, L0_ffn_gate_b), (L1_ffn_Wr, L1_ffn_br)]

    stack = ExitStack()
    with stack:
        def sb(name, shape, dt=f32):
            return stack.enter_context(nc.sbuf_tensor(name, shape, dt))

        def sem(name):
            return stack.enter_context(nc.semaphore(name))

        def row(ap):
            return ap.rearrange("(a n) -> a n", a=1)

        x_sb = sb("x_sb", [128, NB, DM])
        wT = sb("wT", [128, 8, DM])
        bnat = sb("bnat", [4, DM])
        bperm = sb("bperm", [4, DM])
        bcol = sb("bcol", [128, 4])
        bvr = sb("bvr", [128, 2, DM])
        bor = sb("bor", [128, 2, DM])
        gr = sb("gr", [128, 4])
        tg = sb("tg", [128, 4])
        gw = sb("gw", [128, 2, E])
        gb = sb("gb", [128, 2, E])
        ident = sb("ident", [128, 128])
        identb = sb("identb", [128, 128], bf16)
        half = sb("half", [128, 2])
        ones_m = sb("ones_m", [128, 4, 32])
        maskrep = sb("maskrep", [128, NB * S], u8)
        mask8 = sb("mask8", [NB, S], u8)
        mval = sb("mval", [NB, S])
        mparts = sb("mparts", [NB, 3, S], bf16)
        mres = sb("mres", [NB, S])

        B1, B2, W2 = F, F + FC, F + FC + DM
        EW = W2 + FC * DM
        ex = sb("ex", [128, E, EW])
        b1T = sb("b1T", [128, 2, E * FC])
        b1n = sb("b1n", [E * FC, 2, 128])
        tri = sb("tri", [128, 128])
        ones = sb("ones", [128, 256])
        e_row = sb("e_row", [128, NB, E])
        t_row = sb("t_row", [1, NT, E])
        e_int, t_int = sb("e_int", [128, NB, E], i32), sb("t_int", [1, NT, E], i32)
        top, gsum, gate = sb("top", [128, NB]), sb("gsum", [128, NB]), sb("gate", [128, NB])
        below, expd = sb("below", [128, NB, E]), sb("expd", [128, NB, E])
        notop, first, chosen = sb("notop", [128, NB, E]), sb("first", [128, NB]), sb("chosen", [128, NB, E], bf16)
        tot, cum, pos = sb("tot", [128, E, NB]), sb("cum", [128, E, NB]), sb("pos", [128, E, NB])
        cnt, cumn, tiles, cumt, off = (sb(n, [128, E]) for n in ("cnt", "cumn", "tiles", "cumt", "off"))
        cnt_i = sb("cnt_i", [128, 2, E], i32)
        slot_f, slot_i = sb("slot_f", [128, NB]), sb("slot_i", [128, NB], i32)
        within_i, tile_i = sb("within_i", [128, NB], i32), sb("tile_i", [128, NB], i32)
        within, tile = sb("within", [128, NB]), sb("tile", [128, NB], bf16)
        count_i = sb("count_i", [128, 128], i32)
        q1_i, q1 = sb("q1_i", [128, 1], i32), sb("q1", [128, 1])
        spare_i, spare = sb("spare_i", [128, NT], i32), sb("spare", [128, NT])
        at_slot = sb("at_slot", [128, NB, T], bf16)
        wnat = at_slot[:, :, :].rearrange("q b t -> q (b t)")[:, 0:2 * 8 * DM].bitcast(f32).rearrange(
            "p (m n) -> p m n", m=8)
        at_tile = sb("at_tile", [128, NB, NT], bf16)
        token_parts = sb("token_parts", [128, NB, 2, NT], bf16)
        count_b = sb("count_b", [128, 128], bf16)
        tri_b, ones_b = sb("tri_b", [128, 128], bf16), sb("ones_b", [128, 128], bf16)
        row1, id1, empty = sb("row1", [128, NT]), sb("id1", [128, NT]), sb("empty", [128, NT])
        idx = sb("idx", [128, NT, 2], u32)
        past, texp_f, texp = sb("past", [1, NT, E]), sb("texp_f", [1, NT]), sb("texp", [1, NT], i32)
        XR = 4
        stg = [sb(f"stg{v}", [128, EW]) for v in range(XR)]
        xs = [sb(f"xs{v}", [128, DM]) for v in range(XR)]
        xsT = [sb(f"xsT{u}", [128, T]) for u in range(2)]
        hT = [sb(f"hT{u}", [128, FC, T]) for u in range(2)]
        ys = [sb(f"ys{u}", [128, DM]) for u in range(2)]
        yg = [sb(f"yg{j}", [128, GB, DM]) for j in range(3)]
        ixr = [sb(f"ixr{v}", [128, 1], u32) for v in range(XR)]
        ixw = [sb(f"ixw{u}", [128, 1], u32) for u in range(2)]

        Qst = [sb(f"Qst{j}", [128, NP, 2, GB, S], bf16) for j in range(3)]
        Kst = [sb(f"Kst{j}", [128, NP, GB, S], bf16) for j in range(3)]
        Vm = [sb(f"Vm{j}", [128, GB, 4, 128]) for j in range(3)]
        cg = [sb(f"cg{j}", [128, GB, DM]) for j in range(3)]
        cgT = [sb(f"cgT{j}", [128, W]) for j in range(3)]
        xn = sb("xn", [128, GB, DM])
        xn2g = sb("xn2g", [128, GB, DM])
        xT = sb("xT", [128, W])
        Qf, Kf = sb("Qf", [128, W]), sb("Kf", [128, W])
        qres, kres = sb("qres", [128, W]), sb("kres", [128, W])
        qp, kp = sb("qp", [128, 3, W], bf16), sb("kp", [128, 3, W], bf16)
        P = sb("P", [128, 4, 512])
        negm = sb("negm", [128, GB, 2, NP])
        nres = sb("nres", [128, GB, 2, NP])
        negp = sb("negp", [128, GB, 2, 3, NP], bf16)
        mT = sb("mT", [48, GB, 128], bf16)
        R = sb("R", [128, GB, 128])
        cT = sb("cT", [128, GB, 128])
        st1, st2 = sb("st1", [128, GB, 6]), sb("st2", [128, GB, 6])
        mv1, mv2 = sb("mv1", [128, GB, 2]), sb("mv2", [128, GB, 2])
        ve1, ve2 = sb("ve1", [128, GB]), sb("ve2", [128, GB])
        rs1, rs2 = sb("rs1", [128, GB]), sb("rs2", [128, GB])
        x2T = sb("x2T", [128, W])
        logits = sb("logits", [128, NB, E])

        SB = [stack.enter_context(nc.psum_tensor(f"SB{i}", [128, 512], f32)) for i in range(2)]
        ST = [stack.enter_context(nc.psum_tensor(f"ST{i}", [128, 512], f32)) for i in range(2)]
        PV = [stack.enter_context(nc.psum_tensor(f"PV{i}", [128, 512], f32)) for i in range(2)]
        M = [stack.enter_context(nc.psum_tensor(f"M{i}", [128, 512], f32)) for i in range(2)]

        q_dram = nc.dram_tensor("q_parts", [3, 3, 2 * DK, NP * 2 * W], bf16, kind="Internal").ap()
        k_dram = nc.dram_tensor("k_parts", [3, 3, 2 * DK, NP * W], bf16, kind="Internal").ap()
        m_dram = nc.dram_tensor("mask_parts", [3, NB * S], bf16, kind="Internal").ap()

        xn2_dram = nc.dram_tensor("tokens_normed", [NB * S, DM], f32, kind="Internal").ap()
        y_dram = nc.dram_tensor("expert_outputs", [NB * S + NT * T, DM], f32, kind="Internal").ap()

        s_ex, s_b1l, s_b1t, s_b1s = (sem(n) for n in ("experts_loaded", "b1_loaded", "b1_transposed", "b1_stored"))
        s_ri, s_rt = sem("route_constants"), sem("route_steps")
        s_rx, s_rc, s_slot = sem("route_exp"), sem("route_counts"), sem("slots_ready")
        s_oh, s_tp, s_as, s_id1, s_inv, s_tok = sem("tile_one_hot"), sem("token_parts_ready"), sem("slot_one_hot"), sem("slots_tokens_summed"), sem("token_steps"), sem("slots_tokens")
        s_ixr, s_ixw = sem("read_index_copied"), sem("write_index_copied")
        s_sg = sem("stage_filled")
        s_xl = [sem(f"tile_loaded{v}") for v in range(XR)]
        s_ysw = [sem(f"tile_written{u}") for u in range(2)]
        s_ft, s_fte, s_f1, s_fg, s_f2, s_fy = (sem(n) for n in (
            "tile_transposed", "tileT_stored", "hidden_done", "hidden_gelu", "expert_done", "expert_stored"))
        s_yg, s_xu = [sem(f"expert_rows_loaded{j}") for j in range(3)], sem("x_updated")
        s_w, s_x, s_b, s_mk = sem("w_loaded"), sem("x_loaded"), sem("small_loaded"), sem("mask_loaded")
        s_c = [sem(f"ctx_loaded{j}") for j in range(3)]
        s_bn = sem("qk_biases_loaded")
        s_id, s_cst, s_set = sem("ident_steps"), sem("constants_ready"), sem("setup_steps")
        s_tg, s_wtp, s_wte, s_wo_s = sem("tanh_ready"), sem("w_transposed"), sem("w_stored"), sem("out_w_scaled")
        s_mst, s_mpw = sem("mask_steps"), sem("mask_parts_written")
        s_st1, s_pw1, s_xn = sem("norm1_stats"), sem("norm1_rstd"), sem("xn_ready")
        s_v1, s_v2, s_ag1, s_ag2 = sem("norm1_eps"), sem("norm2_eps"), sem("norm1_bn"), sem("norm2_bn")
        s_xT, s_xTe = sem("xT_done"), sem("xT_stored")
        s_cTp, s_cTe = sem("ctxT_done"), sem("ctxT_stored")
        s_q, s_qf, s_k, s_kf, s_v, s_vm = (sem(n) for n in ("q_done", "q_stored", "k_done", "k_stored", "v_done", "v_stored"))
        s_qs, s_ks = sem("q_split"), sem("k_split")
        s_qi, s_ki, s_ni = sem("q_split_steps"), sem("k_split_steps"), sem("max_split_steps")
        s_sl, s_gt, s_rk = sem("slot_steps"), sem("gate_steps"), sem("route_rows")
        s_qt, s_kt = sem("q_rest"), sem("k_rest")
        s_qw, s_kw = [sem(f"q_parts_in_dram{j}") for j in range(3)], [sem(f"k_parts_in_dram{j}") for j in range(3)]
        s_qr, s_kr = [sem(f"q_stack_loaded{j}") for j in range(3)], [sem(f"k_stack_loaded{j}") for j in range(3)]
        s_s, s_max = sem("scores_done"), sem("max_done")
        s_ns, s_mTp, s_mTe = sem("max_split"), sem("max_transposed"), sem("max_stored")
        s_md = [sem(f"max_rows_loaded{b}") for b in range(GB)]
        s_st, s_exp, s_pv = sem("shifted_scores_done"), sem("exp_done"), sem("pv_done")
        s_rec, s_nrm, s_wo, s_xa = sem("recip_done"), sem("ctx_normed"), sem("out_proj_done"), sem("x_added")
        s_xb = sem("out_bias_added")
        s_st2, s_pw2, s_xn2 = sem("norm2_stats"), sem("norm2_rstd"), sem("xn2_ready")
        s_dz, s_bT, s_bp, s_bc = (sem(n) for n in ("dram_zeroed", "bias_transposed", "bias_permuted", "bias_columns"))
        s_qz, s_kz, s_rows = sem("q_stack_zero"), sem("stack_ends_set"), sem("standing_rows_set")
        s_x2k = sem("xn2_in_dram")
        s_x2T, s_x2Te, s_lg, s_lga = sem("xn2T_done"), sem("xn2T_stored"), sem("logits_done"), sem("logits_stored")
        s_out = sem("out_written")

        expert_ins = [(L0_ffn_w1, L0_ffn_b1, L0_ffn_w2, L0_ffn_b2), (L1_ffn_W1, L1_ffn_b1, L1_ffn_W2, L1_ffn_b2)]
        NEX = 2 * FC + 1
        EX_STEPS = list(range(-1, 2)) + list(range(NG - 5, NG + 1))
        assert len(EX_STEPS) == NEX
        TWO_ONES = float(np.array([0x3F803F80], np.uint32).view(np.float32)[0])
        NXD = 4

        def span(gr_):
            return bass.ds(gr_.g * GB, GB) if not isinstance(gr_.g, int) else slice(gr_.g * GB, gr_.g * GB + GB)

        def tokens(gr_):
            n = GB * S
            return bass.ds(gr_.g * n, n) if not isinstance(gr_.g, int) else slice(gr_.g * n, gr_.g * n + n)

        def one(index):
            return bass.ds(index, 1) if not isinstance(index, int) else slice(index, index + 1)

        def cols(gr_):
            return bass.ds(gr_.g * W, W) if not isinstance(gr_.g, int) else slice(gr_.g * W, gr_.g * W + W)

        def turns(layer, step):
            def parts(g):
                return {"A0": -5 <= g <= NG - 6, "A1": -4 <= g <= NG - 5, "A2": -3 <= g <= NG - 4, 
                        "A3": -2 <= g <= NG - 3, "B": -1 <= g <= NG - 2, "C": 0 <= g <= NG - 1, "D": 1 <= g <= NG, "D2": 2 <= g <= NG + 1}
            first, rounds = 2, (NG - 5) // 3
            for g in range(-5, first):
                step(Group(layer, g // 3, g % 3), **parts(g))
            yield rounds, lambda i: [step(Group(layer, i + (first + u) // 3, (first + u) % 3), **parts(first))
                                     for u in range(3)]
            for g in range(first + 3 * rounds, NG + 2):
                step(Group(layer, g // 3, g % 3), **parts(g))

        def experts(eng, L, step):
            for i in range(-2, 2):
                step(Tile(L, i // 4, i % 4), T2=True, F1=i >= -1, F2=i >= 0)
            rounds = (NT - 4) // 4
            with eng.Fori(0, rounds) as h:
                for u in range(2, 6):
                    step(Tile(L, h + u // 4, u % 4), T2=True, F1=True, F2=True)
            for i in range(2 + 4 * rounds, NT):
                step(Tile(L, i // 4, i % 4), T2=i + 2 < NT, F1=i + 1 < NT, F2=True)

        def attention(eng, layer, step):
            for n, body in turns(layer, step):
                with eng.Fori(0, n) as i:
                    body(i)

        block = stack.enter_context(nc.Block())

        @block.sync
        def _(sp):
            for L in range(2):
                for n in range(4):
                    sp.dma_start(wnat[:, 4 * L + n, :], wqkvo[L][n]).then_inc(s_w, 16)
            for n in range(NXD):
                k = NB // NXD
                sp.dma_start(x_sb[:, n * k:(n + 1) * k, :], x[n * k:(n + 1) * k].rearrange("b s d -> s b d")).then_inc(s_x, 16)
            sp.dma_start(maskrep[:, :], mask_BxS2_bf1.rearrange("b s -> (b s)").partition_broadcast(128)).then_inc(s_mk, 16)
            sp.dma_start(mask8[:, :], mask_BxS2_bf1).then_inc(s_mk, 16)
            def expert_load(L, part):
                w1, b1, w2, b2 = expert_ins[L]
                c = part % FC
                if part < FC:
                    sp.dma_start(ex[:, :, c * 128:(c + 1) * 128],
                                 w1[:, :, c * 128:(c + 1) * 128].rearrange("e p n -> p e n")).then_inc(s_ex, 16)
                elif part < 2 * FC:
                    sp.dma_start(ex[:, :, W2 + c * DM:W2 + (c + 1) * DM],
                                 w2[:, c * 128:(c + 1) * 128, :].rearrange("e p n -> p e n")).then_inc(s_ex, 16)
                else:
                    sp.dma_start(ex[:, :, B2:W2], b2.partition_broadcast(128)).then_inc(s_ex, 16)

            for L in range(2):
                sp.dma_start(b1n[:, L, :], expert_ins[L][1].rearrange("e (c p) -> (e c) p", p=128)).then_inc(s_b1l, 16)
            sp.wait_ge(s_qz, 1)
            for j in range(3):
                sp.dma_start(q_dram[j].rearrange("t r n -> (t r) n"), Qst[0][0:6 * DK].rearrange("r p s b q -> r (p s b q)")
                             ).then_inc(s_dz, 16)

            def max_rows(gr_, b):
                alone(sp, s_mTe, gr_.count(NG) * GB + b + 1)
                for s in range(2):
                    sp.dma_start(Qst[gr_.ring][RS + 3 * s:RS + 3 * s + 3, :, s, b, :],
                                 mT[24 * s:24 * s + 24, b, :]).then_inc(s_md[b], 16)

            def rows_load(gr_, N):
                alone(sp, s_xu, (N - 2) * GB)
                sp.dma_start(yg[gr_.ring][:, :, :], y_dram[tokens(gr_)].rearrange("(b s) d -> s b d", s=S)
                             ).then_inc(s_yg[gr_.ring], 16)

            def step(c, A0, A1, A2, A3, B, C, D, D2):
                s1, l, a, a1, a0, d = c.at(1), c.at(2), c.at(3), c.at(4), c.at(5), c.at(-1)
                if C:
                    max_rows(c, 1)
                if A3:
                    j, N = l.ring, l.count(NG)
                    alone(sp, s_st, (N - 3) * 8 + 8)
                    alone(sp, s_qw[j], (l.laps(NG) + 1) * 32)
                    for n, runs in RUNS:
                        t = PRODUCTS[n][0]
                        sp.dma_start(Qst[j][2 * DK * n:2 * DK * (n + runs)].rearrange("r p s b q -> r (p s b q)"),
                                     q_dram[j, t:t + 1].to_broadcast([runs, 2 * DK, NP * 2 * W])).then_inc(s_qr[j], 16)
                    alone(sp, s_kw[j], (l.laps(NG) + 1) * 16)
                    for n, runs in RUNS:
                        t = PRODUCTS[n][1]
                        sp.dma_start(Kst[j][2 * DK * n:2 * DK * (n + runs)].rearrange("r p b k -> r (p b k)"),
                                     k_dram[j, t:t + runs].rearrange("t r n -> (t r) n")).then_inc(s_kr[j], 16)
                    if l.layer == 1:
                        src = m_dram[:, cols(l)].rearrange("r (o n) -> r o n", o=1).to_broadcast([3, NP, W])
                        sp.dma_start(Kst[j][RP:RS].rearrange("r p b k -> r p (b k)"), src).then_inc(s_kr[j], 16)
                if A1:
                    alone(sp, s_cTp, a1.count(NG) - 2)
                    sp.dma_start(cg[a1.ring][:, :, :], ctx_1024[span(a1)].rearrange("b s d -> s b d")).then_inc(s_c[a1.ring], 16)
                if B:
                    max_rows(s1, 0)
                if A2:
                    j, N = a.ring, a.count(NG)
                    if isinstance(a.g, int) and a.g == 0:
                        sp.wait_ge(s_dz, 48)
                    alone(sp, s_s, (N - 3) * 8 + 8)
                    alone(sp, s_qs, N + 1)
                    for s in range(2):
                        sp.dma_start(q_dram[j][:, s * DK:(s + 1) * DK, :].rearrange("t d (p s n) -> s (d p) t n", p=NP, s=2)[s],
                                     qp[64 * s:64 * s + 64, :, :]).then_inc(s_qw[j], 16)
                    alone(sp, s_ks, N + 1)
                    sp.dma_start(k_dram[j].rearrange("t r (p n) -> (r p) t n", p=NP), kp[:, :, :]).then_inc(s_kw[j], 16)
                if D:
                    alone(sp, s_xn2, d.count(NG) + 1)
                    sp.dma_start(xn2_dram[tokens(d)].rearrange("(b s) d -> s b d", s=S), xn2g[:, :, :]).then_inc(s_x2k, 16)
                if A0 and a0.layer == 1:
                    rows_load(a0, a0.g)
                if isinstance(c.g, int) and c.g in EX_STEPS:
                    expert_load(c.layer, EX_STEPS.index(c.g))

            for L in range(2):
                if L == 1:
                    sp.wait_ge(s_mst, 5)
                    sp.dma_start(m_dram.rearrange("r (b k) -> b r k", b=NB), mparts[:, :, :]).then_inc(s_mpw, 16)
                    sp.wait_ge(s_mpw, 16)
                    for u in range(2):
                        sp.wait_ge(s_ysw[u], len(range(u, NT, 2)) * 16)
                    sp.wait_ge(s_sg, NT)
                attention(sp, L, step)
            for u in range(2):
                sp.wait_ge(s_ysw[u], 2 * len(range(u, NT, 2)) * 16)
            for g in range(NG):
                rows_load(Group(2, g // 3, g % 3), NG + g)
            sp.wait_ge(s_out, NG * 16)

        def k_loads(gr_):
            plain, masked = len(RUNS) * 16, (len(RUNS) + 1) * 16
            if gr_.layer == 0:
                return (gr_.turn + 1) * plain
            return len(range(gr_.ring, NG, 3)) * plain + (gr_.turn + 1) * masked

        @block.gpsimd
        def _(pool):
            pool.memset(ident[:, :], 0.0).then_inc(s_id, 1)
            pool.memset(ones_m[:, :, :], 0.0).then_inc(s_id, 1)
            pool.memset(half[:, :], -0.5).then_inc(s_cst, 1)
            pool.wait_ge(s_id, 2)
            pool.affine_select(out=ident[:, :], in_=ident[:, :], compare_op=ALU.not_equal, fill=1.0, base=0,
                               pattern=[[-1, 128]], channel_multiplier=1).then_inc(s_id, 1)
            pool.memset(Qst[0][:, :, :, :, :].rearrange("r p s b q -> r (p s b q)").bitcast(f32), 0.0).then_inc(s_qz, 1)
            for k in range(4):
                pool.memset(ones_m[:, k, 8 * k:8 * k + 8], 1.0).then_inc(s_cst, 1)
            pool.wait_ge(s_id, 3)
            pool.tensor_copy(identb[:, :], ident[:, :]).then_inc(s_cst, 1)
            for j in range(3):
                pool.memset(Vm[j][:, :, :, :], 0.0).then_inc(s_cst, 1)

            def split(src, res, parts, steps, base, done):
                pool.tensor_copy(parts(0), src).then_inc(steps, 1)
                pool.wait_ge(steps, base + 1)
                pool.tensor_tensor(res, src, parts(0), ALU.subtract).then_inc(steps, 1)
                alone(pool, steps, base + 2)
                pool.tensor_copy(parts(1), res).then_inc(steps, 1)
                pool.wait_ge(steps, base + 3)
                pool.tensor_tensor(parts(2), res, parts(1), ALU.subtract).then_inc(done, 1)

            def first_rest(src, res, parts, rounded, rest, N):
                pool.wait_ge(rounded, 2 * N + 1)
                pool.tensor_tensor(res, src, parts[:, 0, :], ALU.subtract).then_inc(rest, 1)

            def last_part(res, parts, rounded, done, N):
                pool.wait_ge(rounded, 2 * N + 2)
                pool.tensor_tensor(parts[:, 2, :], res, parts[:, 1, :], ALU.subtract).then_inc(done, 1)

            def max_split(gr_, b):
                n = gr_.count(NG) * GB + b
                pool.wait_ge(s_max, gr_.count(NG) * 8 + 4 * b + 4)
                alone(pool, s_mTp, n - 1)
                split(negm[:, b, :, :], nres[:, b, :, :], lambda t: negp[:, b, :, t, :], s_ni, n * 3, s_ns)

            def rstd(stats, mv, ve, rs, s_stat, s_v, s_pw, N):
                alone(pool, s_stat, N + 1)
                pool.tensor_scalar_add(ve[:, :], mv[:, :, 1], EPS).then_inc(s_v, 1)
                pool.wait_ge(s_v, N + 1)
                pool.tensor_tensor(rs[:, :], ve[:, :], half[:, :], ALU.pow).then_inc(s_pw, 1)

            def step(c, A0, A1, A2, A3, B, C, D, D2):
                s, l, a, d, a1 = c.at(1), c.at(2), c.at(3), c.at(-1), c.at(4)
                if C:
                    max_split(c, 1)
                if A3:
                    pool.wait_ge(s_xn, l.count(NG) + 1)
                    pool.tensor_tensor(x_sb[:, span(l), :], x_sb[:, span(l), :],
                                       bor[:, l.layer:l.layer + 1, :].to_broadcast([128, GB, DM]), ALU.add).then_inc(s_xb, 1)
                N = a.count(NG)
                if A2:
                    first_rest(Qf[:, :], qres[:, :], qp, s_qi, s_qt, N)
                if A1:
                    rstd(st1, mv1, ve1, rs1, s_ag1, s_v1, s_pw1, a1.count(NG))
                if B:
                    max_split(s, 0)
                if A2:
                    last_part(qres[:, :], qp, s_qi, s_qs, N)
                if D:
                    rstd(st2, mv2, ve2, rs2, s_ag2, s_v2, s_pw2, d.count(NG))
                if A2:
                    first_rest(Kf[:, :], kres[:, :], kp, s_ki, s_kt, N)
                    last_part(kres[:, :], kp, s_ki, s_ks, N)

            pool.iota(e_int[:, :, :], pattern=[[0, NB], [1, E]], base=0, channel_multiplier=0).then_inc(s_ri, 1)
            pool.iota(t_int[:, :, :], pattern=[[1, NT], [0, E]], base=0, channel_multiplier=0).then_inc(s_ri, 1)
            pool.memset(tri[:, :], 1.0).then_inc(s_ri, 1)
            pool.wait_ge(s_ri, 3)
            pool.affine_select(out=tri[:, :], in_=tri[:, :], compare_op=ALU.is_gt, fill=0.0, base=0,
                               pattern=[[1, 128]], channel_multiplier=-1).then_inc(s_ri, 1)
            pool.memset(ones[:, :], 1.0).then_inc(s_ri, 1)
            pool.iota(count_i[:, :], pattern=[[1, 128]], base=0, channel_multiplier=0).then_inc(s_ri, 1)
            pool.iota(q1_i[:, :], pattern=[[0, 1]], base=1, channel_multiplier=1).then_inc(s_ri, 1)
            pool.iota(spare_i[:, :], pattern=[[T, NT]], base=NB * S + 1, channel_multiplier=1).then_inc(s_ri, 1)
            pool.wait_ge(s_ri, 8)
            for j in range(3):
                pool.memset(Kst[j][96:128, :, :, :].rearrange("r p b k -> r (p b k)").bitcast(f32), TWO_ONES).then_inc(s_kz, 1)
                if j > 0:
                    pool.memset(Qst[j][96:128, :, :, :, :].rearrange("r p s b q -> r (p s b q)").bitcast(f32), 0.0).then_inc(s_kz, 1)
            pool.wait_ge(s_kz, 5)

            pool.wait_ge(s_wo_s, 5)
            def read_tile(t):
                alone(pool, s_ixr, t.count(NT) + 1)
                pool.indirect_dma_start(
                    out=xs[t.v][:, :], out_offset=None, in_=xn2_dram[:, :],
                    in_offset=bass.IndirectOffsetOnAxis(ap=ixr[t.v][:, :], axis=0)).then_inc(s_xl[t.v], 16)

            def slot_step(t, T2, F1, F2):
                if isinstance(t.i, int) and t.i == -2:
                    for k in range(2, 4):
                        read_tile(t.at(k))
                if not isinstance(t.i, int) or t.i + 4 < NT:
                    read_tile(t.at(4))
                if F2:
                    alone(pool, s_ixw, t.count(NT) + 1)
                    alone(pool, s_fy, t.count(NT) + 1)
                    pool.indirect_dma_start(
                        out=y_dram[:, :], out_offset=bass.IndirectOffsetOnAxis(ap=ixw[t.u][:, :], axis=0),
                        in_=ys[t.u][:, :], in_offset=None).then_inc(s_ysw[t.u], 16)

            for L in range(2):
                attention(pool, L, step)
                pool.wait_ge(s_x2k, NG * (L + 1) * 16)
                experts(pool, L, slot_step)

        @block.scalar
        def _(act):
            for L in range(2):
                for n in (0, 1):
                    act.dma_start(bnat[2 * L + n:2 * L + n + 1, :], row(bqkvo[L][n])).then_inc(s_bn, 16)
                act.dma_start(bvr[:, L, :], bqkvo[L][2].partition_broadcast(128)).then_inc(s_b, 16)
                act.dma_start(bor[:, L, :], bqkvo[L][3].partition_broadcast(128)).then_inc(s_b, 16)
                act.dma_start(gw[:, L, :], gates[L][0]).then_inc(s_b, 16)
                act.dma_start(gb[:, L, :], gates[L][1].partition_broadcast(128)).then_inc(s_b, 16)
            act.dma_start(gr[:, 0:2], g_xattn.partition_broadcast(128)).then_inc(s_b, 16)
            act.dma_start(gr[:, 2:4], g_ffn.partition_broadcast(128)).then_inc(s_b, 16)
            act.wait_ge(s_b, 10 * 16)
            act.activation(tg[:, :], gr[:, :], ACT.Tanh).then_inc(s_tg, 1)

            def first_part(gr_, src, parts, ready, written, each, rounded):
                N = gr_.count(NG)
                act.wait_ge(ready, N + 1)
                if not (isinstance(N, int) and N == 0):
                    before = Group(0, (NG - 1) // 3, (NG - 1) % 3) if isinstance(gr_.g, int) and gr_.g == 0 else gr_.at(-1)
                    act.wait_ge(written[before.ring], (before.laps(NG) + 1) * each)
                act.activation(parts[:, 0, :], src[:, :], ACT.Copy).then_inc(rounded, 1)

            def second_part(gr_, res, parts, rest, rounded):
                act.wait_ge(rest, gr_.count(NG) + 1)
                act.activation(parts[:, 1, :], res[:, :], ACT.Copy).then_inc(rounded, 1)

            def keep_max(gr_, b):
                n = gr_.count(NG) * GB + b
                act.wait_ge(s_mTp, n + 1)
                wait(act, s_md[b], (gr_.count(NG)) * 32)
                act.activation(mT[:, b, :], M[b][0:48, 0:64].bitcast(bf16), ACT.Copy).then_inc(s_mTe, 1)

            def step(c, A0, A1, A2, A3, B, C, D, D2):
                s, a, d = c.at(1), c.at(3), c.at(-1)
                for n in range(8):
                    if C:
                        m = c.count(NG) * 8 + n
                        act.wait_ge(s_st, m + 1)
                        wait(act, s_pv, m - 3)
                        act.activation(P[:, n % 4, :], ST[n % 2][:, :], ACT.Exp).then_inc(s_exp, 1)
                    if n == 0 and A2:
                        act.wait_ge(s_xT, a.count(NG) + 1)
                        wait(act, s_q, a.count(NG))
                        act.activation(xT[:, :], M[0][:, 0:W], ACT.Copy).then_inc(s_xTe, 1)
                    if n == 1:
                        if C:
                            keep_max(c, 1)
                        if A2:
                            act.wait_ge(s_q, a.count(NG) + 1)
                            wait(act, s_qs, a.count(NG))
                            act.activation(Qf[:, :], M[0][:, 0:W], ACT.Identity, scale=SCALE,
                                           bias=bcol[:, 2 * a.layer:2 * a.layer + 1]).then_inc(s_qf, 1)
                            first_part(a, Qf, qp, s_qf, s_qw, 32, s_qi)
                    if n == 2 and A2:
                        act.wait_ge(s_cTp, a.count(NG) + 1)
                        wait(act, s_v, a.count(NG) - 2)
                        act.activation(cgT[a.ring][:, :], M[1][:, 0:W], ACT.Copy).then_inc(s_cTe, 1)
                    if n == 3 and A2:
                        second_part(a, qres, qp, s_qt, s_qi)
                        if a.layer == 0:
                            act.wait_ge(s_k, a.count(NG) + 1)
                            wait(act, s_ks, a.count(NG))
                            act.activation(Kf[:, :], M[0][:, 0:W], ACT.Identity, bias=bcol[:, 1:2]).then_inc(s_kf, 1)
                    if n == 4 and A2:
                        first_part(a, Kf, kp, s_kf, s_kw, 16, s_ki)
                    if n == 5 and B:
                        keep_max(s, 0)
                    if n == 6 and A2:
                        second_part(a, kres, kp, s_kt, s_ki)
                    if n == 7 and D:
                        act.wait_ge(s_x2T, d.count(NG) + 1)
                        wait(act, s_lg, d.count(NG))
                        act.activation(x2T[:, :], M[1][:, 0:W], ACT.Copy).then_inc(s_x2Te, 1)

            def slot_step(t, T2, F1, F2):
                if T2:
                    t2 = t.at(2)
                    n = t2.count(NT)
                    act.wait_ge(s_ft, n + 1)
                    wait(act, s_f1, n - 1)
                    act.activation(xsT[t2.u][:, :], M[t2.u][:, 0:T], ACT.Copy).then_inc(s_fte, 1)
                if F1:
                    t1 = t.at(1)
                    n = t1.count(NT)
                    act.wait_ge(s_f1, n + 1)
                    wait(act, s_f2, n - 1)
                    for c in range(FC):
                        last = act.activation(hT[t1.u][:, c, :], SB[t1.u][:, c * T:(c + 1) * T], ACT.Gelu,
                                              bias=stg[t1.v][:, B1 + c:B1 + c + 1])
                    last.then_inc(s_fg, 1)

            act.wait_ge(s_wo_s, 5)
            for L in range(2):
                attention(act, L, step)
                act.wait_ge(s_rt, L * 16 + 2)
                act.activation(expd[:, :, :], below[:, :, :], ACT.Exp).then_inc(s_rx, 1)
                act.wait_ge(s_oh, L + 1)
                act.activation(token_parts[:, :, 1, :], at_tile[:, :, :], ACT.Copy, scale=q1[:, :]).then_inc(s_tp, 1)
                experts(act, L, slot_step)
            for g in range(NG):
                act.wait_ge(s_xu, (NG + g + 1) * GB)
                act.dma_start(out[g * GB:g * GB + GB].rearrange("b s d -> s b d"),
                              x_sb[:, g * GB:g * GB + GB, :]).then_inc(s_out, 16)

        @block.vector
        def _(dve):
            for L in range(2):
                for n in range(4):
                    m = 4 * L + n
                    dve.wait_ge(s_wtp, m + 1)
                    src = M[m % 2][:, 0:128]
                    if n < 2:
                        for s in range(2):
                            last = dve.tensor_copy(wT[:, m, :].rearrange("p (s d k e) -> p s d k e", s=2, d=DK, k=4)[:, s],
                                                   src.rearrange("p (e s k d) -> p s d k e", s=2, d=DK, k=4)[:, s])
                        last.then_inc(s_wte, 1)
                    else:
                        dve.tensor_copy(wT[:, m, :], src).then_inc(s_wte, 1)
            dve.wait_ge(s_tg, 1)
            dve.wait_ge(s_wte, 8)
            dve.wait_ge(s_bn, 4 * 16)
            for s in range(2):
                last = dve.tensor_copy(bperm[:, :].rearrange("p (s d k e) -> p s d k e", s=2, d=DK, k=4)[:, s],
                                       bnat[:, :].rearrange("p (e s k d) -> p s d k e", s=2, d=DK, k=4)[:, s])
            last.then_inc(s_bp, 1)
            dve.wait_ge(s_bT, 1)
            dve.tensor_copy(bcol[:, :], M[0][:, 0:4]).then_inc(s_bc, 1)
            dve.wait_ge(s_bc, 1)
            for L in range(2):
                dve.tensor_scalar(wT[:, 4 * L + 3, :], wT[:, 4 * L + 3, :], tg[:, L:L + 1], None, ALU.mult).then_inc(s_wo_s, 1)
                dve.tensor_scalar(bor[:, L, :], bor[:, L, :], tg[:, L:L + 1], None, ALU.mult).then_inc(s_wo_s, 1)
            dve.tensor_scalar(bcol[:, :].rearrange("p (l n) -> p l n", n=2)[:, :, 0],
                              bcol[:, :].rearrange("p (l n) -> p l n", n=2)[:, :, 0], SCALE, None, ALU.mult).then_inc(s_wo_s, 1)

            def standing_rows():
                for j in range(3):
                    if j == 0:
                        dve.wait_ge(s_qz, 1)
                    dve.wait_ge(s_kz, 2 * j + 1)
                    dve.memset(Kst[j][96:96 + 3, :, :, :].rearrange("r p b k -> r (p b k)").bitcast(f32), 0.0).then_inc(s_rows, 1)
                    dve.memset(Qst[j][96:96 + 3, :, :, :, :].rearrange("r p s b q -> r (p s b q)").bitcast(f32), TWO_ONES).then_inc(s_rows, 1)

            def norm(gr_, b):
                n = gr_.count(NG) * GB + b
                dve.wait_ge(s_pv, gr_.count(NG) * 8 + 4 * b + 4)
                dve.reciprocal(R[:, b, :], PV[b][:, 128:256]).then_inc(s_rec, 1)
                dve.wait_ge(s_rec, n + 1)
                wait(dve, s_wo, n - 1)
                dve.tensor_tensor(cT[:, b, :], PV[b][:, 0:128], R[:, b, :], ALU.mult).then_inc(s_nrm, 1)

            def x_add(gr_, b):
                n = gr_.count(NG) * GB + b
                dve.wait_ge(s_wo, n + 1)
                dve.wait_ge(s_xb, gr_.count(NG) + 1)
                at = one(gr_.g * GB + b)
                dve.tensor_tensor(x_sb[:, at, :], x_sb[:, at, :],
                                  PV[b][:, 256:384].rearrange("p (o n) -> p o n", o=1), ALU.add).then_inc(s_xa, 1)

            def x_update(gr_, layer, N, j):
                dve.wait_ge(s_yg[j], (gr_.turn + 1 + (layer - 1) * len(range(j, NG, 3))) * 16)
                for b in range(GB):
                    at = one(gr_.g * GB + b)
                    dve.scalar_tensor_tensor(x_sb[:, at, :], yg[j][:, b:b + 1, :], gate[:, at], x_sb[:, at, :],
                                             ALU.mult, ALU.add).then_inc(s_xu, 1)

            def stats(gr_, st, mv, s_stat, s_agg, s_used, N):
                alone(dve, s_used, N)
                for b in range(GB):
                    dve.bn_stats(st[:, b, :], x_sb[:, one(gr_.g * GB + b), :].rearrange("p o n -> p (o n)")).then_inc(s_stat, 1)
                for b in range(GB):
                    alone(dve, s_stat, N * GB + b + 1)
                    last = dve.bn_aggr(mv[:, b, :], st[:, b, :])
                last.then_inc(s_agg, 1)

            def normed(gr_, mv, rs, to, done):
                for b in range(GB):
                    last = dve.tensor_scalar(to(b), x_sb[:, one(gr_.g * GB + b), :], mv[:, b, 0:1], rs[:, b:b + 1],
                                             ALU.subtract, ALU.mult)
                last.then_inc(done, 1)

            def step(c, A0, A1, A2, A3, B, C, D, D2):
                s, l, a, d, e, a1 = c.at(1), c.at(2), c.at(3), c.at(-1), c.at(-2), c.at(4)
                for n in range(8):
                    if B:
                        m = s.count(NG) * 8 + n
                        b, k = n // 4, n % 4
                        dve.wait_ge(s_s, m + 1)
                        if k == 0:
                            wait(dve, s_ns, s.count(NG) * GB + b - 1)
                        dve.tensor_reduce(negm[:, b, :, 2 * k:2 * k + 2].rearrange("q s e -> q e s"),
                                          SB[n % 2][:, :].rearrange("q (e s k) -> q e s k", e=2, s=2), AX, ALU.max,
                                          negate=True).then_inc(s_max, 1)
                    if n == 0:
                        if D2:
                            dve.wait_ge(s_lg, e.count(NG) + 1)
                            dve.tensor_tensor(logits[:, span(e), :], M[1][:, 0:GB * E].rearrange("p (b e) -> p b e", e=E),
                                              gb[:, e.layer:e.layer + 1, :].to_broadcast([128, GB, E]), ALU.add).then_inc(s_lga, 1)
                        if D:
                            x_add(d, 0)
                    if n == 1 and D:
                        norm(d, 1)
                    if n == 2 and A1:
                        if a1.layer == 0:
                            dve.wait_ge(s_x, 16 * NXD)
                        else:
                            x_update(a1, 1, a1.g, a1.ring)
                            alone(dve, s_xu, (a1.g + 1) * GB)
                        stats(a1, st1, mv1, s_st1, s_ag1, s_xn, a1.count(NG))
                    if n == 4 and D:
                        x_add(d, 1)
                    if n == 4 and A2 and a.layer == 1:
                        dve.wait_ge(s_k, a.count(NG) + 1)
                        wait(dve, s_ks, a.count(NG))
                        dve.scalar_tensor_tensor(Kf[:, :], M[0][:, 0:W], bcol[:, 3:4], maskrep[:, cols(a)],
                                                 ALU.add, ALU.mult).then_inc(s_kf, 1)
                    if n == 4 and D:
                        alone(dve, s_xa, (d.count(NG) + 1) * GB)
                        stats(d, st2, mv2, s_st2, s_ag2, s_xn2, d.count(NG))
                    if n == 5 and A3:
                        dve.wait_ge(s_v, l.count(NG) + 1)
                        wait(dve, s_pv, (l.count(NG) - 3) * 8 + 8)
                        for k in range(4):
                            last = dve.tensor_tensor(
                                Vm[l.ring][:, :, k, :].rearrange("p b (g c) -> p b g c", c=32)[:, :, :, 8 * k:8 * k + 8],
                                M[1][:, 0:W].rearrange("p (b g k d) -> p k b g d", b=GB, k=4, d=DK)[:, k],
                                bvr[:, l.layer:l.layer + 1, :].to_broadcast([128, GB, DM]).rearrange(
                                    "p b (g k d) -> p k b g d", k=4, d=DK)[:, k], ALU.add)
                        last.then_inc(s_vm, 1)
                    if n == 5 and C:
                        norm(c, 0)
                    if n == 5 and D:
                        dve.wait_ge(s_pw2, d.count(NG) + 1)
                        wait(dve, s_x2T, d.count(NG))
                        wait(dve, s_x2k, d.count(NG) * 16)
                        normed(d, mv2, rs2, lambda b: xn2g[:, b:b + 1, :], s_xn2)
                    if n == 6 and A1:
                        dve.wait_ge(s_pw1, a1.count(NG) + 1)
                        wait(dve, s_xT, a1.count(NG))
                        normed(a1, mv1, rs1, lambda b: xn[:, b:b + 1, :], s_xn)
                    if n == 7 and isinstance(c.g, int) and c.g == -3 and c.layer == 0:
                        standing_rows()

            def mask_parts():
                dve.wait_ge(s_mk, 32)
                dve.tensor_scalar(mval[:, :], mask8[:, :], FILL, -FILL, ALU.mult, ALU.add).then_inc(s_mst, 1)
                dve.wait_ge(s_mst, 1)
                dve.tensor_copy(mparts[:, 0, :], mval[:, :]).then_inc(s_mst, 1)
                dve.wait_ge(s_mst, 2)
                dve.tensor_tensor(mres[:, :], mval[:, :], mparts[:, 0, :], ALU.subtract).then_inc(s_mst, 1)
                dve.wait_ge(s_mst, 3)
                dve.tensor_copy(mparts[:, 1, :], mres[:, :]).then_inc(s_mst, 1)
                dve.wait_ge(s_mst, 4)
                dve.tensor_tensor(mparts[:, 2, :], mres[:, :], mparts[:, 1, :], ALU.subtract).then_inc(s_mst, 1)

            def route(L):
                R0 = L * 16
                n = [R0]

                def then(ins):
                    n[0] += 1
                    ins.then_inc(s_rt, 1)
                    dve.wait_ge(s_rt, n[0])

                dve.wait_ge(s_b1s, L + 1)
                if L == 1:
                    dve.wait_ge(s_sg, NT)
                dve.tensor_copy(ex[:, :, B1:B2], b1T[:, L, :].rearrange("p (e c) -> p e c", c=FC)).then_inc(s_b1s, 1)
                dve.wait_ge(s_lga, NG * (L + 1))
                every = lambda a: a.rearrange("p (b o) -> p b o", o=1).to_broadcast([128, NB, E])
                by_e = lambda a: a.rearrange("p (e o) -> p e o", o=1).to_broadcast([128, E, NB])
                then(dve.tensor_reduce(top[:, :], logits[:, :, :], AX, ALU.max))
                then(dve.tensor_tensor(below[:, :, :], logits[:, :, :], every(top[:, :]), ALU.subtract))
                then(dve.tensor_scalar(notop[:, :, :], below[:, :, :], 0.0, float(E), ALU.is_lt, ALU.mult))
                then(dve.tensor_tensor(notop[:, :, :], notop[:, :, :], e_row[:, :, :], ALU.add))
                then(dve.tensor_reduce(first[:, :], notop[:, :, :], AX, ALU.min))
                then(dve.tensor_tensor(chosen[:, :, :], e_row[:, :, :], every(first[:, :]), ALU.is_equal))
                dve.wait_ge(s_rc, L + 1)
                then(dve.tensor_copy(tot[:, :, :], PV[0][:, 256:512].rearrange("p (b e) -> p e b", e=E)))
                then(dve.tensor_reduce(cnt[:, :], tot[:, :, :], AX, ALU.add))
                dve.tensor_scalar(cnt_i[:, 0, :], cnt[:, :], float(T - 1), None, ALU.add).then_inc(s_set, 1)
                dve.wait_ge(s_set, L * 5 + 1)
                dve.tensor_scalar(cnt_i[:, 1, :], cnt_i[:, 0, :], T.bit_length() - 1, None, ALU.arith_shift_right).then_inc(s_set, 1)
                dve.wait_ge(s_set, L * 5 + 2)
                dve.tensor_copy(tiles[:, :], cnt_i[:, 1, :]).then_inc(s_set, 1)
                dve.wait_ge(s_set, L * 5 + 3)
                dve.tensor_tensor_scan(cumt[:, :], ones[:, 0:E], tiles[:, :], 0.0, ALU.mult, ALU.add).then_inc(s_set, 1)
                dve.tensor_tensor_scan(cumn[:, :], ones[:, 0:E], cnt[:, :], 0.0, ALU.mult, ALU.add).then_inc(s_set, 1)
                dve.wait_ge(s_set, L * 5 + 5)
                then(dve.tensor_tensor(off[:, :], cumt[:, :], tiles[:, :], ALU.subtract))
                then(dve.scalar_tensor_tensor(off[:, :], off[:, :], float(T), cumn[:, :], ALU.mult, ALU.subtract))
                then(dve.tensor_tensor(off[:, :], off[:, :], cnt[:, :], ALU.add))
                then(dve.tensor_tensor_scan(cum[:, :, :].rearrange("p e b -> p (e b)"), ones[:, :],
                                            tot[:, :, :].rearrange("p e b -> p (e b)"), 0.0, ALU.mult, ALU.add))
                then(dve.tensor_tensor(pos[:, :, :], cum[:, :, :], tot[:, :, :], ALU.subtract))
                then(dve.tensor_tensor(pos[:, :, :], pos[:, :, :], by_e(off[:, :]), ALU.add))
                then(dve.tensor_tensor(pos[:, :, :], PV[0][:, 0:256].rearrange("p (b e) -> p e b", e=E), pos[:, :, :], ALU.add))
                then(dve.tensor_tensor(pos[:, :, :], pos[:, :, :], chosen[:, :, :].rearrange("p b e -> p e b"), ALU.mult))
                assert n[0] == R0 + 16
                dve.tensor_reduce(slot_f[:, :], pos[:, :, :].rearrange("p e b -> p b e"), AX, ALU.add).then_inc(s_sl, 1)
                dve.tensor_tensor(past[:, :, :], t_row[:, :, :],
                                  cumt[0:1, :].rearrange("p (o e) -> p o e", o=1).to_broadcast([1, NT, E]), ALU.is_ge).then_inc(s_sl, 1)
                dve.wait_ge(s_sl, L * 4 + 2)
                dve.tensor_copy(slot_i[:, :], slot_f[:, :]).then_inc(s_sl, 1)
                dve.tensor_reduce(texp_f[:, :], past[:, :, :], AX, ALU.add).then_inc(s_sl, 1)
                dve.wait_ge(s_sl, L * 4 + 4)
                if L == 1:
                    dve.wait_ge(s_sg, NT)
                dve.tensor_scalar(texp[:, :], texp_f[:, :], float(E - 1), None, ALU.min).then_inc(s_slot, 1)
                I0 = L * 9
                dve.tensor_scalar(within_i[:, :], slot_i[:, :], T - 1, None, ALU.bitwise_and).then_inc(s_inv, 1)
                dve.tensor_scalar(tile_i[:, :], slot_i[:, :], T.bit_length() - 1, None, ALU.arith_shift_right).then_inc(s_inv, 1)
                dve.wait_ge(s_inv, I0 + 2)
                dve.tensor_copy(tile[:, :], tile_i[:, :]).then_inc(s_inv, 1)
                dve.tensor_copy(within[:, :], within_i[:, :]).then_inc(s_inv, 1)
                dve.wait_ge(s_inv, I0 + 4)
                spread = lambda a, n: a.rearrange("p (b o) -> p b o", o=1).to_broadcast([128, NB, n])
                counting = lambda n: count_b[:, 0:n].rearrange("p (o n) -> p o n", o=1).to_broadcast([128, NB, n])
                dve.tensor_tensor(at_tile[:, :, :], counting(NT), spread(tile[:, :], NT), ALU.is_equal).then_inc(s_oh, 1)
                dve.wait_ge(s_slot, L + 1)
                dve.wait_ge(s_oh, L + 1)
                dve.tensor_tensor(token_parts[:, :, 0, :], at_tile[:, :, :], spread(count_b[:, 0:NB], NT), ALU.mult).then_inc(s_tp, 1)
                for b in range(NB):
                    dve.tensor_scalar(at_slot[:, b, :], count_b[:, :], within[:, b:b + 1], None, ALU.is_equal).then_inc(s_as, 1)
                dve.wait_ge(s_id1, L + 1)
                dve.tensor_copy(row1[:, :], M[0][:, NT:2 * NT]).then_inc(s_inv, 1)
                dve.wait_ge(s_inv, I0 + 5)
                dve.scalar_tensor_tensor(id1[:, :], M[0][:, 0:NT], float(S), row1[:, :], ALU.mult, ALU.add).then_inc(s_inv, 1)
                dve.wait_ge(s_inv, I0 + 6)
                dve.tensor_scalar(idx[:, :, 0], id1[:, :], 1.0, -1.0, ALU.max, ALU.add).then_inc(s_inv, 1)
                dve.tensor_scalar(empty[:, :], id1[:, :], 0.0, None, ALU.is_equal).then_inc(s_inv, 1)
                dve.wait_ge(s_inv, I0 + 8)
                dve.tensor_tensor(empty[:, :], empty[:, :], spare[:, :], ALU.mult).then_inc(s_inv, 1)
                dve.wait_ge(s_inv, I0 + 9)
                dve.scalar_tensor_tensor(idx[:, :, 1], id1[:, :], -1.0, empty[:, :], ALU.add, ALU.add).then_inc(s_tok, 1)
                dve.wait_ge(s_tok, L + 1)

            def gates_and_mask(L):
                dve.wait_ge(s_rx, L + 1)
                dve.tensor_reduce(gsum[:, :], expd[:, :, :], AX, ALU.add).then_inc(s_gt, 1)
                dve.wait_ge(s_gt, L * 3 + 1)
                dve.reciprocal(gate[:, :], gsum[:, :]).then_inc(s_gt, 1)
                dve.wait_ge(s_gt, L * 3 + 2)
                dve.tensor_scalar(gate[:, :], gate[:, :], tg[:, 2 + L:3 + L], None, ALU.mult).then_inc(s_gt, 1)
                dve.wait_ge(s_gt, L * 3 + 3)
                if L == 0:
                    mask_parts()

            def read_index(t):
                wait(dve, s_ft, t.count(NT) - 3)
                dve.tensor_copy(ixr[t.v][:, :], idx[:, one(t.i), 0]).then_inc(s_ixr, 1)

            def slot_step(t, T2, F1, F2):
                if isinstance(t.i, int) and t.i == -2:
                    for k in range(2, 4):
                        read_index(t.at(k))
                if not isinstance(t.i, int) or t.i + 4 < NT:
                    read_index(t.at(4))
                if isinstance(t.i, int) and t.i == -2:
                    gates_and_mask(t.layer)
                if T2:
                    t2 = t.at(2)
                    e = dve.value_load(texp[0:1, one(t2.i)], min_val=0, max_val=E - 1)
                    wait(dve, s_fy, t2.count(NT) - 3)
                    dve.tensor_copy(stg[t2.v][:, :], ex[:, bass.ds(e, 1), :].rearrange("p o n -> p (o n)")).then_inc(s_sg, 1)
                if F2:
                    n = t.count(NT)
                    dve.wait_ge(s_f2, n + 1)
                    wait(dve, s_ysw[t.u], t.laps2(NT) * 16)
                    dve.tensor_copy(ixw[t.u][:, :], idx[:, one(t.i), 1]).then_inc(s_ixw, 1)
                    dve.tensor_tensor(ys[t.u][:, :], ST[t.u][:, 0:DM], stg[t.v][:, B2:W2], ALU.add).then_inc(s_fy, 1)

            dve.wait_ge(s_ri, 2)
            dve.tensor_copy(e_row[:, :, :], e_int[:, :, :]).then_inc(s_rk, 1)
            dve.tensor_copy(t_row[:, :, :], t_int[:, :, :]).then_inc(s_rk, 1)
            dve.wait_ge(s_ri, 8)
            dve.tensor_copy(count_b[:, :], count_i[:, :]).then_inc(s_rk, 1)
            dve.tensor_copy(tri_b[:, :], tri[:, :]).then_inc(s_rk, 1)
            dve.tensor_copy(ones_b[:, :], ones[:, 0:128]).then_inc(s_rk, 1)
            dve.tensor_copy(q1[:, :], q1_i[:, :]).then_inc(s_rk, 1)
            dve.tensor_copy(spare[:, :], spare_i[:, :]).then_inc(s_rk, 1)
            dve.wait_ge(s_b1t, 1)
            dve.tensor_copy(b1T[:, :, :], M[1][:, 0:2 * E * FC].rearrange("p (l n) -> p l n", l=2)).then_inc(s_b1s, 1)
            dve.wait_ge(s_rk, 7)

            for L in range(2):
                attention(dve, L, step)
                route(L)
                dve.wait_ge(s_ex, (L + 1) * NEX * 16)
                dve.wait_ge(s_b1s, L + 2)
                experts(dve, L, slot_step)
            for g in range(NG):
                x_update(Group(2, g // 3, g % 3), 2, NG + g, g % 3)

        @block.tensor
        def _(pe):
            pe.wait_ge(s_id, 3)
            for m in range(8):
                if m == 0:
                    pe.wait_ge(s_w, 8 * 16)
                wait(pe, s_wte, m - 1)
                pe.transpose(M[m % 2][:, 0:128], wnat[:, m, :], ident[:, :]).then_inc(s_wtp, 1)
            pe.wait_ge(s_wte, 8)
            pe.wait_ge(s_bp, 1)
            pe.transpose(M[0][:, 0:4], bperm[:, :], ident[0:4, 0:4]).then_inc(s_bT, 1)
            pe.wait_ge(s_wo_s, 5)
            pe.wait_ge(s_cst, 9)
            pe.wait_ge(s_b1l, 32)
            for L in range(2):
                last = pe.transpose(M[1][:, 32 * L:32 * L + 32], b1n[:, L, :], ident[0:32, 0:32])
            last.then_inc(s_b1t, 1)
            pe.wait_ge(s_b1s, 1)

            def scores(gr_, n):
                m, b, k = gr_.count(NG) * 8 + n, n // 4, n % 4
                if n == 0:
                    if isinstance(gr_.g, int) and gr_.count(NG) == 0:
                        pe.wait_ge(s_rows, 6)
                    pe.wait_ge(s_qr[gr_.ring], (gr_.laps(NG) + 1) * len(RUNS) * 16)
                    pe.wait_ge(s_kr[gr_.ring], k_loads(gr_))
                wait(pe, s_max, m - 1)
                q, kk = Qst[gr_.ring], Kst[gr_.ring]
                for e in range(2):
                    for s in range(2):
                        c0 = (2 * e + s) * 128
                        last = pe.matmul(SB[n % 2][:, c0:c0 + 128], q[0:RS, 2 * k + e, s, b, :], kk[0:RS, 2 * k + e, b, :],
                                         start=True, stop=True)
                last.then_inc(s_s, 1)

            def shifted(gr_, n):
                m, b, k = gr_.count(NG) * 8 + n, n // 4, n % 4
                if k == 0:
                    pe.wait_ge(s_md[b], (gr_.count(NG) + 1) * 32)
                wait(pe, s_exp, m - 1)
                for e in range(2):
                    last = pe.matmul(ST[n % 2][:, 256 * e:256 * e + 256], Kst[gr_.ring][0:RT, 2 * k + e, b, :],
                                     Qst[gr_.ring][0:RT, 2 * k + e, :, b, :], start=True, stop=True)
                last.then_inc(s_st, 1)

            def values(gr_, n):
                m, b, k = gr_.count(NG) * 8 + n, n // 4, n % 4
                pe.wait_ge(s_exp, m + 1)
                if n == 0:
                    pe.wait_ge(s_vm, gr_.count(NG) + 1)
                if k == 0:
                    wait(pe, s_xa, gr_.count(NG) * GB + b - 1)
                for g in range(4):
                    pe.matmul(PV[b][32 * g:32 * g + 32, 0:128], Vm[gr_.ring][:, b, k, 32 * g:32 * g + 32],
                              P[:, n % 4, 128 * g:128 * g + 128], start=(k == 0), stop=(k == 3), skip_group_check=True)
                for g in range(4):
                    last = pe.matmul(PV[b][32 * g:32 * g + 32, 128:256], ones_m[:, k, :],
                                     P[:, n % 4, 128 * g:128 * g + 128], start=False, stop=(k == 3), skip_group_check=True)
                last.then_inc(s_pv, 1)

            def out_proj(gr_, b):
                pe.wait_ge(s_nrm, gr_.count(NG) * GB + b + 1)
                pe.matmul(PV[b][:, 256:384], cT[:, b, :], wT[:, 4 * gr_.layer + 3, :], start=True, stop=True).then_inc(s_wo, 1)

            def max_rows(gr_, b):
                alone(pe, s_ns, gr_.count(NG) * GB + b + 1)
                pe.transpose(M[b][0:48, 0:64].bitcast(bf16), negp[:, b, :, :, :].rearrange("q s t p -> q (s t p)"),
                             identb[:, :]).then_inc(s_mTp, 1)

            def step(c, A0, A1, A2, A3, B, C, D, D2):
                s, l, a, d, e = c.at(1), c.at(2), c.at(3), c.at(-1), c.at(-2)
                N = a.count(NG)
                for n in range(8):
                    if C:
                        shifted(c, n)
                    if B:
                        scores(s, n)
                    if n == 4 and A2:
                        pe.wait_ge(s_cTe, N + 1)
                        pe.wait_ge(s_qf, N + 1)
                        pe.matmul(M[0][:, 0:W], wT[:, 4 * a.layer + 1, :], cgT[a.ring][:, :], start=True, stop=True).then_inc(s_k, 1)
                    if n == 5 and B:
                        if A2:
                            pe.wait_ge(s_kf, N + 1)
                        max_rows(s, 0)
                    if n >= 2 and C:
                        values(c, n - 2)
                    if n < 2 and D:
                        values(d, n + 6)
                    if n == 0 and D2:
                        pe.wait_ge(s_x2Te, e.count(NG) + 1)
                        for b in range(GB):
                            last = pe.matmul(M[1][:, E * b:E * b + E], x2T[:, 128 * b:128 * b + 128], gw[:, e.layer, :],
                                             start=True, stop=True)
                        last.then_inc(s_lg, 1)
                    if n == 0 and A2:
                        pe.wait_ge(s_xn, N + 1)
                        wait(pe, s_kf, N)
                        wait(pe, s_mTe, c.count(NG) * GB + 1)
                        for b in range(GB):
                            last = pe.transpose(M[0][:, 128 * b:128 * b + 128], xn[:, b, :], ident[:, :])
                        last.then_inc(s_xT, 1)
                    if n == 1 and C:
                        wait(pe, s_lga, c.count(NG) - 1)
                        wait(pe, s_vm, c.count(NG) + 2 if A3 else NG * (c.layer + 1))
                        max_rows(c, 1)
                    if n == 1 and A2:
                        pe.wait_ge(s_xTe, N + 1)
                        pe.matmul(M[0][:, 0:W], wT[:, 4 * a.layer, :], xT[:, :], start=True, stop=True).then_inc(s_q, 1)
                    if n == 3 and D:
                        out_proj(d, 1)
                    if n == 2:
                        if A2:
                            pe.wait_ge(s_c[a.ring], (a.laps(NG) + 1) * 16)
                            wait(pe, s_vm, N - 1)
                            wait(pe, s_mTe, c.count(NG) * GB + 2)
                            for b in range(GB):
                                last = pe.transpose(M[1][:, 128 * b:128 * b + 128], cg[a.ring][:, b, :], ident[:, :])
                            last.then_inc(s_cTp, 1)
                    if n == 4 and A3:
                        wait(pe, s_mTe, c.count(NG) * GB + 2)
                        pe.wait_ge(s_cTe, N + 1 if A2 else NG * (l.layer + 1))
                        for b in range(GB):
                            last = pe.matmul(M[1][:, 128 * b:128 * b + 128], cgT[l.ring][:, 128 * b:128 * b + 128], wT[:, 4 * l.layer + 2, :],
                                             start=True, stop=True)
                        last.then_inc(s_v, 1)
                    if n == 7:
                        if C:
                            out_proj(c, 0)
                        if D:
                            pe.wait_ge(s_xn2, d.count(NG) + 1)
                            if A3:
                                pe.wait_ge(s_vm, l.count(NG) + 1)
                            elif C:
                                pe.wait_ge(s_mTe, c.count(NG) * GB + 2)
                            for b in range(GB):
                                last = pe.transpose(M[1][:, 128 * b:128 * b + 128], xn2g[:, b, :], ident[:, :])
                            last.then_inc(s_x2T, 1)

            def slot_step(t, T2, F1, F2):
                if T2:
                    t2 = t.at(2)
                    n = t2.count(NT)
                    pe.wait_ge(s_xl[t2.v], (t2.laps4(NT) + 1) * 16)
                    wait(pe, s_fte, n - 1)
                    pe.transpose(M[t2.u][:, 0:T], xs[t2.v][:, :], ident[:, :]).then_inc(s_ft, 1)
                if F1:
                    t1 = t.at(1)
                    n = t1.count(NT)
                    pe.wait_ge(s_fte, n + 1)
                    pe.wait_ge(s_sg, n + 1)
                    wait(pe, s_fg, n - 1)
                    for c in range(FC):
                        last = pe.matmul(SB[t1.u][:, c * T:(c + 1) * T], stg[t1.v][:, c * 128:(c + 1) * 128], xsT[t1.u][:, :],
                                         start=True, stop=True)
                    last.then_inc(s_f1, 1)
                if F2:
                    n = t.count(NT)
                    pe.wait_ge(s_fg, n + 1)
                    wait(pe, s_fy, n - 1)
                    for c in range(FC):
                        last = pe.matmul(ST[t.u][:, 0:DM], hT[t.u][:, c, :],
                                         stg[t.v][:, W2 + c * DM:W2 + (c + 1) * DM],
                                         start=(c == 0), stop=(c == FC - 1))
                    last.then_inc(s_f2, 1)

            for L in range(2):
                attention(pe, L, step)
                pe.wait_ge(s_rt, L * 16 + 6)
                pe.wait_ge(s_ri, 5)
                pe.wait_ge(s_xa, NB * (L + 1))
                pe.matmul(PV[0][:, 0:256], tri_b[:, :], chosen[:, :, :].rearrange("p b e -> p (b e)"), start=True, stop=True)
                pe.matmul(PV[0][:, 256:512], ones_b[:, :], chosen[:, :, :].rearrange("p b e -> p (b e)"),
                          start=True, stop=True).then_inc(s_rc, 1)
                pe.wait_ge(s_lga, NG * (L + 1))
                pe.wait_ge(s_x2Te, NG * (L + 1))
                pe.wait_ge(s_tp, (L + 1) * 2)
                for b in range(NB):
                    pe.wait_ge(s_as, L * NB + b + 1)
                    last = pe.matmul(M[0][:, 0:2 * NT], at_slot[:, b, :], token_parts[:, b, :, :].rearrange("p n t -> p (n t)"),
                                     start=(b == 0), stop=(b == NB - 1))
                last.then_inc(s_id1, 1)
                pe.wait_ge(s_tok, L + 1)
                experts(pe, L, slot_step)
                if L == 0:
                    pe.wait_ge(s_fy, NT)
                    pe.wait_ge(s_slot, 1)


_INS = ["x", "ctx_1024", "mask_BxS2_bf1", "g_xattn", "g_ffn",
        "L0_xattn_wq", "L0_xattn_bq", "L0_xattn_wk", "L0_xattn_bk", "L0_xattn_wv", "L0_xattn_bv", "L0_xattn_wo",
        "L0_xattn_bo", "L0_ffn_gate_w", "L0_ffn_gate_b", "L0_ffn_w1", "L0_ffn_b1", "L0_ffn_w2", "L0_ffn_b2",
        "L1_xattn_Wq", "L1_xattn_bq", "L1_xattn_Wk", "L1_xattn_bk", "L1_xattn_Wv", "L1_xattn_bv", "L1_xattn_Wo",
        "L1_xattn_bo", "L1_ffn_W1", "L1_ffn_b1", "L1_ffn_W2", "L1_ffn_b2", "L1_ffn_Wr", "L1_ffn_br"]


def kernel(**inputs):
    import numpy as _np
    import concourse.bacc as _bacc
    from concourse import mybir as _mybir
    from concourse.bass_utils import run_bass_kernel_spmd as _run

    nc = _bacc.Bacc("TRN2", target_bir_lowering=False, num_devices=1)
    arrays, args = {}, []
    for name in _INS:
        a = _np.ascontiguousarray(inputs[name])
        if a.dtype == _np.bool_:
            a = a.view(_np.uint8)
        arrays[f"in_{name}_dram"] = a
        args.append(nc.dram_tensor(f"in_{name}_dram", a.shape, _mybir.dt.from_np(a.dtype), kind="ExternalInput").ap())
    out = nc.dram_tensor("out_0_dram", inputs["x"].shape, _mybir.dt.float32, kind="ExternalOutput").ap()
    flamingo_kernel(nc, *args, out)
    r = _run(nc, [arrays], core_ids=[0])
    return r.results[0]["out_0_dram"]
```
